# Optimizing a Trainium2 kernel written in Bass

```python
import numpy as np
import jax
import jax.numpy as jnp

def _softmax(x, axis=-1):
    return jax.nn.softmax(x, axis=axis)

def _gelu(x):
    return jax.nn.gelu(x, approximate=True)

def _silu(x):
    return jax.nn.silu(x)

def _sigmoid(x):
    return jax.nn.sigmoid(x)

def _layernorm(x, axis=-1, eps=1e-05):
    m = jnp.mean(x, axis=axis, keepdims=True)
    v = jnp.var(x, axis=axis, keepdims=True)
    return (x - m) / jnp.sqrt(v + eps)

def _scatter_add(tgt, idx, src, axis=0):
    return tgt.at[idx].add(src)

def _segment_sum(src, seg, n):
    return jax.ops.segment_sum(src, seg, n)
kernel_name = 'mk_xattn_ffn_d2_seqx_r4_9aef0b'

def setup_inputs(seed: int=0):
    np.random.seed(seed)
    _w = jnp.asarray

    def _rec_inputs():
        import jax
        import jax.numpy as jnp
        _rk = jax.random.key(seed)
        x = -0.000125 + 0.9999 * jax.random.normal(jax.random.fold_in(_rk, 1), (4, 512, 256), jnp.float32)
        _lenS = 512 - jax.random.randint(jax.random.fold_in(_rk, 7), (4,), 0, max(1, 512 // 4) + 1, jnp.int32)
        _lenS2 = 64 - jax.random.randint(jax.random.fold_in(_rk, 8), (4,), 0, max(1, 64 // 4) + 1, jnp.int32)
        _ctx_2048P = jax.random.normal(jax.random.fold_in(_rk, 11), (4, 16, 512), jnp.float32)
        _ctx_2048c = jax.random.dirichlet(jax.random.fold_in(_rk, 511), 0.3 * jnp.ones((16,), jnp.float32), (4, 64))
        _ctx_2048t = jnp.einsum('bsk,bkd->bsd', _ctx_2048c, _ctx_2048P)
        _ctx_2048t = _ctx_2048t * jax.lax.rsqrt(jnp.mean(jnp.square(_ctx_2048t)) + 1e-12) * 0.953939
        ctx_2048 = -1.39393e-06 + 0.999914 * (_ctx_2048t + 0.3 * jax.random.normal(jax.random.fold_in(_rk, 611), (4, 64, 512), jnp.float32))
        _validS = jnp.arange(512)[None, :] < _lenS[:, None]
        _validS2 = jnp.arange(64)[None, :] < _lenS2[:, None]
        _causal = jnp.tril(jnp.ones((512, 512), dtype=bool))
        mask_BxS2_ik0 = jnp.where(jnp.broadcast_to(_validS2[:, :], (4, 64)), 0, 1).astype(jnp.int32)
        return (x, ctx_2048, mask_BxS2_ik0)
    x, ctx_2048, mask_BxS2_ik0 = _rec_inputs()

    def _L0_xattn_setup():
        import jax, jax.numpy as jnp
        import numpy as np
        B, N, DIM = (8, 1024, 256)
        M, CTX = (64, 512)
        HEADS, DH = (16, 64)
        INNER = HEADS * DH
        EPS = 1e-06

        def _split_heads(t):
            b, n, _ = t.shape
            return t.reshape(b, n, HEADS, DH).transpose(0, 2, 1, 3)
        key = jax.random.key(seed)
        ks = jax.random.split(key, 6)
        x = jax.random.normal(ks[0], (B, N, DIM), dtype=jnp.float32)
        context = jax.random.normal(ks[1], (B, M, CTX), dtype=jnp.float32)
        Wq = jax.random.normal(ks[2], (DIM, INNER), dtype=jnp.float32) / np.sqrt(DIM)
        Wkv = jax.random.normal(ks[3], (CTX, 2 * INNER), dtype=jnp.float32) / np.sqrt(CTX)
        null_kv = jax.random.normal(ks[4], (2, DH), dtype=jnp.float32) / np.sqrt(2.0)
        Wout = jax.random.normal(ks[5], (INNER, DIM), dtype=jnp.float32) / np.sqrt(INNER)
        ln_scale = jnp.ones((DIM,), dtype=jnp.float32)
        ln_bias = jnp.zeros((DIM,), dtype=jnp.float32)
        return {'x': x, 'context': context, 'Wq': Wq, 'Wkv': Wkv, 'null_kv': null_kv, 'Wout': Wout, 'ln_scale': ln_scale, 'ln_bias': ln_bias}
    _L0_xattn_all = _L0_xattn_setup()
    _L0_xattn_in = {k: v for k, v in _L0_xattn_all.items() if k in ('Wq', 'Wkv', 'null_kv', 'Wout', 'ln_scale', 'ln_bias')}
    del _L0_xattn_all

    def _L0_ffn_setup():
        import jax, jax.numpy as jnp
        import numpy as np
        import math
        B, S, D = (2, 512, 256)
        H = 16
        HD = D // H
        FFN = 512
        E = 8
        TOP_K = 2
        CAP_FACTOR = 1.25
        EPS = 1e-06
        BASE = 10000.0
        CAP = max(math.ceil(B * S * TOP_K * CAP_FACTOR / E), 1)

        def _rmsnorm(x, w):
            rms = jax.lax.rsqrt(jnp.mean(x * x, axis=-1, keepdims=True) + EPS)
            return w * x * rms

        def _rope(x, cos, sin):
            xr = x[..., 0::2]
            xi = x[..., 1::2]
            c = cos[None, None]
            s_ = sin[None, None]
            out_r = xr * c - xi * s_
            out_i = xr * s_ + xi * c
            return jnp.stack([out_r, out_i], axis=-1).reshape(x.shape)

        def _mha(x, w_qkv, w_o):
            b, s, d = x.shape
            qkv = x @ w_qkv
            q, k, v = jnp.split(qkv, 3, axis=-1)
            to_heads = lambda z: z.reshape(b, s, H, HD).transpose(0, 2, 1, 3)
            q, k, v = (to_heads(q), to_heads(k), to_heads(v))
            theta = BASE ** (-2.0 * (jnp.arange(HD // 2, dtype=jnp.float32) / HD))
            freqs = jnp.arange(s, dtype=jnp.float32)[:, None] * theta[None, :]
            cos, sin = (jnp.cos(freqs), jnp.sin(freqs))
            q = _rope(q, cos, sin)
            k = _rope(k, cos, sin)
            scores = jnp.einsum('bhqd,bhkd->bhqk', q, k) / jnp.sqrt(jnp.float32(HD))
            causal = jnp.tril(jnp.ones((s, s), dtype=bool))
            scores = jnp.where(causal, scores, -jnp.inf)
            attn = jax.nn.softmax(scores, axis=-1)
            y = jnp.einsum('bhqk,bhkd->bhqd', attn, v)
            y = y.transpose(0, 2, 1, 3).reshape(b, s, d)
            return y @ w_o

        def _moe(x, w_router, w1, w2):
            b, s, d = x.shape
            t = b * s
            xf = x.reshape(t, d)
            logits = xf.astype(jnp.float32) @ w_router.astype(jnp.float32)
            probs = jax.nn.softmax(logits, axis=-1)
            g, eidx = jax.lax.top_k(probs, TOP_K)
            fg = g.reshape(t * TOP_K)
            fe = eidx.reshape(t * TOP_K)
            tok_of = jnp.arange(t * TOP_K) // TOP_K
            masked = jnp.where(fe[None, :] == jnp.arange(E)[:, None], fg[None, :], -jnp.inf)
            vals, idx = jax.lax.top_k(masked, CAP)
            valid = jnp.isfinite(vals)
            gates = jnp.where(valid, vals, 0.0)
            tok = tok_of[idx]
            xe = xf[tok]
            h = jax.nn.relu(jnp.einsum('ecd,edf->ecf', xe, w1))
            ye = jnp.einsum('ecf,efd->ecd', h, w2) * gates[..., None]
            y = jnp.zeros_like(xf).at[tok.reshape(-1)].add(ye.reshape(-1, d))
            return y.reshape(b, s, d)
        key = jax.random.key(seed)
        ks = jax.random.split(key, 6)
        sd = 0.02
        return {'x': jax.random.normal(ks[0], (B, S, D), jnp.float32), 'g1': jnp.ones((D,), jnp.float32), 'w_qkv': jax.random.normal(ks[1], (D, 3 * D), jnp.float32) * sd, 'w_o': jax.random.normal(ks[2], (D, D), jnp.float32) * sd, 'g2': jnp.ones((D,), jnp.float32), 'w_router': jax.random.normal(ks[3], (D, E), jnp.float32) * sd, 'w1': jax.random.normal(ks[4], (E, D, FFN), jnp.float32) * sd, 'w2': jax.random.normal(ks[5], (E, FFN, D), jnp.float32) * sd}
    _L0_ffn_all = _L0_ffn_setup()
    _L0_ffn_in = {k: v for k, v in _L0_ffn_all.items() if k in ('g1', 'w_qkv', 'w_o', 'g2', 'w_router', 'w1', 'w2')}
    del _L0_ffn_all

    def _L1_xattn_setup():
        import jax, jax.numpy as jnp
        import numpy as np
        UNITS = 256
        NUM_HEADS = 8

        def _split_heads(x, n):
            B, S, D = x.shape
            return x.reshape(B, S, n, D // n).transpose(0, 2, 1, 3)
        key = jax.random.key(seed)
        k1, k2, k3 = jax.random.split(key, 3)
        B, S = (8, 256)
        memory = jax.random.normal(k1, (B, S, 2 * UNITS), dtype=jnp.float32)
        query = jax.random.normal(k2, (B, S, UNITS), dtype=jnp.float32)
        seq_mask = jax.random.randint(k3, (B, S), 0, 2, dtype=jnp.int32)
        b = jnp.zeros((1,), dtype=jnp.float32)
        return {'memory': memory, 'query': query, 'seq_mask': seq_mask, 'b': b}
    _L1_xattn_all = _L1_xattn_setup()
    _L1_xattn_in = {k: v for k, v in _L1_xattn_all.items() if k in ('b',)}
    del _L1_xattn_all

    def _L1_ffn_setup():
        import jax, jax.numpy as jnp
        import numpy as np
        DIM = 256
        DEPTH = 6
        HEADS = 16
        DIM_HEAD = 64
        WINDOW = 64
        INNER = HEADS * DIM_HEAD
        DIM_INNER = int(DIM * 4 * 2 / 3)
        QK_SCALE = 8.0

        def shift_tokens(t):
            a, s = jnp.split(t, 2, -1)
            s = jnp.pad(s, ((0, 0), (1, 0), (0, 0)))[:, :-1]
            return jnp.concatenate([a, s], -1)

        def l2norm(t):
            return t / jnp.maximum(jnp.linalg.norm(t, axis=-1, keepdims=True), 1e-12)

        def rotate_half(x):
            x1, x2 = jnp.split(x, 2, -1)
            return jnp.concatenate([-x2, x1], -1)

        def rotary_tables(n):
            half = jnp.arange(0, DIM_HEAD, 2, dtype=jnp.float32)
            inv_freq = 1.0 / 10000.0 ** (half / DIM_HEAD)
            t = jnp.arange(n, dtype=jnp.float32)
            freqs = t[:, None] * inv_freq[None, :]
            freqs = jnp.concatenate([freqs, freqs], -1)
            base_scale = (half + 0.4 * DIM_HEAD) / (1.4 * DIM_HEAD)
            power = (t - n // 2) / (WINDOW // 2)
            scale = base_scale[None, :] ** power[:, None]
            scale = jnp.concatenate([scale, scale], -1)
            return (freqs, scale)

        def local_attention(q, k, v):
            b, h, n, d = q.shape
            w = WINDOW
            nw = n // w
            bq = q.reshape(b, h, nw, w, d)
            bk = k.reshape(b, h, nw, w, d)
            bv = v.reshape(b, h, nw, w, d)

            def look(t):
                p = jnp.pad(t, ((0, 0), (0, 0), (1, 0), (0, 0), (0, 0)))
                return jnp.concatenate([p[:, :, :nw], p[:, :, 1:]], axis=3)
            bk2, bv2 = (look(bk), look(bv))
            seq = jnp.arange(n).reshape(nw, w)
            seq_p = jnp.pad(seq, ((1, 0), (0, 0)), constant_values=-1)
            jt = jnp.concatenate([seq_p[:nw], seq_p[1:]], axis=1)
            it = seq[:, :, None]
            jb = jt[:, None, :]
            mask = (it < jb) | (it > jb + w) | (jb == -1)
            sim = jnp.einsum('bhwie,bhwje->bhwij', bq, bk2) * QK_SCALE
            sim = jnp.where(mask, -jnp.finfo(sim.dtype).max, sim)
            attn = jax.nn.softmax(sim, -1)
            out = jnp.einsum('bhwij,bhwje->bhwie', attn, bv2)
            return out.reshape(b, h, n, d)

        def attn_layer(x, Wqkv, qs, ksc, Wo):
            b, n, _ = x.shape
            qkv = x @ Wqkv
            q, k, v = jnp.split(qkv, 3, -1)
            sh = lambda t: t.reshape(b, n, HEADS, DIM_HEAD).transpose(0, 2, 1, 3)
            q, k, v = (sh(q), sh(k), sh(v))
            q = l2norm(q) * qs
            k = l2norm(k) * ksc
            freqs, scale = rotary_tables(n)
            cos, sin = (jnp.cos(freqs), jnp.sin(freqs))
            q = q * cos * scale + rotate_half(q) * sin * scale
            inv = 1.0 / scale
            k = k * cos * inv + rotate_half(k) * sin * inv
            out = local_attention(q, k, v)
            out = out.transpose(0, 2, 1, 3).reshape(b, n, INNER)
            return out @ Wo

        def ffn_layer(x, g, bln, W1, b1, W2, b2):
            mu = x.mean(-1, keepdims=True)
            var = ((x - mu) ** 2).mean(-1, keepdims=True)
            xn = (x - mu) / jnp.sqrt(var + 1e-05) * g + bln
            hg = xn @ W1 + b1
            a, gate = jnp.split(hg, 2, -1)
            return a * jax.nn.gelu(gate, approximate=False) @ W2 + b2
        key = jax.random.key(seed)
        ks = jax.random.split(key, 8)
        B, N = (2, 512)
        init = lambda k, shape: jax.random.normal(k, shape, jnp.float32) * 0.02
        return {'x': jax.random.normal(ks[0], (B, N, DIM), jnp.float32), 'Wqkv': init(ks[1], (DEPTH, DIM, 3 * INNER)), 'q_scale': jnp.ones((DEPTH, DIM_HEAD), jnp.float32), 'k_scale': jnp.ones((DEPTH, DIM_HEAD), jnp.float32), 'Wo': init(ks[2], (DEPTH, INNER, DIM)), 'ln_g': jnp.ones((DEPTH, DIM), jnp.float32), 'ln_b': jnp.zeros((DEPTH, DIM), jnp.float32), 'W1': init(ks[3], (DEPTH, DIM, 2 * DIM_INNER)), 'b1': jnp.zeros((DEPTH, 2 * DIM_INNER), jnp.float32), 'W2': init(ks[4], (DEPTH, DIM_INNER, DIM)), 'b2': jnp.zeros((DEPTH, DIM), jnp.float32)}
    _L1_ffn_all = _L1_ffn_setup()
    _L1_ffn_in = {k: v for k, v in _L1_ffn_all.items() if k in ('Wqkv', 'q_scale', 'k_scale', 'Wo', 'ln_g', 'ln_b', 'W1', 'b1', 'W2', 'b2')}
    del _L1_ffn_all
    return {'x': x, 'ctx_2048': ctx_2048, 'mask_BxS2_ik0': mask_BxS2_ik0, 'L0_xattn_Wq': _L0_xattn_in['Wq'], 'L0_xattn_Wkv': _L0_xattn_in['Wkv'], 'L0_xattn_null_kv': _L0_xattn_in['null_kv'], 'L0_xattn_Wout': _L0_xattn_in['Wout'], 'L0_xattn_ln_scale': _L0_xattn_in['ln_scale'], 'L0_xattn_ln_bias': _L0_xattn_in['ln_bias'], 'L0_ffn_g1': _L0_ffn_in['g1'], 'L0_ffn_w_qkv': _L0_ffn_in['w_qkv'], 'L0_ffn_w_o': _L0_ffn_in['w_o'], 'L0_ffn_g2': _L0_ffn_in['g2'], 'L0_ffn_w_router': _L0_ffn_in['w_router'], 'L0_ffn_w1': _L0_ffn_in['w1'], 'L0_ffn_w2': _L0_ffn_in['w2'], 'L1_xattn_b': _L1_xattn_in['b'], 'L1_ffn_Wqkv': _L1_ffn_in['Wqkv'], 'L1_ffn_q_scale': _L1_ffn_in['q_scale'], 'L1_ffn_k_scale': _L1_ffn_in['k_scale'], 'L1_ffn_Wo': _L1_ffn_in['Wo'], 'L1_ffn_ln_g': _L1_ffn_in['ln_g'], 'L1_ffn_ln_b': _L1_ffn_in['ln_b'], 'L1_ffn_W1': _L1_ffn_in['W1'], 'L1_ffn_b1': _L1_ffn_in['b1'], 'L1_ffn_W2': _L1_ffn_in['W2'], 'L1_ffn_b2': _L1_ffn_in['b2']}

def reference(x, ctx_2048, mask_BxS2_ik0, L0_xattn_Wq, L0_xattn_Wkv, L0_xattn_null_kv, L0_xattn_Wout, L0_xattn_ln_scale, L0_xattn_ln_bias, L0_ffn_g1, L0_ffn_w_qkv, L0_ffn_w_o, L0_ffn_g2, L0_ffn_w_router, L0_ffn_w1, L0_ffn_w2, L1_xattn_b, L1_ffn_Wqkv, L1_ffn_q_scale, L1_ffn_k_scale, L1_ffn_Wo, L1_ffn_ln_g, L1_ffn_ln_b, L1_ffn_W1, L1_ffn_b1, L1_ffn_W2, L1_ffn_b2):
    import jax
    import jax.numpy as jnp

    def _L0_xattn_ref(x, context, Wq, Wkv, null_kv, Wout, ln_scale, ln_bias):
        import jax, jax.numpy as jnp
        import numpy as np
        B, N, DIM = (8, 1024, 256)
        M, CTX = (64, 512)
        HEADS, DH = (16, 64)
        INNER = HEADS * DH
        EPS = 1e-06

        def _split_heads(t):
            b, n, _ = t.shape
            return t.reshape(b, n, HEADS, DH).transpose(0, 2, 1, 3)
        scale = DH ** (-0.5)
        b = x.shape[0]
        q = _split_heads(jnp.einsum('bnd,df->bnf', x, Wq))
        kv = jnp.einsum('bmc,cf->bmf', context, Wkv)
        k, v = jnp.split(kv, 2, axis=-1)
        k, v = (_split_heads(k), _split_heads(v))
        nk = jnp.broadcast_to(null_kv[0], (b, HEADS, 1, DH))
        nv = jnp.broadcast_to(null_kv[1], (b, HEADS, 1, DH))
        k = jnp.concatenate((nk, k), axis=-2)
        v = jnp.concatenate((nv, v), axis=-2)
        q = q * scale
        sim = jnp.einsum('bhid,bhjd->bhij', q, k)
        attn = jax.nn.softmax(sim, axis=-1)
        out = jnp.einsum('bhij,bhjd->bhid', attn, v)
        out = out.transpose(0, 2, 1, 3).reshape(b, -1, INNER)
        out = jnp.einsum('bnf,fd->bnd', out, Wout)
        mu = jnp.mean(out, axis=-1, keepdims=True)
        var = jnp.var(out, axis=-1, keepdims=True)
        out = (out - mu) * jax.lax.rsqrt(var + EPS) * ln_scale + ln_bias
        return out

    def _L0_ffn_ref(x, g1, w_qkv, w_o, g2, w_router, w1, w2):
        import jax, jax.numpy as jnp
        import numpy as np
        import math
        B, S, D = (2, 512, 256)
        H = 16
        HD = D // H
        FFN = 512
        E = 8
        TOP_K = 2
        CAP_FACTOR = 1.25
        EPS = 1e-06
        BASE = 10000.0
        CAP = max(math.ceil(B * S * TOP_K * CAP_FACTOR / E), 1)

        def _rmsnorm(x, w):
            rms = jax.lax.rsqrt(jnp.mean(x * x, axis=-1, keepdims=True) + EPS)
            return w * x * rms

        def _rope(x, cos, sin):
            xr = x[..., 0::2]
            xi = x[..., 1::2]
            c = cos[None, None]
            s_ = sin[None, None]
            out_r = xr * c - xi * s_
            out_i = xr * s_ + xi * c
            return jnp.stack([out_r, out_i], axis=-1).reshape(x.shape)

        def _mha(x, w_qkv, w_o):
            b, s, d = x.shape
            qkv = x @ w_qkv
            q, k, v = jnp.split(qkv, 3, axis=-1)
            to_heads = lambda z: z.reshape(b, s, H, HD).transpose(0, 2, 1, 3)
            q, k, v = (to_heads(q), to_heads(k), to_heads(v))
            theta = BASE ** (-2.0 * (jnp.arange(HD // 2, dtype=jnp.float32) / HD))
            freqs = jnp.arange(s, dtype=jnp.float32)[:, None] * theta[None, :]
            cos, sin = (jnp.cos(freqs), jnp.sin(freqs))
            q = _rope(q, cos, sin)
            k = _rope(k, cos, sin)
            scores = jnp.einsum('bhqd,bhkd->bhqk', q, k) / jnp.sqrt(jnp.float32(HD))
            causal = jnp.tril(jnp.ones((s, s), dtype=bool))
            scores = jnp.where(causal, scores, -jnp.inf)
            attn = jax.nn.softmax(scores, axis=-1)
            y = jnp.einsum('bhqk,bhkd->bhqd', attn, v)
            y = y.transpose(0, 2, 1, 3).reshape(b, s, d)
            return y @ w_o

        def _moe(x, w_router, w1, w2):
            b, s, d = x.shape
            t = b * s
            xf = x.reshape(t, d)
            logits = xf.astype(jnp.float32) @ w_router.astype(jnp.float32)
            probs = jax.nn.softmax(logits, axis=-1)
            g, eidx = jax.lax.top_k(probs, TOP_K)
            fg = g.reshape(t * TOP_K)
            fe = eidx.reshape(t * TOP_K)
            tok_of = jnp.arange(t * TOP_K) // TOP_K
            masked = jnp.where(fe[None, :] == jnp.arange(E)[:, None], fg[None, :], -jnp.inf)
            vals, idx = jax.lax.top_k(masked, CAP)
            valid = jnp.isfinite(vals)
            gates = jnp.where(valid, vals, 0.0)
            tok = tok_of[idx]
            xe = xf[tok]
            h = jax.nn.relu(jnp.einsum('ecd,edf->ecf', xe, w1))
            ye = jnp.einsum('ecf,efd->ecd', h, w2) * gates[..., None]
            y = jnp.zeros_like(xf).at[tok.reshape(-1)].add(ye.reshape(-1, d))
            return y.reshape(b, s, d)
        x = x + _mha(_rmsnorm(x, g1), w_qkv, w_o)
        x = x + _moe(_rmsnorm(x, g2), w_router, w1, w2)
        return x

    def _L1_xattn_ref(memory, query, seq_mask, b):
        import jax, jax.numpy as jnp
        import numpy as np
        UNITS = 256
        NUM_HEADS = 8

        def _split_heads(x, n):
            B, S, D = x.shape
            return x.reshape(B, S, n, D // n).transpose(0, 2, 1, 3)
        H = NUM_HEADS
        depth = UNITS // H
        Q = _split_heads(query, H) * depth ** (-0.5)
        k_mem, v_mem = jnp.split(memory, 2, axis=2)
        K = _split_heads(k_mem, H)
        V = _split_heads(v_mem, H)
        logits = jnp.einsum('bhqd,bhkd->bhqk', Q, K) + b[0]
        mask = seq_mask.astype(jnp.float32)[:, None, None, :]
        logits = logits + -1e+30 * (1.0 - mask)
        weights = jax.nn.softmax(logits, axis=-1)
        out = jnp.einsum('bhqk,bhkd->bhqd', weights, V)
        B, _, S, _ = out.shape
        return out.transpose(0, 2, 1, 3).reshape(B, S, UNITS)

    def _L1_ffn_ref(x, Wqkv, q_scale, k_scale, Wo, ln_g, ln_b, W1, b1, W2, b2):
        import jax, jax.numpy as jnp
        import numpy as np
        DIM = 256
        DEPTH = 6
        HEADS = 16
        DIM_HEAD = 64
        WINDOW = 64
        INNER = HEADS * DIM_HEAD
        DIM_INNER = int(DIM * 4 * 2 / 3)
        QK_SCALE = 8.0

        def shift_tokens(t):
            a, s = jnp.split(t, 2, -1)
            s = jnp.pad(s, ((0, 0), (1, 0), (0, 0)))[:, :-1]
            return jnp.concatenate([a, s], -1)

        def l2norm(t):
            return t / jnp.maximum(jnp.linalg.norm(t, axis=-1, keepdims=True), 1e-12)

        def rotate_half(x):
            x1, x2 = jnp.split(x, 2, -1)
            return jnp.concatenate([-x2, x1], -1)

        def rotary_tables(n):
            half = jnp.arange(0, DIM_HEAD, 2, dtype=jnp.float32)
            inv_freq = 1.0 / 10000.0 ** (half / DIM_HEAD)
            t = jnp.arange(n, dtype=jnp.float32)
            freqs = t[:, None] * inv_freq[None, :]
            freqs = jnp.concatenate([freqs, freqs], -1)
            base_scale = (half + 0.4 * DIM_HEAD) / (1.4 * DIM_HEAD)
            power = (t - n // 2) / (WINDOW // 2)
            scale = base_scale[None, :] ** power[:, None]
            scale = jnp.concatenate([scale, scale], -1)
            return (freqs, scale)

        def local_attention(q, k, v):
            b, h, n, d = q.shape
            w = WINDOW
            nw = n // w
            bq = q.reshape(b, h, nw, w, d)
            bk = k.reshape(b, h, nw, w, d)
            bv = v.reshape(b, h, nw, w, d)

            def look(t):
                p = jnp.pad(t, ((0, 0), (0, 0), (1, 0), (0, 0), (0, 0)))
                return jnp.concatenate([p[:, :, :nw], p[:, :, 1:]], axis=3)
            bk2, bv2 = (look(bk), look(bv))
            seq = jnp.arange(n).reshape(nw, w)
            seq_p = jnp.pad(seq, ((1, 0), (0, 0)), constant_values=-1)
            jt = jnp.concatenate([seq_p[:nw], seq_p[1:]], axis=1)
            it = seq[:, :, None]
            jb = jt[:, None, :]
            mask = (it < jb) | (it > jb + w) | (jb == -1)
            sim = jnp.einsum('bhwie,bhwje->bhwij', bq, bk2) * QK_SCALE
            sim = jnp.where(mask, -jnp.finfo(sim.dtype).max, sim)
            attn = jax.nn.softmax(sim, -1)
            out = jnp.einsum('bhwij,bhwje->bhwie', attn, bv2)
            return out.reshape(b, h, n, d)

        def attn_layer(x, Wqkv, qs, ksc, Wo):
            b, n, _ = x.shape
            qkv = x @ Wqkv
            q, k, v = jnp.split(qkv, 3, -1)
            sh = lambda t: t.reshape(b, n, HEADS, DIM_HEAD).transpose(0, 2, 1, 3)
            q, k, v = (sh(q), sh(k), sh(v))
            q = l2norm(q) * qs
            k = l2norm(k) * ksc
            freqs, scale = rotary_tables(n)
            cos, sin = (jnp.cos(freqs), jnp.sin(freqs))
            q = q * cos * scale + rotate_half(q) * sin * scale
            inv = 1.0 / scale
            k = k * cos * inv + rotate_half(k) * sin * inv
            out = local_attention(q, k, v)
            out = out.transpose(0, 2, 1, 3).reshape(b, n, INNER)
            return out @ Wo

        def ffn_layer(x, g, bln, W1, b1, W2, b2):
            mu = x.mean(-1, keepdims=True)
            var = ((x - mu) ** 2).mean(-1, keepdims=True)
            xn = (x - mu) / jnp.sqrt(var + 1e-05) * g + bln
            hg = xn @ W1 + b1
            a, gate = jnp.split(hg, 2, -1)
            return a * jax.nn.gelu(gate, approximate=False) @ W2 + b2
        for i in range(DEPTH):
            x = attn_layer(shift_tokens(x), Wqkv[i], q_scale[i], k_scale[i], Wo[i]) + x
            x = ffn_layer(shift_tokens(x), ln_g[i], ln_b[i], W1[i], b1[i], W2[i], b2[i]) + x
        return x
    x = x + _L0_xattn_ref(_layernorm(x, axis=-1), ctx_2048, L0_xattn_Wq, L0_xattn_Wkv, L0_xattn_null_kv, L0_xattn_Wout, L0_xattn_ln_scale, L0_xattn_ln_bias)
    x = x + _L0_ffn_ref(_layernorm(x, axis=-1), L0_ffn_g1, L0_ffn_w_qkv, L0_ffn_w_o, L0_ffn_g2, L0_ffn_w_router, L0_ffn_w1, L0_ffn_w2)
    x = x + _L1_xattn_ref(ctx_2048, _layernorm(x, axis=-1), mask_BxS2_ik0, L1_xattn_b)
    x = x + _L1_ffn_ref(_layernorm(x, axis=-1), L1_ffn_Wqkv, L1_ffn_q_scale, L1_ffn_k_scale, L1_ffn_Wo, L1_ffn_ln_g, L1_ffn_ln_b, L1_ffn_W1, L1_ffn_b1, L1_ffn_W2, L1_ffn_b2)
    return x

_drawn_inputs = setup_inputs


def setup_inputs(seed=0):
    import zlib

    import numpy as np

    out = dict(_drawn_inputs(seed))
    spreads = {'L0_xattn_ln_scale': (1.0, 0.2),
     'L0_xattn_ln_bias': (0.0, 0.1),
     'L0_ffn_g1': (1.0, 0.6),
     'L0_ffn_g2': (1.0, 0.6),
     'L1_ffn_q_scale': (1.0, 0.6),
     'L1_ffn_k_scale': (1.0, 0.6),
     'L1_ffn_ln_g': (1.0, 0.6),
     'L1_ffn_ln_b': (0.0, 0.8),
     'L1_ffn_b1': (0.0, 0.783),
     'L1_ffn_b2': (0.0, 0.1)}
    factors = {'L0_ffn_w_router': 7.053, 'L0_ffn_w1': 7.906, 'L0_ffn_w2': 6.429}
    for name, (base, spread) in spreads.items():
        noise = np.random.default_rng([zlib.crc32(name.encode()), seed]).standard_normal(out[name].shape)
        drawn = base * np.exp(spread * noise) if base else spread * noise
        out[name] = jnp.asarray(drawn.astype(out[name].dtype))
    for name, factor in factors.items():
        out[name] = (out[name] * factor).astype(out[name].dtype)
    return out
```

```python
from contextlib import ExitStack

import numpy as np
import concourse.bass as bass
from concourse import mybir

F32 = mybir.dt.float32
BF16 = mybir.dt.bfloat16
I32 = mybir.dt.int32
ALU = mybir.AluOpType
ACT = mybir.ActivationFunctionType
AX = mybir.AxisListType.X

P = 128
B, S, D = 4, 512, 256
T = S // P
DC = D // P
NEG = -1e30

DEPTH, HEADS, DH, WIN = 6, 16, 64, 64
INNER = HEADS * DH
FI = int(D * 4 * 2 / 3)
FC = -(-FI // P)
FR = FI - (FC - 1) * P
HALF = DH // 2
GROUP = 4
NG = T * HEADS // GROUP
QK_SCALE = 8.0


def rows(tensor, p=P):
    return tensor.rearrange("(t p) d -> p t d", p=p)


def clear(nc, sems):
    nums = [s.num for s in sems]
    assert nums == list(range(nums[0], nums[0] + len(nums)))
    nc.gpsimd.sem_clear(range(nums[0], nums[0] + len(nums)))
    nc.all_engine_barrier()


class Semaphores:

    def __init__(self, nc, ctx, stage, names):
        self.all = [ctx.enter_context(nc.semaphore(f"s_{stage}_{n}")) for n in names.split()]
        self.by_name = dict(zip(names.split(), self.all))

    def __getitem__(self, name):
        return self.by_name[name]




def normalise(nc, mem, src, dst, eps, centred):
    stats, mv, rstd, exponent = mem["stats"], mem["mv"], mem["rstd"], mem["exponent"]
    sems = mem["norm_sems"]
    mv_done, chain, pow_done, scaled = sems.all
    with nc.Block() as block:
        @block.vector
        def _(dve):
            for t in range(T):
                nc.vector.bn_stats(stats[:, t], src(t)).then_inc(chain, 1)
            for t in range(T):
                dve.wait_ge(chain, t + 1)
                nc.vector.bn_aggr(mv[:, t], stats[:, t]).then_inc(mv_done, 1)
            dve.wait_ge(mv_done, T)
            if centred:
                nc.vector.tensor_scalar(rstd[:], mv[:, :, 1], eps, None, ALU.add).then_inc(chain, 1)
            else:
                nc.vector.tensor_tensor(rstd[:], mv[:, :, 0], mv[:, :, 0], ALU.mult).then_inc(mv_done, 1)
                dve.wait_ge(mv_done, T + 1)
                nc.vector.scalar_tensor_tensor(rstd[:], mv[:, :, 1], eps, rstd[:], ALU.add, ALU.add).then_inc(chain, 1)
            dve.wait_ge(pow_done, 1)
            for t in range(T):
                if centred:
                    nc.vector.tensor_scalar(dst(t), src(t), mv[:, t, 0:1], rstd[:, t:t + 1], ALU.subtract, ALU.mult).then_inc(scaled, 1)
                else:
                    nc.vector.tensor_scalar(dst(t), src(t), rstd[:, t:t + 1], None, ALU.mult).then_inc(scaled, 1)
            dve.wait_ge(scaled, T)

        @block.gpsimd
        def _(pool):
            pool.wait_ge(chain, T + 1)
            nc.gpsimd.tensor_tensor(rstd[:], rstd[:], exponent[:], ALU.pow).then_inc(pow_done, 1)
            pool.wait_ge(pow_done, 1)
    clear(nc, sems.all)



CTX, M = 512, 64
CC = CTX // P
MN = M + 1


def null_attention(nc, mem, w):
    with ExitStack() as ctx:
        def sb(name, shape, dt=F32):
            return ctx.enter_context(nc.sbuf_tensor("xa_" + name, shape, dt))

        x_all, ident, bank = mem["x_all"], mem["ident"], mem["bank"]
        wq = sb("wq", [P, DC, INNER])
        wkv = sb("wkv", [P, CC, 2 * INNER])
        wout = sb("wout", [P, INNER // P, D])
        ln_scale = sb("ln_scale", [P, D])
        ln_bias = sb("ln_bias", [P, D])
        null_k = sb("null_k", [P, 1])
        null_v = sb("null_v", [MN, DH])
        x = sb("x", [P, T, D])
        xn = sb("xn", [P, T, D])
        xnT = sb("xnT", [P, DC, S])
        context = sb("context", [M, CTX])
        contextT = sb("contextT", [P, CC, M])
        qT = sb("qT", [P, INNER // P, S])
        kT = sb("kT", [P, INNER // P, MN])
        v = sb("v", [MN, HEADS, DH + 1])
        smax = sb("smax", [P, 2, GROUP])
        prob = sb("prob", [P, 2, GROUP, MN])
        probT = sb("probT", [MN, 2, GROUP * P])
        rsum = sb("rsum", [P, 2, GROUP])
        o = sb("o", [P, 2, INNER])
        oT = sb("oT", [P, INNER])
        y = sb("y", [P, T, D])

        sems = Semaphores(nc, ctx, "xa", "wload setup xin ctx_in xt_full xt_read ct_full ct_read kv_full kv_read q_full q_read "
                          "s_full s_read exp_done tr_full tr_read o_full o_read dve_chain back")
        (wload, setup, xin, ctx_in, xt_full, xt_read, ct_full, ct_read, kv_full, kv_read, q_full, q_read,
         s_full, s_read, exp_done, tr_full, tr_read, o_full, o_read, dve_chain, back) = sems.all

        with nc.Block() as block:
            @block.sync
            def _(sp):
                sp.dma_start(wq[:], w["Wq"].rearrange("(c p) n -> p c n", p=P)).then_inc(wload, 16)
                sp.dma_start(wout[:], w["Wout"].rearrange("(c p) n -> p c n", p=P)).then_inc(wload, 16)
                sp.dma_start(ln_scale[:], w["ln_scale"][None, :].to_broadcast([P, D])).then_inc(wload, 16)
                sp.dma_start(ln_bias[:], w["ln_bias"][None, :].to_broadcast([P, D])).then_inc(wload, 16)
                for r in range(2):
                    sp.dma_start(null_k[r * DH:(r + 1) * DH, :], w["null_kv"][0, :, None]).then_inc(wload, 16)
                sp.dma_start(null_v[M:MN, :], w["null_kv"][1, None, :]).then_inc(wload, 16)
                sp.wait_ge(wload, 16 * 8)

            @block.scalar
            def _(act):
                act.dma_start(wkv[:], w["Wkv"].rearrange("(c p) n -> p c n", p=P)).then_inc(wload, 16)

            @block.vector
            def _(dve):
                nc.vector.memset(v[:], 1.0).then_inc(setup, 1)
                dve.wait_ge(setup, 1)
                dve.wait_ge(wload, 16 * 8)
                nc.vector.tensor_copy(v[M:MN, :, 0:DH], null_v[M:MN, None, :].to_broadcast([1, HEADS, DH])).then_inc(setup, 1)
                nc.vector.tensor_copy(kT[:, :, M:MN], null_k[:, None, :].to_broadcast([P, INNER // P, 1])).then_inc(setup, 1)
                dve.wait_ge(setup, 3)
        clear(nc, sems.all)

        attention = []
        for i in range(NG + 5):
            if i < NG:
                attention.append(("scores", i))
            if 1 <= i <= NG:
                attention.append(("probT", i - 1))
            if 2 <= i < NG + 2:
                attention.append(("values", i - 2))
            if i >= 4 and i % GROUP == 3 and (i - 4) // GROUP < T:
                attention += [("oT", 2 * ((i - 4) // GROUP)), ("oT", 2 * ((i - 4) // GROUP) + 1)]
            if i >= 5 and i % GROUP == 0 and (i - 5) // GROUP < T:
                attention.append(("project", (i - 5) // GROUP))
        tr_turn = {key: n for n, key in enumerate([a for a in attention if a[0] in ("probT", "oT")])}
        out_turn = {key: n for n, key in enumerate([a for a in attention if a[0] in ("values", "project")])}

        with nc.Fori(0, B) as b:
            with nc.Block() as block:
                @block.vector
                def _(dve):
                    nc.vector.tensor_copy(x[:].rearrange("p t d -> p (t d)"), x_all[:, b]).then_inc(xin, 1)
                    dve.wait_ge(xin, 1)

                @block.sync
                def _(sp):
                    sp.dma_start(context[:], w["ctx"][b]).then_inc(ctx_in, 16)
                    sp.wait_ge(ctx_in, 16)
            clear(nc, sems.all)
            normalise(nc, mem, lambda t: x[:, t], lambda t: xn[:, t], 1e-5, True)

            with nc.Block() as block:
                @block.tensor
                def _(pe):
                    for d in range(DC):
                        for t in range(T):
                            mm = nc.tensor.transpose(bank[d][:, t * P:(t + 1) * P], xn[:, t, d * P:(d + 1) * P], ident[:])
                        mm.then_inc(xt_full, 1)
                    for c in range(CC):
                        mm = nc.tensor.transpose(bank[2][:, c * M:(c + 1) * M], context[:, c * P:(c + 1) * P], ident[0:M, 0:M])
                    mm.then_inc(ct_full, 1)
                    pe.wait_ge(ct_read, 1)
                    for c in range(INNER // P):
                        for k in range(CC):
                            mm = nc.tensor.matmul(bank[3][:, c * M:(c + 1) * M], wkv[:, k, c * P:(c + 1) * P], contextT[:, k, :],
                                                  start=(k == 0), stop=(k == CC - 1), skip_group_check=True)
                    mm.then_inc(kv_full, 1)
                    for n in range(2):
                        for k in range(CC):
                            mm = nc.tensor.matmul(bank[4 + n][0:M, :], contextT[:, k, :], wkv[:, k, INNER + n * S:INNER + (n + 1) * S],
                                                  start=(k == 0), stop=(k == CC - 1))
                        mm.then_inc(kv_full, 1)
                    pe.wait_ge(xt_read, DC)
                    for c in range(INNER // P):
                        if c >= 2:
                            pe.wait_ge(q_read, c - 1)
                        for d in range(DC):
                            mm = nc.tensor.matmul(bank[6 + c % 2][:], wq[:, d, c * P:(c + 1) * P], xnT[:, d, :], start=(d == 0), stop=(d == DC - 1))
                        mm.then_inc(q_full, 1)

                    pe.wait_ge(kv_read, 3)
                    pe.wait_ge(q_read, INNER // P)
                    for kind, n in attention:
                        t, hg = n // GROUP, n % GROUP
                        if kind == "scores":
                            if n >= 4:
                                pe.wait_ge(s_read, n - 3)
                            r = DH * (hg % 2)
                            for j in range(GROUP):
                                c = GROUP * (hg // 2) + j
                                mm = nc.tensor.matmul(bank[n % 4][:, j * MN:(j + 1) * MN], qT[r:r + DH, c, t * P:(t + 1) * P], kT[r:r + DH, c, :],
                                                      start=True, stop=True, skip_group_check=True)
                            mm.then_inc(s_full, 1)
                        elif kind in ("probT", "oT"):
                            u = tr_turn[kind, n]
                            if u >= 2:
                                pe.wait_ge(tr_read, u - 1)
                            if kind == "probT":
                                pe.wait_ge(exp_done, n + 1)
                                for j in range(GROUP):
                                    mm = nc.tensor.transpose(bank[4 + u % 2][0:MN, j * P:(j + 1) * P], prob[:, n % 2, j, :], ident[:])
                            else:
                                pe.wait_ge(o_read, out_turn["values", GROUP * (n // 2) + GROUP - 1] + 1)
                                for j in range(4):
                                    at = (n % 2) * S + j * P
                                    mm = nc.tensor.transpose(bank[4 + u % 2][:, j * P:(j + 1) * P], o[:, (n // 2) % 2, at:at + P], ident[:])
                            mm.then_inc(tr_full, 1)
                        elif kind == "values":
                            u = out_turn[kind, n]
                            pe.wait_ge(tr_read, tr_turn["probT", n] + 1)
                            if u >= 2:
                                pe.wait_ge(o_read, u - 1)
                            for j in range(GROUP):
                                mm = nc.tensor.matmul(bank[6 + u % 2][:, j * MN:(j + 1) * MN], probT[:, n % 2, j * P:(j + 1) * P],
                                                      v[:, 2 * (GROUP * (hg // 2) + j) + hg % 2, :], start=True, stop=True, skip_group_check=True)
                            mm.then_inc(o_full, 1)
                        else:
                            u = out_turn[kind, n]
                            pe.wait_ge(tr_read, tr_turn["oT", 2 * n + 1] + 1)
                            pe.wait_ge(o_read, u - 1)
                            for c in range(INNER // P):
                                mm = nc.tensor.matmul(bank[6 + u % 2][:, 0:D], oT[:, c * P:(c + 1) * P], wout[:, c, :],
                                                      start=(c == 0), stop=(c == INNER // P - 1))
                            mm.then_inc(o_full, 1)

                @block.scalar
                def _(act):
                    for d in range(DC):
                        act.wait_ge(xt_full, d + 1)
                        nc.scalar.copy(xnT[:, d, :], bank[d][:]).then_inc(xt_read, 1)
                    act.wait_ge(ct_full, 1)
                    nc.scalar.copy(contextT[:].rearrange("p c m -> p (c m)"), bank[2][:, 0:CC * M]).then_inc(ct_read, 1)
                    act.wait_ge(kv_full, 1)
                    nc.scalar.copy(kT[:, :, 0:M], bank[3][:].rearrange("p (c m) -> p c m", m=M)).then_inc(kv_read, 1)
                    for n in range(2):
                        act.wait_ge(kv_full, n + 2)
                        nc.scalar.copy(v[0:M, 8 * n:8 * n + 8, 0:DH], bank[4 + n][0:M, :].rearrange("p (h d) -> p h d", h=8)).then_inc(kv_read, 1)
                    for c in range(INNER // P):
                        act.wait_ge(q_full, c + 1)
                        nc.scalar.mul(qT[:, c, :], bank[6 + c % 2][:], DH ** -0.5).then_inc(q_read, 1)
                    for kind, n in attention:
                        if kind == "scores":
                            act.wait_ge(s_read, n + 1)
                            nc.scalar.activation(prob[:, n % 2], prob[:, n % 2], ACT.Exp).then_inc(exp_done, 1)
                        elif kind == "probT":
                            u = tr_turn[kind, n]
                            act.wait_ge(tr_full, u + 1)
                            if n >= 2:
                                act.wait_ge(o_full, out_turn["values", n - 2] + 1)
                            nc.scalar.copy(probT[:, n % 2], bank[4 + u % 2][0:MN, :]).then_inc(tr_read, 1)
                        elif kind == "oT":
                            u = tr_turn[kind, n]
                            act.wait_ge(tr_full, u + 1)
                            if n >= 2:
                                act.wait_ge(o_full, out_turn["project", n // 2 - 1] + 1)
                            nc.scalar.copy(oT[:, (n % 2) * S:(n % 2 + 1) * S], bank[4 + u % 2][:]).then_inc(tr_read, 1)

                @block.vector
                def _(dve):
                    links = [0]

                    def link(ins):
                        links[0] += 1
                        ins.then_inc(dve_chain, 1)
                        dve.wait_ge(dve_chain, links[0])

                    for kind, n in attention:
                        if kind == "scores":
                            dve.wait_ge(s_full, n + 1)
                            s3 = bank[n % 4][:, 0:GROUP * MN].rearrange("p (g q) -> p g q", g=GROUP)
                            link(nc.vector.tensor_reduce(smax[:, n % 2], s3, AX, ALU.max))
                            if n >= 2:
                                dve.wait_ge(tr_full, tr_turn["probT", n - 2] + 1)
                            nc.vector.tensor_tensor(prob[:, n % 2], s3, smax[:, n % 2, :, None].to_broadcast([P, GROUP, MN]),
                                                    ALU.subtract).then_inc(s_read, 1)
                        elif kind == "values":
                            t, hg = n // GROUP, n % GROUP
                            u = out_turn[kind, n]
                            dve.wait_ge(o_full, u + 1)
                            if n % GROUP == 0 and t >= 2:
                                dve.wait_ge(tr_full, tr_turn["oT", 2 * (t - 2) + 1] + 1)
                            ob = bank[6 + u % 2][:, 0:GROUP * MN].rearrange("p (g d) -> p g d", g=GROUP)
                            link(nc.vector.reciprocal(rsum[:, n % 2, :, None], ob[:, :, DH:MN]))
                            nc.vector.tensor_tensor(o[:, t % 2].rearrange("p (a g b d) -> p a g b d", a=2, g=GROUP, b=2)[:, hg // 2, :, hg % 2],
                                                    ob[:, :, 0:DH], rsum[:, n % 2, :, None].to_broadcast([P, GROUP, DH]),
                                                    ALU.mult).then_inc(o_read, 1)
                        elif kind == "project":
                            u = out_turn[kind, n]
                            dve.wait_ge(o_full, u + 1)
                            nc.vector.tensor_copy(y[:, n, :], bank[6 + u % 2][:, 0:D]).then_inc(o_read, 1)
                    dve.wait_ge(o_read, len(out_turn))
            clear(nc, sems.all)
            normalise(nc, mem, lambda t: y[:, t], lambda t: y[:, t], 1e-6, True)
            with nc.Block() as block:
                @block.vector
                def _(dve):
                    nc.vector.tensor_tensor(y[:], y[:], ln_scale[:, None, :].to_broadcast([P, T, D]), ALU.mult).then_inc(back, 1)
                    dve.wait_ge(back, 1)
                    nc.vector.tensor_tensor(y[:], y[:], ln_bias[:, None, :].to_broadcast([P, T, D]), ALU.add).then_inc(back, 1)
                    dve.wait_ge(back, 2)
                    nc.vector.tensor_tensor(x_all[:, b], x[:].rearrange("p t d -> p (t d)"), y[:].rearrange("p t d -> p (t d)"), ALU.add).then_inc(back, 1)
                    dve.wait_ge(back, 3)
            clear(nc, sems.all)



HD = D // HEADS
SLOT = 32
HPC = P // SLOT
HC = HEADS // HPC
E, FF = 8, 512


def causal_attention(nc, mem, w):
    with ExitStack() as ctx:
        def sb(name, shape, dt=F32):
            return ctx.enter_context(nc.sbuf_tensor("ca_" + name, shape, dt))

        x_all, ident, ident_bf, bank = mem["x_all"], mem["ident"], mem["ident_bf"], mem["bank"]
        wqkv = sb("wqkv", [P, DC, 3 * D])
        wo = sb("wo", [P, DC, D])
        wr = sb("wr", [P, DC, E])
        g12 = sb("g12", [P, 2 * DC])
        rope = sb("rope", [P, T, 2, HD])
        causal = sb("causal", [P, P])
        causal_bf = sb("causal_bf", [P, P], BF16)
        z = sb("z", [P, T, D])
        zr = sb("zr", [P, T, D])
        zT = sb("zT", [P, DC, S])
        cosd = sb("cosd", [P, 2, 2 * D])
        rot = sb("rot", [P, 2, 2 * D])
        qk = sb("qk", [P, 2, 2 * HEADS, SLOT])
        qT = sb("qT", [P, HC, S])
        kT = sb("kT", [P, HC, S])
        v = sb("v", [P, T, HEADS, HD + 1])
        smax = sb("smax", [P, 4])
        prob = sb("prob", [P, 2, S])
        probT = sb("probT", [P, 2, S])
        rsum = sb("rsum", [P, HEADS])
        o = sb("o", [P, D])
        oT = sb("oT", [P, D])
        sems = Semaphores(nc, ctx, "ca", "wload setup xin zt_full zt_read qk_full qk_read v_read padded tr_full tr_read s_full "
                          "max_done exp_done o_full o_read dve_chain back")
        (wload, setup, xin, zt_full, zt_read, qk_full, qk_read, v_read, padded, tr_full, tr_read, s_full,
         max_done, exp_done, o_full, o_read, dve_chain, back) = sems.all
        HS = HD ** -0.5

        with nc.Block() as block:
            @block.sync
            def _(sp):
                sp.dma_start(wqkv[:], w["w_qkv"].rearrange("(c p) n -> p c n", p=P)).then_inc(wload, 16)
                sp.dma_start(wo[:], w["w_o"].rearrange("(c p) n -> p c n", p=P)).then_inc(wload, 16)
                sp.dma_start(wr[:], w["w_router"].rearrange("(c p) n -> p c n", p=P)).then_inc(wload, 16)
                sp.dma_start(g12[:], w["g12"]).then_inc(wload, 16)
                sp.dma_start(rope[:], w["rope0"].rearrange("(t p) k d -> p t k d", p=P)).then_inc(wload, 16)
                sp.dma_start(causal[:], w["causal"]).then_inc(wload, 16)
                sp.wait_ge(wload, 16 * 6)

            @block.vector
            def _(dve):
                nc.vector.memset(v[:], 1.0).then_inc(setup, 1)
                nc.vector.memset(qk[:], 0.0).then_inc(setup, 1)
                dve.wait_ge(wload, 16 * 6)
                nc.vector.tensor_copy(causal_bf[:], causal[:]).then_inc(setup, 1)
                dve.wait_ge(setup, 3)
        clear(nc, sems.all)

        steps = T * HEADS
        attention = []
        for i in range(steps + 5):
            if i < steps:
                attention.append(("scores", i))
            if 1 <= i <= steps:
                attention.append(("probT", i - 1))
            if 2 <= i < steps + 2:
                attention.append(("values", i - 2))
            if i >= 3 and (i - 3) % HEADS == HEADS - 1:
                attention.append(("oT", (i - 3) // HEADS))
            if i >= 4 and (i - 4) % HEADS == HEADS - 1:
                attention.append(("project", (i - 4) // HEADS))
        tr_turn = {key: n for n, key in enumerate([("qk", n) for n in range(2 * T)] +
                                                  [a for a in attention if a[0] in ("probT", "oT")])}
        products = [a for a in attention if a[0] in ("values", "project")]
        values_count = {n: k + 1 for k, (kind, n) in enumerate(products) if kind == "values"}
        project_count = {n: k + 1 for k, (kind, n) in enumerate(products) if kind == "project"}

        with nc.Fori(0, B) as b:
            with nc.Block() as block:
                @block.vector
                def _(dve):
                    nc.vector.tensor_copy(z[:].rearrange("p t d -> p (t d)"), x_all[:, b]).then_inc(xin, 1)
                    dve.wait_ge(xin, 1)
            clear(nc, sems.all)
            normalise(nc, mem, lambda t: z[:, t], lambda t: z[:, t], 1e-5, True)
            normalise(nc, mem, lambda t: z[:, t], lambda t: zr[:, t], 1e-6, False)

            with nc.Block() as block:
                @block.tensor
                def _(pe):
                    for d in range(DC):
                        for t in range(T):
                            mm = nc.tensor.transpose(bank[d][:, t * P:(t + 1) * P], zr[:, t, d * P:(d + 1) * P], ident[:])
                        mm.then_inc(zt_full, 1)
                    pe.wait_ge(zt_read, DC)
                    for t in range(T + 1):
                        if t < T:
                            if t >= 2:
                                pe.wait_ge(qk_read, t - 1)
                                pe.wait_ge(v_read, t - 1)
                            for at, n, to in ((0, 2 * D, bank[t % 2]), (2 * D, D, bank[2 + t % 2])):
                                for d in range(DC):
                                    mm = nc.tensor.matmul(to[:, 0:n], zT[:, d, t * P:(t + 1) * P], wqkv[:, d, at:at + n],
                                                          start=(d == 0), stop=(d == DC - 1))
                                mm.then_inc(qk_full, 1)
                        if t >= 1:
                            pe.wait_ge(padded, t)
                            for part in range(2):
                                u = 2 * (t - 1) + part
                                if u >= 2:
                                    pe.wait_ge(tr_read, u - 1)
                                for c in range(HC):
                                    head = part * HEADS + c * HPC
                                    mm = nc.tensor.transpose(bank[4 + u % 2][:, c * P:(c + 1) * P],
                                                             qk[:, (t - 1) % 2, head:head + HPC, :].rearrange("p h d -> p (h d)"), ident[:])
                                mm.then_inc(tr_full, 1)
                    pe.wait_ge(tr_read, 2 * T)
                    pe.wait_ge(v_read, T)
                    for kind, n in attention:
                        t, hd = n // HEADS, n % HEADS
                        if kind == "scores":
                            if n >= 4:
                                pe.wait_ge(exp_done, n - 3)
                            r, c, keys = SLOT * (hd % HPC), hd // HPC, (t + 1) * P
                            nc.tensor.matmul(bank[n % 4][:, 0:keys], qT[r:r + HD, c, t * P:(t + 1) * P], kT[r:r + HD, c, 0:keys],
                                             start=True, stop=False)
                            nc.tensor.matmul(bank[n % 4][:, t * P:keys], ident_bf[:], causal_bf[:], start=False, stop=True).then_inc(s_full, 1)
                        elif kind == "probT":
                            u = tr_turn[kind, n]
                            pe.wait_ge(tr_read, u - 1)
                            pe.wait_ge(exp_done, n + 1)
                            for k in range(t + 1):
                                mm = nc.tensor.transpose(bank[4 + u % 2][:, k * P:(k + 1) * P], prob[:, n % 2, k * P:(k + 1) * P], ident[:])
                            mm.then_inc(tr_full, 1)
                        elif kind == "values":
                            pe.wait_ge(tr_read, tr_turn["probT", n] + 1)
                            if hd == 0 and t >= 1:
                                pe.wait_ge(o_read, 2 * t - 1)
                            for k in range(t + 1):
                                mm = nc.tensor.matmul(bank[6][:, hd * (HD + 1):(hd + 1) * (HD + 1)], probT[:, n % 2, k * P:(k + 1) * P],
                                                      v[:, k, hd, :], start=(k == 0), stop=(k == t), skip_group_check=True)
                            mm.then_inc(o_full, 1)
                        elif kind == "oT":
                            u = tr_turn[kind, n]
                            pe.wait_ge(tr_read, u - 1)
                            pe.wait_ge(o_read, 2 * n + 1)
                            for d in range(DC):
                                mm = nc.tensor.transpose(bank[4 + u % 2][:, d * P:(d + 1) * P], o[:, d * P:(d + 1) * P], ident[:])
                            mm.then_inc(tr_full, 1)
                        else:
                            pe.wait_ge(tr_read, tr_turn["oT", n] + 1)
                            for d in range(DC):
                                mm = nc.tensor.matmul(bank[7][:, 0:D], oT[:, d * P:(d + 1) * P], wo[:, d, :], start=(d == 0), stop=(d == DC - 1))
                            mm.then_inc(o_full, 1)

                @block.scalar
                def _(act):
                    for d in range(DC):
                        act.wait_ge(zt_full, d + 1)
                        nc.scalar.mul(zT[:, d, :], bank[d][:], g12[:, d:d + 1]).then_inc(zt_read, 1)
                    for t in range(T + 1):
                        if t < T:
                            act.wait_ge(qk_full, 2 * t + 2)
                            nc.scalar.copy(v[:, t, :, 0:HD], bank[2 + t % 2][:, 0:D].rearrange("p (h d) -> p h d", h=HEADS)).then_inc(v_read, 1)
                        if t >= 1:
                            for part, dst in ((0, qT), (1, kT)):
                                u = 2 * (t - 1) + part
                                act.wait_ge(tr_full, u + 1)
                                nc.scalar.copy(dst[:, :, (t - 1) * P:t * P], bank[4 + u % 2][:].rearrange("p (c q) -> p c q", c=HC)).then_inc(tr_read, 1)
                    for kind, n in attention:
                        t = n // HEADS
                        if kind == "scores":
                            keys = (t + 1) * P
                            act.wait_ge(max_done, n + 1)
                            if n >= 2:
                                act.wait_ge(tr_full, tr_turn["probT", n - 2] + 1)
                            nc.scalar.activation(prob[:, n % 2, 0:keys], bank[n % 4][:, 0:keys], ACT.Exp,
                                                 bias=smax[:, n % 4:n % 4 + 1], scale=HS).then_inc(exp_done, 1)
                        elif kind == "probT":
                            u = tr_turn[kind, n]
                            act.wait_ge(tr_full, u + 1)
                            if n >= 2:
                                act.wait_ge(o_full, values_count[n - 2])
                            nc.scalar.copy(probT[:, n % 2, 0:(t + 1) * P], bank[4 + u % 2][:, 0:(t + 1) * P]).then_inc(tr_read, 1)
                        elif kind == "oT":
                            u = tr_turn[kind, n]
                            act.wait_ge(tr_full, u + 1)
                            if n >= 1:
                                act.wait_ge(o_full, project_count[n - 1])
                            nc.scalar.copy(oT[:], bank[4 + u % 2][:, 0:D]).then_inc(tr_read, 1)

                @block.vector
                def _(dve):
                    links = [0]

                    def link(ins):
                        links[0] += 1
                        ins.then_inc(dve_chain, 1)
                        dve.wait_ge(dve_chain, links[0])

                    for t in range(T):
                        dve.wait_ge(qk_full, 2 * t + 1)
                        src = bank[t % 2][:].rearrange("p (h d) -> p h d", d=HD)
                        pairs = bank[t % 2][:].rearrange("p (h k i) -> p h k i", i=2, k=HD // 2)
                        cd = cosd[:, t % 2].rearrange("p (h d) -> p h d", d=HD)
                        rt = rot[:, t % 2].rearrange("p (h d) -> p h d", d=HD)
                        rp = rot[:, t % 2].rearrange("p (h k i) -> p h k i", i=2, k=HD // 2)
                        sn = rope[:, t, 1].rearrange("p (k i) -> p k i", i=2)
                        shape = [P, 2 * HEADS, HD // 2]
                        nc.vector.tensor_tensor(cd, src, rope[:, t, 0, None, :].to_broadcast([P, 2 * HEADS, HD]), ALU.mult).then_inc(dve_chain, 1)
                        nc.vector.tensor_tensor(rp[:, :, :, 0], pairs[:, :, :, 1], sn[:, None, :, 0].to_broadcast(shape), ALU.mult).then_inc(dve_chain, 1)
                        nc.vector.tensor_tensor(rp[:, :, :, 1], pairs[:, :, :, 0], sn[:, None, :, 1].to_broadcast(shape), ALU.mult).then_inc(qk_read, 1)
                        links[0] += 2
                        dve.wait_ge(dve_chain, links[0])
                        dve.wait_ge(qk_read, t + 1)
                        if t >= 2:
                            dve.wait_ge(tr_full, 2 * (t - 1))
                        nc.vector.tensor_tensor(qk[:, t % 2, :, 0:HD], cd, rt, ALU.add).then_inc(padded, 1)

                    for kind, n in attention:
                        t = n // HEADS
                        if kind == "scores":
                            dve.wait_ge(s_full, n + 1)
                            col = smax[:, n % 4:n % 4 + 1]
                            link(nc.vector.tensor_reduce(col, bank[n % 4][:, 0:(t + 1) * P], AX, ALU.max))
                            nc.vector.tensor_scalar(col, col, -HS, None, ALU.mult).then_inc(max_done, 1)
                        elif kind == "oT":
                            dve.wait_ge(o_full, values_count[HEADS * n + HEADS - 1])
                            ob = bank[6][:, 0:HEADS * (HD + 1)].rearrange("p (h d) -> p h d", h=HEADS)
                            link(nc.vector.reciprocal(rsum[:, :, None], ob[:, :, HD:HD + 1]))
                            if n >= 1:
                                dve.wait_ge(tr_full, tr_turn["oT", n - 1] + 1)
                            nc.vector.tensor_tensor(o[:].rearrange("p (h d) -> p h d", h=HEADS), ob[:, :, 0:HD],
                                                    rsum[:, :, None].to_broadcast([P, HEADS, HD]), ALU.mult).then_inc(o_read, 1)
                        elif kind == "project":
                            dve.wait_ge(o_full, project_count[n])
                            nc.vector.tensor_tensor(z[:, n], z[:, n], bank[7][:, 0:D], ALU.add).then_inc(o_read, 1)
                    dve.wait_ge(o_read, 2 * T)
            clear(nc, sems.all)
            normalise(nc, mem, lambda t: z[:, t], lambda t: zr[:, t], 1e-6, False)
            with nc.Block() as block:
                @block.tensor
                def _(pe):
                    for d in range(DC):
                        for t in range(T):
                            mm = nc.tensor.transpose(bank[d][:, t * P:(t + 1) * P], zr[:, t, d * P:(d + 1) * P], ident[:])
                        mm.then_inc(zt_full, 1)
                    pe.wait_ge(zt_read, DC)
                    for t in range(T):
                        for d in range(DC):
                            mm = nc.tensor.matmul(bank[2][:, t * E:(t + 1) * E], zT[:, d, t * P:(t + 1) * P], wr[:, d, :],
                                                  start=(d == 0), stop=(d == DC - 1), skip_group_check=True)
                    mm.then_inc(qk_full, 1)

                @block.scalar
                def _(act):
                    for d in range(DC):
                        act.wait_ge(zt_full, d + 1)
                        nc.scalar.mul(zT[:, d, :], bank[d][:], g12[:, DC + d:DC + d + 1]).then_inc(zt_read, 1)
                    act.wait_ge(zt_read, DC)
                    act.copy(mem["moe_inT"][:, b], zT[:]).then_inc(back, 1)
                    act.wait_ge(back, 1)

                @block.vector
                def _(dve):
                    nc.vector.tensor_tensor(x_all[:, b], x_all[:, b], z[:].rearrange("p t d -> p (t d)"), ALU.add).then_inc(setup, 1)
                    dve.wait_ge(qk_full, 1)
                    nc.vector.tensor_copy(mem["logits"][:, b], bank[2][:, 0:T * E].rearrange("p (t e) -> p t e", e=E)).then_inc(setup, 1)
                    dve.wait_ge(setup, 2)
            clear(nc, sems.all)



NT = B * T
TOP_K = 2
CAP = max(-(-(2 * 512 * TOP_K * 5) // (4 * E)), 1)
BITS = 30


def gating(nc, mem, w):
    with ExitStack() as ctx:
        def sb(name, shape, dt=F32):
            return ctx.enter_context(nc.sbuf_tensor("gt_" + name, shape, dt))

        bank = mem["bank"]
        prob = mem["logits"][:].rearrange("p b t e -> p (b t) e")
        gates = mem["gates"]
        ones = sb("ones", [P, P])
        upper = sb("upper", [P, P])
        col = sb("col", [P, NT])
        rcp = sb("rcp", [P, NT])
        rest = sb("rest", [P, NT, E])
        equal = sb("equal", [P, NT, E])
        seen = sb("seen", [P, NT, E])
        first = sb("first", [P, NT, E])
        chosen = sb("chosen", [P, NT, E])
        hit = sb("hit", [P, NT, E])
        count = sb("count", [P, E])
        least = sb("least", [P, E], I32)
        trial = sb("trial", [P, E], I32)
        bit = sb("bit", [P, E], I32)
        bit_f = sb("bit_f", [P, E])
        taken = sb("taken", [P, E], I32)
        room = sb("room", [P, E])
        rank = sb("rank", [P, NT, E])
        before = sb("before", [P, NT, E])
        sems = Semaphores(nc, ctx, "gt", "loaded dve_chain to_exp exp_done counted totals")
        loaded, dve_chain, to_exp, exp_done, counted, totals = sems.all
        wide = [P, NT, E]

        with nc.Block() as block:
            @block.sync
            def _(sp):
                sp.dma_start(ones[:], w["ones"]).then_inc(loaded, 16)
                sp.dma_start(upper[:], w["upper"]).then_inc(loaded, 16)
                sp.wait_ge(loaded, 32)

            @block.scalar
            def _(act):
                act.wait_ge(to_exp, 1)
                nc.scalar.activation(prob, prob, ACT.Exp).then_inc(exp_done, 1)

            @block.vector
            def _(dve):
                links = [0]

                def link(ins):
                    links[0] += 1
                    ins.then_inc(dve_chain, 1)
                    dve.wait_ge(dve_chain, links[0])

                link(nc.vector.tensor_reduce(col[:], prob, AX, ALU.max))
                nc.vector.tensor_tensor(prob, prob, col[:, :, None].to_broadcast(wide), ALU.subtract).then_inc(to_exp, 1)
                dve.wait_ge(exp_done, 1)
                link(nc.vector.tensor_reduce(col[:], prob, AX, ALU.add))
                link(nc.vector.reciprocal(rcp[:], col[:]))
                link(nc.vector.tensor_tensor(prob, prob, rcp[:, :, None].to_broadcast(wide), ALU.mult))
                link(nc.vector.memset(seen[:], 0.0))
                for k in range(TOP_K):
                    src = prob if k == 0 else rest[:]
                    dst = chosen if k == 0 else first
                    link(nc.vector.tensor_reduce(col[:], src, AX, ALU.max))
                    link(nc.vector.tensor_tensor(equal[:], src, col[:, :, None].to_broadcast(wide), ALU.is_equal))
                    for e in range(1, E):
                        link(nc.vector.tensor_tensor(seen[:, :, e], seen[:, :, e - 1], equal[:, :, e - 1], ALU.add))
                    link(nc.vector.scalar_tensor_tensor(dst[:], seen[:], 0.0, equal[:], ALU.is_equal, ALU.mult))
                    if k == 0:
                        link(nc.vector.scalar_tensor_tensor(rest[:], chosen[:], -4.0, prob, ALU.mult, ALU.add))
                link(nc.vector.tensor_tensor(chosen[:], chosen[:], first[:], ALU.add))
                link(nc.vector.tensor_tensor(gates[:], prob, chosen[:], ALU.mult))
                link(nc.vector.memset(least[:], 0))
                link(nc.vector.memset(bit_f[:], float(2 ** (BITS - 1))))
                link(nc.vector.tensor_copy(bit[:], bit_f[:]))
                link(nc.vector.tensor_copy(trial[:], bit[:]))
        clear(nc, sems.all)

        by_expert = "p n e -> p e n"
        bcast = [P, NT, E]

        with nc.Block() as block:
            @block.tensor
            def _(pe):
                with pe.Fori(0, BITS) as i:
                    pe.wait_ge(counted, i + 1)
                    nc.tensor.matmul(bank[0][:, 0:E], ones[:], count[:], start=True, stop=True).then_inc(totals, 1)

            @block.vector
            def _(dve):
                with dve.Fori(0, BITS) as i:
                    nc.vector.tensor_tensor(hit[:], gates[:], trial[:].bitcast(F32)[:, None, :].to_broadcast(bcast), ALU.is_ge).then_inc(dve_chain, 1)
                    dve.wait_ge(dve_chain, 5 * i + 1)
                    nc.vector.tensor_reduce(count[:], hit[:].rearrange(by_expert), AX, ALU.add).then_inc(counted, 1)
                    dve.wait_ge(totals, i + 1)
                    nc.vector.scalar_tensor_tensor(taken[:], bank[0][:, 0:E], float(CAP), bit_f[:], ALU.is_ge, ALU.mult).then_inc(dve_chain, 1)
                    dve.wait_ge(dve_chain, 5 * i + 2)
                    nc.vector.tensor_tensor(least[:], least[:], taken[:], ALU.bitwise_or)
                    nc.vector.tensor_scalar(bit_f[:], bit_f[:], 0.5, None, ALU.mult).then_inc(dve_chain, 1)
                    dve.wait_ge(dve_chain, 5 * i + 3)
                    nc.vector.tensor_copy(bit[:], bit_f[:]).then_inc(dve_chain, 1)
                    dve.wait_ge(dve_chain, 5 * i + 4)
                    nc.vector.tensor_tensor(trial[:], least[:], bit[:], ALU.bitwise_or).then_inc(dve_chain, 1)
                    dve.wait_ge(dve_chain, 5 * i + 5)
        clear(nc, sems.all)

        with nc.Block() as block:
            @block.tensor
            def _(pe):
                pe.wait_ge(counted, 1)
                nc.tensor.matmul(bank[0][:, 0:E], ones[:], count[:], start=True, stop=True).then_inc(totals, 1)
                pe.wait_ge(counted, 2)
                flat = equal[:].rearrange("p n e -> p (n e)")
                nc.tensor.matmul(bank[1][:, 0:NT * E], upper[:], flat, start=True, stop=True).then_inc(totals, 1)
                nc.tensor.matmul(bank[2][:, 0:NT * E], ones[:], flat, start=True, stop=True).then_inc(totals, 1)

            @block.vector
            def _(dve):
                links = [0]

                def link(ins):
                    links[0] += 1
                    ins.then_inc(dve_chain, 1)
                    dve.wait_ge(dve_chain, links[0])

                edge = least[:].bitcast(F32)[:, None, :].to_broadcast(bcast)
                link(nc.vector.tensor_tensor(hit[:], gates[:], edge, ALU.is_gt))
                nc.vector.tensor_reduce(count[:], hit[:].rearrange(by_expert), AX, ALU.add).then_inc(counted, 1)
                nc.vector.tensor_tensor(equal[:], gates[:], edge, ALU.is_equal).then_inc(counted, 1)
                dve.wait_ge(totals, 1)
                link(nc.vector.tensor_scalar(room[:], bank[0][:, 0:E], -1.0, float(CAP), ALU.mult, ALU.add))
                link(nc.vector.memset(before[:, 0, :], 0.0))
                dve.wait_ge(totals, 3)
                tiles = bank[2][:, 0:NT * E].rearrange("p (n e) -> p n e", e=E)
                for n in range(1, NT):
                    link(nc.vector.tensor_tensor(before[:, n], before[:, n - 1], tiles[:, n - 1], ALU.add))
                link(nc.vector.tensor_tensor(rank[:], before[:], bank[1][:, 0:NT * E].rearrange("p (n e) -> p n e", e=E), ALU.add))
                link(nc.vector.tensor_tensor(rank[:], rank[:], room[:, None, :].to_broadcast(bcast), ALU.is_lt))
                link(nc.vector.tensor_tensor(rank[:], rank[:], equal[:], ALU.mult))
                link(nc.vector.tensor_tensor(hit[:], hit[:], rank[:], ALU.add))
                link(nc.vector.tensor_tensor(gates[:], gates[:], hit[:], ALU.mult))
        clear(nc, sems.all)


def experts(nc, mem, w):
    with ExitStack() as ctx:
        def sb(name, shape, dt=F32):
            return ctx.enter_context(nc.sbuf_tensor("ex_" + name, shape, dt))

        x_all, bank, moe_inT = mem["x_all"], mem["bank"], mem["moe_inT"]
        w1 = sb("w1", [P, 2, DC, FF])
        w2 = sb("w2", [P, 2, FF // P, D])
        gate = sb("gate", [P, 2, NT])
        hT = sb("hT", [P, 2, FF // P, S])
        sems = Semaphores(nc, ctx, "ex", "wload gate_in h_full h_read y_full y_read")
        wload, gate_in, h_full, h_read, y_full, y_read = sems.all
        NF = FF // P
        jobs = [(k, b) for k in range(2) for b in range(B)]

        order = []
        for m in range(len(jobs) + 1):
            if m < len(jobs):
                order += [("relu", NF * m + f) for f in range(1, NF, 2)]
            if m >= 1:
                order += [("add", T * (m - 1) + t) for t in range(T)]
        relu_count = {n: i + 1 for i, (kind, n) in enumerate(order) if kind == "relu"}
        add_count = {n: i + 1 for i, (kind, n) in enumerate(order) if kind == "add"}
        reads_before = {n: (relu_count[n - 4] if n % 2 else (n - 4) // 2 + 1) for n in range(4, NF * len(jobs))}

        with nc.Fori(0, E // 2) as pair:
            with nc.Block() as block:
                @block.sync
                def _(sp):
                    for k in range(2):
                        sp.dma_start(w1[:, k], w["w1"][2 * pair + k].rearrange("(c p) n -> p c n", p=P)).then_inc(wload, 16)
                    sp.wait_ge(wload, 16 * 4)

                @block.scalar
                def _(act):
                    for k in range(2):
                        act.dma_start(w2[:, k], w["w2"][2 * pair + k].rearrange("(c p) n -> p c n", p=P)).then_inc(wload, 16)
                    for m, (k, b) in enumerate(jobs):
                        for f in range(0, NF, 2):
                            n = NF * m + f
                            act.wait_ge(h_full, n + 1)
                            if m >= 2:
                                act.wait_ge(y_full, T * (m - 1))
                            nc.scalar.activation(hT[:, m % 2, f], bank[n % 4][:], ACT.Relu).then_inc(h_read, 1)

                @block.tensor
                def _(pe):
                    def second(m):
                        k, b = jobs[m]
                        pe.wait_ge(h_read, NF // 2 * (m + 1))
                        pe.wait_ge(y_read, relu_count[NF * m + NF - 1])
                        for t in range(T):
                            n = T * m + t
                            if n >= 4:
                                pe.wait_ge(y_read, add_count[n - 4])
                            for f in range(NF):
                                mm = nc.tensor.matmul(bank[4 + n % 4][:, 0:D], hT[:, m % 2, f, t * P:(t + 1) * P], w2[:, k, f, :],
                                                      start=(f == 0), stop=(f == NF - 1))
                            mm.then_inc(y_full, 1)

                    pe.wait_ge(wload, 16 * 4)
                    for m, (k, b) in enumerate(jobs):
                        for f in range(NF):
                            n = NF * m + f
                            if n >= 4:
                                pe.wait_ge(h_read if f % 2 == 0 else y_read, reads_before[n])
                            for d in range(DC):
                                mm = nc.tensor.matmul(bank[n % 4][:], w1[:, k, d, f * P:(f + 1) * P], moe_inT[:, b, d, :],
                                                      start=(d == 0), stop=(d == DC - 1))
                            mm.then_inc(h_full, 1)
                        if m >= 1:
                            second(m - 1)
                    second(len(jobs) - 1)

                @block.vector
                def _(dve):
                    for k in range(2):
                        nc.vector.tensor_copy(gate[:, k, :, None], mem["gates"][:, :, bass.ds(2 * pair + k, 1)]).then_inc(gate_in, 1)
                    dve.wait_ge(gate_in, 2)
                    for kind, n in order:
                        if kind == "relu":
                            m = n // NF
                            dve.wait_ge(h_full, n + 1)
                            if m >= 2:
                                dve.wait_ge(y_full, T * (m - 1))
                            nc.vector.tensor_scalar(hT[:, m % 2, n % NF], bank[n % 4][:], 0.0, None, ALU.max).then_inc(y_read, 1)
                        else:
                            (k, b), t = jobs[n // T], n % T
                            dve.wait_ge(y_full, n + 1)
                            xs = x_all[:, b, t * D:(t + 1) * D]
                            nc.vector.scalar_tensor_tensor(xs, bank[4 + n % 4][:, 0:D], gate[:, k, b * T + t:b * T + t + 1], xs,
                                                           ALU.mult, ALU.add).then_inc(y_read, 1)
                    dve.wait_ge(y_read, len(order))
            clear(nc, sems.all)



MH = 8
MD = D // MH


def memory_attention(nc, mem, w):
    with ExitStack() as ctx:
        def sb(name, shape, dt=F32):
            return ctx.enter_context(nc.sbuf_tensor("ma_" + name, shape, dt))

        x_all, ident, psum, bank = mem["x_all"], mem["ident"], mem["psum"], mem["bank"]
        x = sb("x", [P, T, D])
        xn = sb("xn", [P, T, D])
        qT = sb("qT", [P, DC, S])
        context = sb("context", [P, CTX])
        kT = sb("kT", [P, DC, M])
        bias = sb("bias", [P, 1])
        mask_i = sb("mask_i", [P, M], I32)
        mask = sb("mask", [P, M])
        smax = sb("smax", [P, MH])
        rsum = sb("rsum", [P, MH])
        prob = sb("prob", [P, 2, MH * M])
        probT = sb("probT", [P, 2, MH * M])
        sems = Semaphores(nc, ctx, "ma", "loaded xin xt_full xt_read s_full s_read exp_in exp_done normed tr_full tr_read o_full o_read "
                          "dve_chain masked")
        (loaded, xin, xt_full, xt_read, s_full, s_read, exp_in, exp_done, normed, tr_full, tr_read, o_full, o_read,
         dve_chain, masked) = sems.all
        R = P // MD

        with nc.Fori(0, B) as b:
            with nc.Block() as block:
                @block.sync
                def _(sp):
                    for half in range(2):
                        sp.dma_start(context[half * M:(half + 1) * M, :], w["ctx"][b]).then_inc(loaded, 16)
                    sp.dma_start(mask_i[:], w["mask"][b, None, :].to_broadcast([P, M])).then_inc(loaded, 16)
                    sp.dma_start(bias[:], w["b"][None, :].to_broadcast([P, 1])).then_inc(loaded, 16)
                    sp.wait_ge(loaded, 64)

                @block.vector
                def _(dve):
                    nc.vector.tensor_copy(x[:].rearrange("p t d -> p (t d)"), x_all[:, b]).then_inc(xin, 1)
                    dve.wait_ge(loaded, 64)
                    nc.vector.tensor_copy(mask[:], mask_i[:]).then_inc(masked, 1)
                    dve.wait_ge(masked, 1)
                    nc.vector.tensor_scalar(mask[:], mask[:], -1.0, 1.0, ALU.mult, ALU.add).then_inc(masked, 1)
                    dve.wait_ge(masked, 2)
                    nc.vector.tensor_scalar(mask[:], mask[:], NEG, None, ALU.mult).then_inc(masked, 1)
                    dve.wait_ge(masked, 3)
                    dve.wait_ge(xin, 1)
            clear(nc, sems.all)
            normalise(nc, mem, lambda t: x[:, t], lambda t: xn[:, t], 1e-5, True)
            with nc.Block() as block:
                @block.tensor
                def _(pe):
                    for d in range(DC):
                        for t in range(T):
                            mm = nc.tensor.transpose(bank[d][:, t * P:(t + 1) * P], xn[:, t, d * P:(d + 1) * P], ident[:])
                        mm.then_inc(xt_full, 1)
                    for d in range(DC):
                        mm = nc.tensor.transpose(bank[2][:, d * M:(d + 1) * M], context[0:M, d * P:(d + 1) * P], ident[0:M, 0:M])
                    mm.then_inc(xt_full, 1)
                    pe.wait_ge(xt_read, DC + 1)
                    for t in range(T + 1):
                        if t < T:
                            if t >= 1:
                                pe.wait_ge(s_read, t)
                            for r in range(R):
                                for c in range(DC):
                                    mm = nc.tensor.matmul(bank[r][:, c * M:(c + 1) * M], qT[r * MD:(r + 1) * MD, c, t * P:(t + 1) * P],
                                                          kT[r * MD:(r + 1) * MD, c, :], start=True, stop=True, skip_group_check=True)
                            mm.then_inc(s_full, 1)
                        if t >= 1:
                            u = t - 1
                            pe.wait_ge(normed, u + 1)
                            if u >= 1:
                                pe.wait_ge(tr_read, u)
                            for r in range(R):
                                mm = nc.tensor.transpose(bank[4][:, r * P:(r + 1) * P], prob[:, u % 2, r * P:(r + 1) * P], ident[:])
                            mm.then_inc(tr_full, 1)
                            pe.wait_ge(tr_read, u + 1)
                            if u >= 1:
                                pe.wait_ge(o_read, u)
                            for c in range(DC):
                                for r in range(R):
                                    at = D + (R * c + r) * MD
                                    mm = nc.tensor.matmul(bank[5 + c][:, r * MD:(r + 1) * MD], probT[c * M:(c + 1) * M, u % 2, r * P:(r + 1) * P],
                                                          context[c * M:(c + 1) * M, at:at + MD], start=True, stop=True, skip_group_check=True)
                            mm.then_inc(o_full, 1)

                @block.scalar
                def _(act):
                    for d in range(DC):
                        act.wait_ge(xt_full, d + 1)
                        nc.scalar.mul(qT[:, d, :], bank[d][:], MD ** -0.5).then_inc(xt_read, 1)
                    act.wait_ge(xt_full, DC + 1)
                    nc.scalar.copy(kT[:].rearrange("p c m -> p (c m)"), bank[2][:, 0:DC * M]).then_inc(xt_read, 1)
                    for t in range(T):
                        act.wait_ge(exp_in, t + 1)
                        nc.scalar.activation(prob[:, t % 2], prob[:, t % 2], ACT.Exp).then_inc(exp_done, 1)
                        act.wait_ge(tr_full, t + 1)
                        if t >= 2:
                            act.wait_ge(o_full, t - 1)
                        nc.scalar.copy(probT[:, t % 2], bank[4][:]).then_inc(tr_read, 1)

                @block.vector
                def _(dve):
                    links = [0]

                    def link(ins):
                        links[0] += 1
                        ins.then_inc(dve_chain, 1)
                        dve.wait_ge(dve_chain, links[0])

                    for t in range(T):
                        dve.wait_ge(s_full, t + 1)
                        if t >= 2:
                            dve.wait_ge(tr_full, t - 1)
                        for r in range(R):
                            s3 = bank[r][:, 0:DC * M].rearrange("p (c m) -> p c m", m=M)
                            p3 = prob[:, t % 2, r * P:(r + 1) * P].rearrange("p (c m) -> p c m", m=M)
                            op = nc.vector.scalar_tensor_tensor(p3, s3, bias[:, 0:1], mask[:, None, :].to_broadcast([P, DC, M]), ALU.add, ALU.add)
                        op.then_inc(s_read, 1)
                        dve.wait_ge(s_read, t + 1)
                        p8 = prob[:, t % 2].rearrange("p (h m) -> p h m", m=M)
                        link(nc.vector.tensor_reduce(smax[:], p8, AX, ALU.max))
                        nc.vector.tensor_tensor(p8, p8, smax[:, :, None].to_broadcast([P, MH, M]), ALU.subtract).then_inc(exp_in, 1)
                        dve.wait_ge(exp_done, t + 1)
                        link(nc.vector.tensor_reduce(rsum[:], p8, AX, ALU.add))
                        link(nc.vector.reciprocal(rsum[:], rsum[:]))
                        nc.vector.tensor_tensor(p8, p8, rsum[:, :, None].to_broadcast([P, MH, M]), ALU.mult).then_inc(normed, 1)
                        dve.wait_ge(o_full, t + 1)
                        for c in range(DC):
                            xs = x[:, t, c * P:(c + 1) * P]
                            op = nc.vector.tensor_tensor(xs, xs, bank[5 + c][:, 0:P], ALU.add)
                        op.then_inc(o_read, 1)
                    dve.wait_ge(o_read, T)
                    link(nc.vector.tensor_copy(x_all[:, b], x[:].rearrange("p t d -> p (t d)")))
            clear(nc, sems.all)




def local_layers(nc, mem, w):
    with ExitStack() as ctx:
        def sb(name, shape, dt=F32):
            return ctx.enter_context(nc.sbuf_tensor("l1_" + name, shape, dt))

        x_all, ident, ident_bf, bank = mem["x_all"], mem["ident"], mem["ident_bf"], mem["bank"]
        wqkv = sb("wqkv", [P, DC, 3 * INNER])
        wo = sb("wo", [P, INNER // P, D])
        w1 = sb("w1", [P, DC, 2 * FI])
        w2 = sb("w2", [P, FC, D])
        cols = sb("cols", [P, 2 * FC + 2 * DC])
        b1 = cols[:, 0:2 * FC].rearrange("p (k c) -> p k c", k=2)
        ln_g = cols[:, 2 * FC:2 * FC + DC]
        ln_b = cols[:, 2 * FC + DC:2 * FC + 2 * DC]
        scale_qk = sb("scale_qk", [P, 2, DH])
        rope = sb("rope", [P, 4, T, DH])
        turn = sb("turn", [P, 4, T, DH])
        shift = sb("shift", [P, 2, P])
        mask = sb("mask", [P, 2, P])
        mask_bf = sb("mask_bf", [P, 2, P], BF16)
        x = sb("x", [P, T, D])
        xT = sb("xT", [P, DC, S + 1])
        sq = sb("sq", [P, 2, S])
        norm = sb("norm", [P, 2, 8])
        minus_half = sb("minus_half", [P, 8])
        qn = sb("qn", [P, 2, S])
        rot = sb("rot", [P, 2, S])
        cosd = sb("cosd", [P, 2, S])
        qr = sb("qr", [P, 2, S])
        qT = sb("qT", [P, INNER // P, S])
        kT = sb("kT", [P, INNER // P, S])
        v_odd = sb("v_odd", [P, T, HEADS, DH + 1])
        v_even = sb("v_even", [P, T, HEADS, DH + 1])
        smax = sb("smax", [P, 2, GROUP])
        prob = sb("prob", [P, 2, GROUP * P])
        probT = sb("probT", [P, 2, GROUP * P])
        rsum = sb("rsum", [P, 2, GROUP])
        o = sb("o", [P, 2, INNER])
        oT = sb("oT", [P, INNER])
        stats = sb("stats", [P, T, 2, 6])
        mv = sb("mv", [P, T, 2])
        rstd = sb("rstd", [P, T])
        xn = sb("xn", [P, 2, D])
        xnT, gate = cosd, rot
        h = sb("h", [P, FC, S])

        sems = Semaphores(nc, ctx, "l1", "table wload xin xt_full xt_read qkv_full sq_done qk_read "
                          "rot_done qr_done v_read tr_full tr_read s_full s_read exp_done o_full "
                          "ss_done norm_done pow_chain mv_done rstd_done o_read sh_full xn_done ga_full gelu_done h_done back dve_chain setup")
        (table, wload, xin, xt_full, xt_read, qkv_full, sq_done, qk_read, rot_done, qr_done, v_read,
         tr_full, tr_read, s_full, s_read, exp_done, o_full, ss_done, norm_done, pow_chain, mv_done, rstd_done, o_read, sh_full, xn_done, ga_full, gelu_done,
         h_done, back, dve_chain, setup) = sems.all

        with nc.Block() as block:
            @block.sync
            def _(sp):
                sp.dma_start(rope[:], w["rope1"].rearrange("k (t p) d -> p k t d", p=P)).then_inc(table, 16)
                sp.dma_start(shift[:], w["shift"].rearrange("k p q -> p k q")).then_inc(table, 16)
                sp.dma_start(mask[:], w["win_mask"].rearrange("k p q -> p k q")).then_inc(table, 16)

            @block.gpsimd
            def _(pool):
                nc.gpsimd.memset(v_odd[:], 1.0).then_inc(setup, 1)
                nc.gpsimd.memset(v_even[:], 1.0).then_inc(setup, 1)
                nc.gpsimd.memset(xT[:, 1, 0:1], 0.0).then_inc(setup, 1)
                nc.gpsimd.memset(minus_half[:], -0.5).then_inc(setup, 1)

            @block.vector
            def _(dve):
                nc.vector.memset(h[32:64, FC - 1, :], 1.0).then_inc(setup, 1)
                dve.wait_ge(table, 48)
                for k in range(2):
                    nc.vector.tensor_copy(mask_bf[:, k], mask[:, k]).then_inc(setup, 1)
                dve.wait_ge(setup, 7)
        clear(nc, sems.all)

        QK = 4 * T
        attention = []
        for i in range(NG + 5):
            if i < NG:
                attention.append(("scores", i))
            if 1 <= i <= NG:
                attention.append(("probT", i - 1))
            if 2 <= i < NG + 2:
                attention.append(("values", i - 2))
            if i >= 4 and i % GROUP == 3 and (i - 4) // GROUP < T:
                attention += [("oT", 2 * ((i - 4) // GROUP)), ("oT", 2 * ((i - 4) // GROUP) + 1)]
            if i >= 5 and i % GROUP == 0 and (i - 5) // GROUP < T:
                attention.append(("project", (i - 5) // GROUP))
        tr_turn = {key: n for n, key in enumerate(
            [("qk", m) for m in range(QK)] + [a for a in attention if a[0] in ("probT", "oT")] + [("xn", t) for t in range(T)])}
        out_turn = {key: n for n, key in enumerate(
            [a for a in attention if a[0] in ("values", "project")] + [("ffn", t) for t in range(T)])}
        chunk_order = []
        m = 0
        for n in range(6 * T + 4):
            if n < 6 * T:
                chunk_order.append(("chunk", n))
            while m < QK and 6 * (m // 4) + m % 4 <= n - 3:
                chunk_order.append(("qk", m))
                m += 1

        with nc.Fori(0, DEPTH) as layer:
            with nc.Block() as block:
                @block.sync
                def _(sp):
                    for s in range(2):
                        sp.dma_start(scale_qk[:, s], w["qk_scale"][s][layer, None, :].to_broadcast([P, DH])).then_inc(table, 16)
                    sp.dma_start(wqkv[:], w["Wqkv"][layer].rearrange("(c p) n -> p c n", p=P)).then_inc(wload, 16)
                    sp.dma_start(w1[:], w["W1"][layer].rearrange("(c p) n -> p c n", p=P)).then_inc(wload, 16)
                    sp.wait_ge(wload, 16 * 7)

                @block.scalar
                def _(act):
                    act.dma_start(wo[:], w["Wo"][layer].rearrange("(c p) n -> p c n", p=P)).then_inc(wload, 16)
                    act.dma_start(w2[:, 0:FC - 1], w["W2"][layer][0:(FC - 1) * P].rearrange("(c p) n -> p c n", p=P)).then_inc(wload, 16)
                    act.dma_start(w2[0:FR, FC - 1], w["W2"][layer][(FC - 1) * P:FI]).then_inc(wload, 16)
                    act.dma_start(w2[FR:FR + 1, FC - 1], w["b2"][layer, None, :]).then_inc(wload, 16)
                    act.dma_start(cols[:], w["cols"][layer]).then_inc(wload, 16)

                @block.vector
                def _(dve):
                    dve.wait_ge(table, 32)
                    for s in range(2):
                        sc = scale_qk[:, s]
                        nc.vector.tensor_tensor(turn[:, 2 * s], rope[:, 2 * s], sc[:, None, :].to_broadcast([P, T, DH]), ALU.mult).then_inc(back, 1)
                        nc.vector.tensor_tensor(turn[:, 2 * s + 1, :, 0:HALF], rope[:, 2 * s + 1, :, 0:HALF],
                                                sc[:, None, HALF:DH].to_broadcast([P, T, HALF]), ALU.mult).then_inc(back, 1)
                        nc.vector.tensor_tensor(turn[:, 2 * s + 1, :, HALF:DH], rope[:, 2 * s + 1, :, HALF:DH],
                                                sc[:, None, 0:HALF].to_broadcast([P, T, HALF]), ALU.mult).then_inc(back, 1)
                    dve.wait_ge(back, 6)
            clear(nc, sems.all)

            with nc.Fori(0, B) as b:
                with nc.Block() as block:
                    @block.tensor
                    def _(pe):
                        pe.wait_ge(xin, 1)
                        for d in range(DC):
                            for t in range(T):
                                mm = nc.tensor.transpose(bank[d][:, t * P:(t + 1) * P], x[:, t, d * P:(d + 1) * P], ident[:])
                            mm.then_inc(xt_full, 1)

                        pe.wait_ge(xt_read, DC)
                        for kind, n in chunk_order:
                            if kind == "chunk":
                                t, c = n // 6, n % 6
                                if n >= 4:
                                    t4, c4 = (n - 4) // 6, (n - 4) % 6
                                    if c4 < 4:
                                        pe.wait_ge(qk_read, 4 * t4 + c4 + 1)
                                    else:
                                        pe.wait_ge(v_read, 2 * t4 + c4 - 3)
                                for d in range(DC):
                                    mm = nc.tensor.matmul(bank[n % 4][:], xT[:, d, t * P:(t + 1) * P],
                                                          wqkv[:, d, c * S:(c + 1) * S], start=(d == 0), stop=(d == DC - 1))
                                mm.then_inc(qkv_full, 1)
                            else:
                                pe.wait_ge(qr_done, n + 1)
                                if n >= 2:
                                    pe.wait_ge(tr_read, n - 1)
                                for j in range(4):
                                    mm = nc.tensor.transpose(bank[4 + n % 2][:, j * P:(j + 1) * P], qr[:, n % 2, j * P:(j + 1) * P], ident[:])
                                mm.then_inc(tr_full, 1)

                        pe.wait_ge(qk_read, QK)
                        pe.wait_ge(v_read, 2 * T)
                        pe.wait_ge(tr_read, QK)
                        for kind, n in attention:
                            t, hg = n // GROUP, n % GROUP
                            if kind == "scores" and n % 2 == 0:
                                if n >= 4:
                                    pe.wait_ge(s_read, n - 2)
                                for k in range(2):
                                    nc.tensor.matmul(bank[(n + k) % 4][:].rearrange("p (g q) -> p g q", g=GROUP), ident_bf[:],
                                                     mask_bf[:, 0 if t == 0 else 1, None, :].to_broadcast([P, GROUP, P]),
                                                     start=True, stop=False, skip_group_check=True)
                                for j in range(GROUP):
                                    c = GROUP * (hg // 2) + j
                                    for odd in range(2):
                                        for k in range(2):
                                            half = odd ^ k
                                            r, q0, s = DH * k, t * P + half * WIN, bank[(n + k) % 4]
                                            before = WIN if q0 > 0 else 0
                                            mm = nc.tensor.matmul(s[half * WIN:(half + 1) * WIN, j * P + WIN - before:(j + 1) * P],
                                                                  qT[r:r + DH, c, q0:q0 + WIN], kT[r:r + DH, c, q0 - before:q0 + WIN],
                                                                  start=False, stop=(j == GROUP - 1 and odd == 1), skip_group_check=True)
                                            if j == GROUP - 1 and odd == 1:
                                                mm.then_inc(s_full, 1)
                            elif kind == "scores":
                                pass
                            elif kind in ("probT", "oT"):
                                u = tr_turn[kind, n]
                                pe.wait_ge(tr_read, u - 1)
                                if kind == "probT":
                                    pe.wait_ge(exp_done, n + 1)
                                    src = prob[:, n % 2]
                                else:
                                    pe.wait_ge(o_read, out_turn["values", GROUP * (n // 2) + GROUP - 1] + 1)
                                    src = o[:, (n // 2) % 2, (n % 2) * S:(n % 2 + 1) * S]
                                for j in range(4):
                                    mm = nc.tensor.transpose(bank[4 + u % 2][:, j * P:(j + 1) * P], src[:, j * P:(j + 1) * P], ident[:])
                                mm.then_inc(tr_full, 1)
                            elif kind == "values":
                                u = out_turn[kind, n]
                                pe.wait_ge(tr_read, tr_turn["probT", n] + 1)
                                if u >= 2:
                                    pe.wait_ge(o_read, u - 1)
                                for j in range(GROUP):
                                    for half, v in ((0, v_even), (1, v_odd)):
                                        mm = nc.tensor.matmul(bank[6 + u % 2][half * WIN:(half + 1) * WIN, j * (DH + 1):(j + 1) * (DH + 1)],
                                                              probT[:, n % 2, j * P + half * WIN:j * P + (half + 1) * WIN],
                                                              v[:, t, 2 * (GROUP * (hg // 2) + j) + hg % 2, :], start=True, stop=True, skip_group_check=True)
                                mm.then_inc(o_full, 1)
                            else:
                                u = out_turn[kind, n]
                                pe.wait_ge(tr_read, tr_turn["oT", 2 * n + 1] + 1)
                                pe.wait_ge(o_read, u - 1)
                                for c in range(INNER // P):
                                    mm = nc.tensor.matmul(bank[6 + u % 2][:, 0:D], oT[:, c * P:(c + 1) * P], wo[:, c, :],
                                                          start=(c == 0), stop=(c == INNER // P - 1))
                                mm.then_inc(o_full, 1)

                        pe.wait_ge(s_read, NG)
                        for t in range(T):
                            pe.wait_ge(o_read, out_turn["project", t] + 1)
                            mm = nc.tensor.matmul(bank[t][:, 0:P], shift[:, 0], x[:, t, P:D], start=True, stop=(t == 0))
                            if t > 0:
                                mm = nc.tensor.matmul(bank[t][:, 0:P], shift[:, 1], x[:, t - 1, P:D], start=False, stop=True)
                            mm.then_inc(sh_full, 1)
                        for t in range(T):
                            u = tr_turn["xn", t]
                            pe.wait_ge(xn_done, t + 1)
                            pe.wait_ge(tr_read, u - 1)
                            for d in range(DC):
                                mm = nc.tensor.transpose(bank[4 + u % 2][:, d * P:(d + 1) * P], xn[:, t % 2, d * P:(d + 1) * P], ident[:])
                            mm.then_inc(tr_full, 1)
                        pe.wait_ge(tr_read, len(tr_turn))
                        for i in range(FC):
                            n = P if i < FC - 1 else FR
                            if i >= 2:
                                pe.wait_ge(h_done, i - 1)
                            for k, at in ((1, FI), (0, 0)):
                                for d in range(DC):
                                    mm = nc.tensor.matmul(bank[2 * (i % 2) + k][0:n, :], w1[:, d, at + i * P:at + i * P + n], xnT[:, d, :],
                                                          start=(d == 0), stop=(d == DC - 1))
                                mm.then_inc(ga_full, 1)
                        pe.wait_ge(h_done, FC)
                        for t in range(T):
                            u = out_turn["ffn", t]
                            pe.wait_ge(o_read, u - 1)
                            for i in range(FC):
                                n = P if i < FC - 1 else FR + 1
                                mm = nc.tensor.matmul(bank[6 + u % 2][:, 0:D], h[0:n, i, t * P:(t + 1) * P], w2[0:n, i, :],
                                                      start=(i == 0), stop=(i == FC - 1))
                            mm.then_inc(o_full, 1)

                    @block.scalar
                    def _(act):
                        for d in range(DC):
                            act.wait_ge(xt_full, d + 1)
                            nc.scalar.copy(xT[:, d, d:d + S], bank[d][:]).then_inc(xt_read, 1)
                        for kind, n in chunk_order:
                            if kind == "chunk":
                                t, c = n // 6, n % 6
                                act.wait_ge(qkv_full, n + 1)
                                if c < 4:
                                    m = 4 * t + c
                                    if m >= 2:
                                        act.wait_ge(ss_done, m - 1)
                                    nc.scalar.activation(sq[:, m % 2], bank[n % 4][:], ACT.Square).then_inc(sq_done, 1)
                                else:
                                    src = bank[n % 4][:].rearrange("p (h d) -> p h d", h=8)
                                    hs = slice(8 * (c - 4), 8 * (c - 3))
                                    nc.scalar.copy(v_even[WIN:P, t, hs, 0:DH], src[0:WIN])
                                    if t < T - 1:
                                        nc.scalar.copy(v_even[0:WIN, t + 1, hs, 0:DH], src[WIN:P])
                                    nc.scalar.copy(v_odd[:, t, hs, 0:DH], src).then_inc(v_read, 1)
                            else:
                                act.wait_ge(tr_full, n + 1)
                                t, c = n // 4, n % 4
                                dst = qT if c < 2 else kT
                                nc.scalar.copy(dst[:, 4 * (c % 2):4 * (c % 2) + 4, t * P:(t + 1) * P],
                                               bank[4 + n % 2][:].rearrange("p (c q) -> p c q", c=4)).then_inc(tr_read, 1)
                        for kind, n in attention:
                            if kind == "scores":
                                act.wait_ge(s_read, n + 1)
                                nc.scalar.activation(prob[:, n % 2], prob[:, n % 2], ACT.Exp, scale=QK_SCALE).then_inc(exp_done, 1)
                            elif kind == "probT":
                                u = tr_turn[kind, n]
                                act.wait_ge(tr_full, u + 1)
                                if n >= 2:
                                    act.wait_ge(o_full, out_turn["values", n - 2] + 1)
                                nc.scalar.copy(probT[:, n % 2], bank[4 + u % 2][:]).then_inc(tr_read, 1)
                            elif kind == "oT":
                                u = tr_turn[kind, n]
                                act.wait_ge(tr_full, u + 1)
                                if n >= 2:
                                    act.wait_ge(o_full, out_turn["project", n // 2 - 1] + 1)
                                nc.scalar.copy(oT[:, (n % 2) * S:(n % 2 + 1) * S], bank[4 + u % 2][:]).then_inc(tr_read, 1)
                        for t in range(T):
                            u = tr_turn["xn", t]
                            act.wait_ge(tr_full, u + 1)
                            for d in range(DC):
                                cp = nc.scalar.activation(xnT[:, d, t * P:(t + 1) * P], bank[4 + u % 2][:, d * P:(d + 1) * P],
                                                          ACT.Identity, bias=ln_b[:, d:d + 1], scale=ln_g[:, d:d + 1])
                            cp.then_inc(tr_read, 1)
                        for i in range(FC):
                            n = P if i < FC - 1 else FR
                            act.wait_ge(ga_full, 2 * i + 1)
                            if i >= 2:
                                act.wait_ge(h_done, i - 1)
                            nc.scalar.activation(gate[0:n, i % 2], bank[2 * (i % 2) + 1][0:n, :], ACT.Gelu,
                                                 bias=b1[0:n, 1, i:i + 1]).then_inc(gelu_done, 1)

                    @block.gpsimd
                    def _(pool):
                        def turn_half(m):
                            t, c = m // 4, m % 4
                            pool.wait_ge(qk_read, m + 1)
                            if m >= 2:
                                pool.wait_ge(qr_done, m - 1)
                            q3 = qn[:, m % 2].rearrange("p (h d) -> p h d", h=8)
                            r3 = rot[:, m % 2].rearrange("p (h d) -> p h d", h=8)
                            sn = turn[:, 2 * (c // 2) + 1, t, None, :]
                            nc.gpsimd.tensor_tensor(r3[:, :, 0:HALF], q3[:, :, HALF:DH],
                                                    sn[:, :, 0:HALF].to_broadcast([P, 8, HALF]), ALU.mult)
                            nc.gpsimd.tensor_tensor(r3[:, :, HALF:DH], q3[:, :, 0:HALF],
                                                    sn[:, :, HALF:DH].to_broadcast([P, 8, HALF]), ALU.mult).then_inc(rot_done, 1)

                        for m in range(QK):
                            pool.wait_ge(ss_done, m + 1)
                            nc.gpsimd.tensor_scalar(norm[:, m % 2], norm[:, m % 2], 1e-24, None, ALU.max).then_inc(pow_chain, 1)
                            pool.wait_ge(pow_chain, m + 1)
                            nc.gpsimd.tensor_tensor(norm[:, m % 2], norm[:, m % 2], minus_half[:], ALU.pow).then_inc(norm_done, 1)
                            if m >= 1:
                                turn_half(m - 1)
                        turn_half(QK - 1)
                        pool.wait_ge(mv_done, T)
                        nc.gpsimd.tensor_scalar(rstd[:], mv[:, :, 1], 1e-5, None, ALU.add).then_inc(pow_chain, 1)
                        pool.wait_ge(pow_chain, QK + 1)
                        nc.gpsimd.tensor_tensor(rstd[:], rstd[:], minus_half[:, 0:T], ALU.pow).then_inc(rstd_done, 1)

                    @block.vector
                    def _(dve):
                        links = [0]

                        def link(ins):
                            links[0] += 1
                            ins.then_inc(dve_chain, 1)
                            dve.wait_ge(dve_chain, links[0])

                        nc.vector.tensor_copy(x[:].rearrange("p t d -> p (t d)"), x_all[:, b]).then_inc(xin, 1)

                        def add_turned(m):
                            dve.wait_ge(rot_done, m + 1)
                            if m >= 2:
                                dve.wait_ge(tr_full, m - 1)
                            nc.vector.tensor_tensor(qr[:, m % 2], cosd[:, m % 2], rot[:, m % 2], ALU.add).then_inc(qr_done, 1)

                        def normalise(m):
                            t, c = m // 4, m % 4
                            src = bank[(6 * t + c) % 4][:].rearrange("p (h d) -> p h d", h=8)
                            q3 = qn[:, m % 2].rearrange("p (h d) -> p h d", h=8)
                            dve.wait_ge(norm_done, m + 1)
                            if m >= 2:
                                dve.wait_ge(rot_done, m - 1)
                            nc.vector.tensor_tensor(q3, src, norm[:, m % 2, :, None].to_broadcast([P, 8, DH]), ALU.mult).then_inc(qk_read, 1)
                            dve.wait_ge(qk_read, m + 1)
                            link(nc.vector.tensor_tensor(cosd[:, m % 2].rearrange("p (h d) -> p h d", h=8), q3,
                                                         turn[:, 2 * (c // 2), t, None, :].to_broadcast([P, 8, DH]), ALU.mult))

                        for m in range(QK + 2):
                            if m >= 2:
                                add_turned(m - 2)
                            if m < QK:
                                dve.wait_ge(sq_done, m + 1)
                                if m >= 2:
                                    dve.wait_ge(qk_read, m - 1)
                                nc.vector.tensor_reduce(norm[:, m % 2], sq[:, m % 2].rearrange("p (h d) -> p h d", h=8), AX, ALU.add).then_inc(ss_done, 1)
                            if 1 <= m <= QK:
                                normalise(m - 1)

                        for kind, n in attention:
                            if kind == "scores":
                                dve.wait_ge(s_full, n + 1)
                                s3 = bank[n % 4][:].rearrange("p (g q) -> p g q", g=GROUP)
                                link(nc.vector.tensor_reduce(smax[:, n % 2], s3, AX, ALU.max))
                                if n >= 2:
                                    dve.wait_ge(tr_full, tr_turn["probT", n - 2] + 1)
                                nc.vector.tensor_tensor(prob[:, n % 2].rearrange("p (g q) -> p g q", g=GROUP), s3,
                                                        smax[:, n % 2, :, None].to_broadcast([P, GROUP, P]), ALU.subtract).then_inc(s_read, 1)
                            elif kind == "values":
                                t, hg = n // GROUP, n % GROUP
                                u = out_turn[kind, n]
                                dve.wait_ge(o_full, u + 1)
                                if n % GROUP == 0 and t >= 2:
                                    dve.wait_ge(tr_full, tr_turn["oT", 2 * (t - 2) + 1] + 1)
                                ob = bank[6 + u % 2][:, 0:GROUP * (DH + 1)].rearrange("p (g d) -> p g d", g=GROUP)
                                link(nc.vector.reciprocal(rsum[:, n % 2, :, None], ob[:, :, DH:DH + 1]))
                                nc.vector.tensor_tensor(o[:, t % 2].rearrange("p (a g b d) -> p a g b d", a=2, g=GROUP, b=2)[:, hg // 2, :, hg % 2],
                                                        ob[:, :, 0:DH], rsum[:, n % 2, :, None].to_broadcast([P, GROUP, DH]),
                                                        ALU.mult).then_inc(o_read, 1)
                            elif kind == "project":
                                u = out_turn[kind, n]
                                dve.wait_ge(o_full, u + 1)
                                nc.vector.tensor_tensor(x[:, n, :], x[:, n, :], bank[6 + u % 2][:, 0:D], ALU.add).then_inc(o_read, 1)

                        for t in range(T):
                            dve.wait_ge(o_read, out_turn["project", t] + 1)
                            nc.vector.bn_stats(stats[:, t, 0, :], x[:, t, 0:P])
                            dve.wait_ge(sh_full, t + 1)
                            link(nc.vector.bn_stats(stats[:, t, 1, :], bank[t][:, 0:P]))
                            nc.vector.bn_aggr(mv[:, t], stats[:, t].rearrange("p a b -> p (a b)")).then_inc(mv_done, 1)
                        dve.wait_ge(mv_done, T)
                        dve.wait_ge(rstd_done, 1)
                        for t in range(T):
                            if t >= 2:
                                dve.wait_ge(tr_full, tr_turn["xn", t - 2] + 1)
                            nc.vector.tensor_scalar(xn[:, t % 2, 0:P], x[:, t, 0:P], mv[:, t, 0:1], rstd[:, t:t + 1], ALU.subtract, ALU.mult)
                            nc.vector.tensor_scalar(xn[:, t % 2, P:D], bank[t][:, 0:P], mv[:, t, 0:1], rstd[:, t:t + 1], ALU.subtract, ALU.mult).then_inc(xn_done, 1)
                        for i in range(FC):
                            n = P if i < FC - 1 else FR
                            dve.wait_ge(ga_full, 2 * i + 2)
                            dve.wait_ge(gelu_done, i + 1)
                            nc.vector.scalar_tensor_tensor(h[0:n, i, :], bank[2 * (i % 2)][0:n, :], b1[0:n, 0, i:i + 1], gate[0:n, i % 2],
                                                           ALU.add, ALU.mult).then_inc(h_done, 1)
                        for t in range(T):
                            u = out_turn["ffn", t]
                            dve.wait_ge(o_full, u + 1)
                            nc.vector.tensor_tensor(x[:, t, :], x[:, t, :], bank[6 + u % 2][:, 0:D], ALU.add).then_inc(o_read, 1)
                        dve.wait_ge(o_read, len(out_turn))
                        nc.vector.tensor_copy(x_all[:, b], x[:].rearrange("p t d -> p (t d)")).then_inc(back, 1)
                        dve.wait_ge(back, 1)
                clear(nc, sems.all)




def constants(nc, mem, w):
    with ExitStack() as ctx:
        sems = Semaphores(nc, ctx, "init", "loaded done")
        loaded, done = sems.all
        with nc.Block() as block:
            @block.sync
            def _(sp):
                sp.dma_start(mem["ident"][:], w["ident"]).then_inc(loaded, 16)
                sp.dma_start(mem["x_all"][:].rearrange("p b (t d) -> p b t d", t=T),
                             w["x"].rearrange("b (t p) d -> p b t d", p=P)).then_inc(loaded, 16)
                sp.wait_ge(loaded, 32)

            @block.vector
            def _(dve):
                dve.wait_ge(loaded, 32)
                nc.vector.tensor_copy(mem["ident_bf"][:], mem["ident"][:]).then_inc(done, 1)
                dve.wait_ge(done, 1)
        clear(nc, sems.all)


def setup_exponent(nc, mem):
    sems = mem["norm_sems"]
    with nc.Block() as block:
        @block.vector
        def _(dve):
            nc.vector.memset(mem["exponent"][:], -0.5).then_inc(sems["chain"], 1)
            dve.wait_ge(sems["chain"], 1)
    clear(nc, sems.all)


def layer_norm(nc, mem, w):
    x_all = mem["x_all"]
    with ExitStack() as ctx:
        stats = ctx.enter_context(nc.sbuf_tensor("ln_stats", [P, B * T, 6], F32))
        mv = ctx.enter_context(nc.sbuf_tensor("ln_mv", [P, B * T, 2], F32))
        rstd = ctx.enter_context(nc.sbuf_tensor("ln_rstd", [P, B * T, 1], F32))
        exponent = ctx.enter_context(nc.sbuf_tensor("ln_exponent", [P, B * T, 1], F32))
        sems = Semaphores(nc, ctx, "ln", "kept chain pow_chain")
        kept, chain, pow_chain = sems.all
        x3 = x_all[:].rearrange("p b (t d) -> p (b t) d", t=T)
        with nc.Block() as block:
            @block.sync
            def _(sp):
                sp.dma_start(w["x_kept"], x_all[:].rearrange("p b n -> p (b n)")).then_inc(kept, 16)
                sp.wait_ge(kept, 16)

            @block.gpsimd
            def _(pool):
                nc.gpsimd.memset(exponent[:], -0.5).then_inc(pow_chain, 1)
                pool.wait_ge(pow_chain, 1)
                pool.wait_ge(chain, 2 * B * T + 1)
                nc.gpsimd.tensor_tensor(rstd[:], rstd[:], exponent[:], ALU.pow).then_inc(pow_chain, 1)

            @block.vector
            def _(dve):
                for k in range(B * T):
                    nc.vector.bn_stats(stats[:, k], x3[:, k]).then_inc(chain, 1)
                    dve.wait_ge(chain, 2 * k + 1)
                    nc.vector.bn_aggr(mv[:, k], stats[:, k]).then_inc(chain, 1)
                dve.wait_ge(chain, 2 * B * T)
                nc.vector.tensor_scalar(rstd[:], mv[:, :, 1:2], 1e-5, None, ALU.add).then_inc(chain, 1)
                dve.wait_ge(pow_chain, 2)
                dve.wait_ge(kept, 16)
                for k in range(B * T):
                    nc.vector.tensor_scalar(x3[:, k], x3[:, k], mv[:, k, 0:1], rstd[:, k], ALU.subtract, ALU.mult).then_inc(chain, 1)
                dve.wait_ge(chain, 3 * B * T + 1)
        clear(nc, sems.all)


def finish(nc, mem, w, out):
    x_all = mem["x_all"]
    with ExitStack() as ctx:
        kept = ctx.enter_context(nc.sbuf_tensor("kept_x", [P, B, T * D], F32))
        sems = Semaphores(nc, ctx, "fin", "loaded added stored")
        loaded, added, stored = sems.all
        with nc.Block() as block:
            @block.sync
            def _(sp):
                for b in range(B):
                    sp.dma_start(kept[:, b], w["x_kept"][:, b * T * D:(b + 1) * T * D]).then_inc(loaded, 16)
                    sp.wait_ge(loaded, 16 * (b + 1))
                for b in range(B):
                    sp.wait_ge(added, b + 1)
                    sp.dma_start(out[b].rearrange("(t p) d -> p t d", p=P), x_all[:, b].rearrange("p (t d) -> p t d", t=T)).then_inc(stored, 16)
                sp.wait_ge(stored, 16 * B)

            @block.vector
            def _(dve):
                for b in range(B):
                    dve.wait_ge(loaded, 16 * (b + 1))
                    nc.vector.tensor_tensor(x_all[:, b], x_all[:, b], kept[:, b], ALU.add).then_inc(added, 1)
        clear(nc, sems.all)


def program(nc, a, out):
    w = {"x": a["x"], "ident": a["c_ident"], "shift": a["c_shift"], "win_mask": a["c_win_mask"], "rope1": a["c_rope1"],
         "rope0": a["c_rope0"], "causal": a["c_causal"], "ones": a["c_ones"], "upper": a["c_upper"],
         "ctx": a["ctx_2048"], "mask": a["mask_BxS2_ik0"],
         "Wq": a["L0_xattn_Wq"], "Wkv": a["L0_xattn_Wkv"], "null_kv": a["L0_xattn_null_kv"], "Wout": a["L0_xattn_Wout"],
         "ln_scale": a["L0_xattn_ln_scale"], "ln_bias": a["L0_xattn_ln_bias"],
         "w_qkv": a["L0_ffn_w_qkv"], "w_o": a["L0_ffn_w_o"], "w_router": a["L0_ffn_w_router"], "g12": a["c_l0_g12"],
         "w1": a["L0_ffn_w1"], "w2": a["L0_ffn_w2"], "b": a["L1_xattn_b"],
         "Wqkv": a["L1_ffn_Wqkv"], "qk_scale": (a["L1_ffn_q_scale"], a["L1_ffn_k_scale"]), "Wo": a["L1_ffn_Wo"],
         "W1": a["L1_ffn_W1"], "cols": a["c_l1_cols"], "W2": a["L1_ffn_W2"], "b2": a["L1_ffn_b2"]}
    w["x_kept"] = nc.dram_tensor("x_kept", (P, B * T * D), F32, kind="Internal").ap()
    with ExitStack() as ctx:
        psum = ctx.enter_context(nc.psum_tensor("psum", [P, 8, 512], F32))
        mem = {"x_all": ctx.enter_context(nc.sbuf_tensor("x_all", [P, B, T * D], F32)),
               "ident": ctx.enter_context(nc.sbuf_tensor("ident", [P, P], F32)),
               "ident_bf": ctx.enter_context(nc.sbuf_tensor("ident_bf", [P, P], BF16)),
               "psum": psum, "bank": [psum[:, i] for i in range(8)]}
        constants(nc, mem, w)
        with ExitStack() as l0:
            for name, shape in (("stats", [P, T, 6]), ("mv", [P, T, 2]), ("rstd", [P, T]), ("exponent", [P, T])):
                mem[name] = l0.enter_context(nc.sbuf_tensor(name, shape, F32))
            mem["norm_sems"] = Semaphores(nc, l0, "nm", "mv_done chain pow_done scaled")
            setup_exponent(nc, mem)
            null_attention(nc, mem, w)
            with ExitStack() as moe:
                mem["moe_inT"] = moe.enter_context(nc.sbuf_tensor("moe_inT", [P, B, DC, S], F32))
                mem["logits"] = moe.enter_context(nc.sbuf_tensor("logits", [P, B, T, E], F32))
                mem["gates"] = moe.enter_context(nc.sbuf_tensor("gates", [P, NT, E], F32))
                causal_attention(nc, mem, w)
                gating(nc, mem, w)
                experts(nc, mem, w)
            memory_attention(nc, mem, w)
        layer_norm(nc, mem, w)
        local_layers(nc, mem, w)
        finish(nc, mem, w, out)


def shape_constants():
    f = np.float32
    out = {"c_ident": np.eye(P, dtype=f)}
    shift = np.zeros((2, P, P), f)
    shift[0, np.arange(P - 1), np.arange(1, P)] = 1.0
    shift[1, P - 1, 0] = 1.0
    out["c_shift"] = shift
    i = np.arange(WIN)[:, None]
    k = np.arange(WIN)[None, :]
    own, before = np.where(k <= i, 0, NEG), np.where(k >= i, 0, NEG)
    both = np.concatenate([before, own], 1)
    first = np.concatenate([np.full_like(before, NEG), own], 1)
    out["c_win_mask"] = np.stack([np.concatenate([first, both], 0), np.concatenate([both, both], 0)]).astype(f)
    half = np.arange(0, DH, 2, dtype=f)
    inv = (f(1.0) / f(10000.0) ** (half / f(DH))).astype(f)
    t = np.arange(S, dtype=f)
    fr = t[:, None] * inv[None, :]
    fr = np.concatenate([fr, fr], -1)
    base = (half + f(0.4 * DH)) / f(1.4 * DH)
    power = (t - S // 2) / f(WIN // 2)
    sc = base[None, :] ** power[:, None]
    sc = np.concatenate([sc, sc], -1).astype(f)
    sign = np.where(np.arange(DH) < HALF, -1.0, 1.0).astype(f)
    cos, sin = np.cos(fr), np.sin(fr) * sign
    out["c_rope1"] = np.stack([cos * sc, sin * sc, cos * (f(1.0) / sc), sin * (f(1.0) / sc)]).astype(f)
    theta = f(10000.0) ** (f(-2.0) * (np.arange(HD // 2, dtype=f) / f(HD)))
    fr0 = (t[:, None] * theta[None, :].astype(f)).astype(f)
    cos0 = np.repeat(np.cos(fr0), 2, axis=1)
    sin0 = np.repeat(np.sin(fr0), 2, axis=1) * np.where(np.arange(HD) % 2 == 0, -1.0, 1.0)
    out["c_rope0"] = np.stack([cos0, sin0], 1).astype(f)
    q = np.arange(P)
    out["c_causal"] = np.where(q[None, :] <= q[:, None], 0, NEG).astype(f)
    out["c_ones"] = np.ones((P, P), f)
    out["c_upper"] = (q[:, None] < q[None, :]).astype(f)
    return out


_INS = ['x', 'ctx_2048', 'mask_BxS2_ik0', 'L0_xattn_Wq', 'L0_xattn_Wkv', 'L0_xattn_null_kv', 'L0_xattn_Wout', 'L0_xattn_ln_scale', 'L0_xattn_ln_bias', 'L0_ffn_w_qkv', 'L0_ffn_w_o', 'L0_ffn_w_router', 'L0_ffn_w1', 'L0_ffn_w2', 'L1_xattn_b', 'L1_ffn_Wqkv', 'L1_ffn_q_scale', 'L1_ffn_k_scale', 'L1_ffn_Wo', 'L1_ffn_W1', 'L1_ffn_W2', 'L1_ffn_b2']
_OUT = (B, S, D)


def l1_columns(b1, ln_g, ln_b):
    halves = b1.reshape(DEPTH, 2, FI)
    padded = np.zeros((DEPTH, 2, FC * P), b1.dtype)
    padded[:, :, 0:FI] = halves
    columns = [padded.reshape(DEPTH, 2 * FC, P), ln_g.reshape(DEPTH, DC, P), ln_b.reshape(DEPTH, DC, P)]
    return np.ascontiguousarray(np.concatenate(columns, 1).transpose(0, 2, 1))


def kernel(**inputs):
    import concourse.bacc as bacc
    from concourse.bass_utils import run_bass_kernel_spmd

    nc = bacc.Bacc("TRN2", target_bir_lowering=False, num_devices=1)
    arrays = {name: np.ascontiguousarray(inputs[name]) for name in _INS}
    arrays.update(shape_constants())
    arrays["c_l1_cols"] = l1_columns(*(np.asarray(inputs[n]) for n in ("L1_ffn_b1", "L1_ffn_ln_g", "L1_ffn_ln_b")))
    arrays["c_l0_g12"] = np.ascontiguousarray(np.concatenate([np.asarray(inputs[n]).reshape(DC, P) for n in ("L0_ffn_g1", "L0_ffn_g2")]).T)
    aps = {name: nc.dram_tensor(name, a.shape, mybir.dt.from_np(a.dtype), kind="ExternalInput").ap() for name, a in arrays.items()}
    out = nc.dram_tensor("out", _OUT, F32, kind="ExternalOutput").ap()
    program(nc, aps, out)
    return run_bass_kernel_spmd(nc, [arrays], core_ids=[0]).results[0]["out"]
```

```python
from contextlib import ExitStack

import numpy as np
import concourse.bass as bass
from concourse import mybir

F32 = mybir.dt.float32
BF16 = mybir.dt.bfloat16
I32 = mybir.dt.int32
ALU = mybir.AluOpType
ACT = mybir.ActivationFunctionType
AX = mybir.AxisListType.X

P = 128
B, S, D = 4, 512, 256
T = S // P
DC = D // P
NEG = -1e30

DEPTH, HEADS, DH, WIN = 6, 16, 64, 64
INNER = HEADS * DH
FI = int(D * 4 * 2 / 3)
FC = -(-FI // P)
FR = FI - (FC - 1) * P
HALF = DH // 2
GROUP = 4
NG = T * HEADS // GROUP
QK_SCALE = 8.0


def rows(tensor, p=P):
    return tensor.rearrange("(t p) d -> p t d", p=p)


def clear(nc, sems):
    nums = [s.num for s in sems]
    assert nums == list(range(nums[0], nums[0] + len(nums)))
    nc.gpsimd.sem_clear(range(nums[0], nums[0] + len(nums)))
    nc.all_engine_barrier()


class Semaphores:

    def __init__(self, nc, ctx, stage, names):
        self.all = [ctx.enter_context(nc.semaphore(f"s_{stage}_{n}")) for n in names.split()]
        self.by_name = dict(zip(names.split(), self.all))

    def __getitem__(self, name):
        return self.by_name[name]




def normalise(nc, mem, src, dst, eps, centred):
    stats, mv, rstd, exponent = mem["stats"], mem["mv"], mem["rstd"], mem["exponent"]
    sems = mem["norm_sems"]
    mv_done, chain, pow_done, scaled = sems.all
    with nc.Block() as block:
        @block.vector
        def _(dve):
            for t in range(T):
                nc.vector.bn_stats(stats[:, t], src(t)).then_inc(chain, 1)
            for t in range(T):
                dve.wait_ge(chain, t + 1)
                nc.vector.bn_aggr(mv[:, t], stats[:, t]).then_inc(mv_done, 1)
            dve.wait_ge(mv_done, T)
            if centred:
                nc.vector.tensor_scalar(rstd[:], mv[:, :, 1], eps, None, ALU.add).then_inc(chain, 1)
            else:
                nc.vector.tensor_tensor(rstd[:], mv[:, :, 0], mv[:, :, 0], ALU.mult).then_inc(mv_done, 1)
                dve.wait_ge(mv_done, T + 1)
                nc.vector.scalar_tensor_tensor(rstd[:], mv[:, :, 1], eps, rstd[:], ALU.add, ALU.add).then_inc(chain, 1)
            dve.wait_ge(pow_done, 1)
            for t in range(T):
                if centred:
                    nc.vector.tensor_scalar(dst(t), src(t), mv[:, t, 0:1], rstd[:, t:t + 1], ALU.subtract, ALU.mult).then_inc(scaled, 1)
                else:
                    nc.vector.tensor_scalar(dst(t), src(t), rstd[:, t:t + 1], None, ALU.mult).then_inc(scaled, 1)
            dve.wait_ge(scaled, T)

        @block.gpsimd
        def _(pool):
            pool.wait_ge(chain, T + 1)
            nc.gpsimd.tensor_tensor(rstd[:], rstd[:], exponent[:], ALU.pow).then_inc(pow_done, 1)
            pool.wait_ge(pow_done, 1)
    clear(nc, sems.all)



CTX, M = 512, 64
CC = CTX // P
MN = M + 1


def null_attention(nc, mem, w):
    with ExitStack() as ctx:
        def sb(name, shape, dt=F32):
            return ctx.enter_context(nc.sbuf_tensor("xa_" + name, shape, dt))

        x_all, ident, bank = mem["x_all"], mem["ident"], mem["bank"]
        wq = sb("wq", [P, DC, INNER])
        wkv = sb("wkv", [P, CC, 2 * INNER])
        wout = sb("wout", [P, INNER // P, D])
        ln_scale = sb("ln_scale", [P, D])
        ln_bias = sb("ln_bias", [P, D])
        null_k = sb("null_k", [P, 1])
        null_v = sb("null_v", [MN, DH])
        x = sb("x", [P, T, D])
        xn = sb("xn", [P, T, D])
        xnT = sb("xnT", [P, DC, S])
        context = sb("context", [M, CTX])
        contextT = sb("contextT", [P, CC, M])
        qT = sb("qT", [P, INNER // P, S])
        kT = sb("kT", [P, INNER // P, MN])
        v = sb("v", [MN, HEADS, DH + 1])
        smax = sb("smax", [P, 2, GROUP])
        prob = sb("prob", [P, 4, GROUP, MN])
        probT = sb("probT", [MN, 2, GROUP * P])
        rsum = sb("rsum", [P, 2, GROUP])
        o = sb("o", [P, 2, INNER])
        oT = sb("oT", [P, INNER])
        y = sb("y", [P, T, D])

        sems = Semaphores(nc, ctx, "xa", "wload setup xin ctx_in xt_full xt_read ct_full ct_read kv_full kv_read q_full q_read "
                          "s_full s_read exp_done tr_full tr_read o_full o_read dve_chain back")
        (wload, setup, xin, ctx_in, xt_full, xt_read, ct_full, ct_read, kv_full, kv_read, q_full, q_read,
         s_full, s_read, exp_done, tr_full, tr_read, o_full, o_read, dve_chain, back) = sems.all

        with nc.Block() as block:
            @block.sync
            def _(sp):
                sp.dma_start(wq[:], w["Wq"].rearrange("(c p) n -> p c n", p=P)).then_inc(wload, 16)
                sp.dma_start(wout[:], w["Wout"].rearrange("(c p) n -> p c n", p=P)).then_inc(wload, 16)
                sp.dma_start(ln_scale[:], w["ln_scale"][None, :].to_broadcast([P, D])).then_inc(wload, 16)
                sp.dma_start(ln_bias[:], w["ln_bias"][None, :].to_broadcast([P, D])).then_inc(wload, 16)
                for r in range(2):
                    sp.dma_start(null_k[r * DH:(r + 1) * DH, :], w["null_kv"][0, :, None]).then_inc(wload, 16)
                sp.dma_start(null_v[M:MN, :], w["null_kv"][1, None, :]).then_inc(wload, 16)
                sp.wait_ge(wload, 16 * 8)

            @block.scalar
            def _(act):
                act.dma_start(wkv[:], w["Wkv"].rearrange("(c p) n -> p c n", p=P)).then_inc(wload, 16)

            @block.vector
            def _(dve):
                nc.vector.memset(v[:], 1.0).then_inc(setup, 1)
                dve.wait_ge(setup, 1)
                dve.wait_ge(wload, 16 * 8)
                nc.vector.tensor_copy(v[M:MN, :, 0:DH], null_v[M:MN, None, :].to_broadcast([1, HEADS, DH])).then_inc(setup, 1)
                nc.vector.tensor_copy(kT[:, :, M:MN], null_k[:, None, :].to_broadcast([P, INNER // P, 1])).then_inc(setup, 1)
                dve.wait_ge(setup, 3)
        clear(nc, sems.all)

        attention = []
        for k in range(NG // 2 + 3):
            def pair(kind, first):
                if 0 <= first < NG:
                    attention.extend([(kind, first), (kind, first + 1)])
            t, ends = (2 * k - 4) // GROUP, (2 * k - 2) % GROUP == 0
            pair("scores", 2 * k)
            if not ends and 0 <= t - 1 < T:
                attention.append(("project", t - 1))
            pair("values", 2 * k - 4)
            pair("probT", 2 * k - 2)
            pair("exp", 2 * k)
            if ends and 0 <= t < T:
                attention += [("oT", 2 * t), ("oT", 2 * t + 1)]
        tr_turn = {key: n for n, key in enumerate([a for a in attention if a[0] in ("probT", "oT")])}
        out_turn = {key: n for n, key in enumerate([a for a in attention if a[0] in ("values", "project")])}

        with nc.Fori(0, B) as b:
            with nc.Block() as block:
                @block.vector
                def _(dve):
                    nc.vector.tensor_copy(x[:].rearrange("p t d -> p (t d)"), x_all[:, b]).then_inc(xin, 1)
                    dve.wait_ge(xin, 1)

                @block.sync
                def _(sp):
                    sp.dma_start(context[:], w["ctx"][b]).then_inc(ctx_in, 16)
                    sp.wait_ge(ctx_in, 16)
            clear(nc, sems.all)
            normalise(nc, mem, lambda t: x[:, t], lambda t: xn[:, t], 1e-5, True)

            with nc.Block() as block:
                @block.tensor
                def _(pe):
                    for d in range(DC):
                        for t in range(T):
                            mm = nc.tensor.transpose(bank[d][:, t * P:(t + 1) * P], xn[:, t, d * P:(d + 1) * P], ident[:])
                        mm.then_inc(xt_full, 1)
                    for c in range(CC):
                        mm = nc.tensor.transpose(bank[2][:, c * M:(c + 1) * M], context[:, c * P:(c + 1) * P], ident[0:M, 0:M])
                    mm.then_inc(ct_full, 1)
                    pe.wait_ge(ct_read, 1)
                    for c in range(INNER // P):
                        for k in range(CC):
                            mm = nc.tensor.matmul(bank[3][:, c * M:(c + 1) * M], wkv[:, k, c * P:(c + 1) * P], contextT[:, k, :],
                                                  start=(k == 0), stop=(k == CC - 1), skip_group_check=True)
                    mm.then_inc(kv_full, 1)
                    for n in range(2):
                        for k in range(CC):
                            mm = nc.tensor.matmul(bank[4 + n][0:M, :], contextT[:, k, :], wkv[:, k, INNER + n * S:INNER + (n + 1) * S],
                                                  start=(k == 0), stop=(k == CC - 1))
                        mm.then_inc(kv_full, 1)
                    pe.wait_ge(xt_read, DC)
                    for c in range(INNER // P):
                        if c >= 2:
                            pe.wait_ge(q_read, c - 1)
                        for d in range(DC):
                            mm = nc.tensor.matmul(bank[6 + c % 2][:], wq[:, d, c * P:(c + 1) * P], xnT[:, d, :], start=(d == 0), stop=(d == DC - 1))
                        mm.then_inc(q_full, 1)

                    pe.wait_ge(kv_read, 3)
                    pe.wait_ge(q_read, INNER // P)
                    for kind, n in attention:
                        t, hg = n // GROUP, n % GROUP
                        if kind == "scores" and n % 2 == 0:
                            if n >= 4:
                                pe.wait_ge(s_read, n - 2)
                            for j in range(GROUP):
                                c = GROUP * (hg // 2) + j
                                for k in range(2):
                                    r = DH * k
                                    mm = nc.tensor.matmul(bank[(n + k) % 4][:, j * MN:(j + 1) * MN], qT[r:r + DH, c, t * P:(t + 1) * P],
                                                          kT[r:r + DH, c, :], start=True, stop=True, skip_group_check=True)
                                    if j == GROUP - 1:
                                        mm.then_inc(s_full, 1)
                        elif kind in ("probT", "oT"):
                            u = tr_turn[kind, n]
                            if u >= 2:
                                pe.wait_ge(tr_read, u - 1)
                            if kind == "probT":
                                pe.wait_ge(exp_done, n + 1)
                                for j in range(GROUP):
                                    mm = nc.tensor.transpose(bank[4 + u % 2][0:MN, j * P:(j + 1) * P], prob[:, n % 4, j, :], ident[:])
                            else:
                                pe.wait_ge(o_read, out_turn["values", GROUP * (n // 2) + GROUP - 1] + 1)
                                for j in range(4):
                                    at = (n % 2) * S + j * P
                                    mm = nc.tensor.transpose(bank[4 + u % 2][:, j * P:(j + 1) * P], o[:, (n // 2) % 2, at:at + P], ident[:])
                            mm.then_inc(tr_full, 1)
                        elif kind == "values":
                            u = out_turn[kind, n]
                            pe.wait_ge(tr_read, tr_turn["probT", n] + 1)
                            if u >= 2:
                                pe.wait_ge(o_read, u - 1)
                            for j in range(GROUP):
                                mm = nc.tensor.matmul(bank[6 + u % 2][:, j * MN:(j + 1) * MN], probT[:, n % 2, j * P:(j + 1) * P],
                                                      v[:, 2 * (GROUP * (hg // 2) + j) + hg % 2, :], start=True, stop=True, skip_group_check=True)
                            mm.then_inc(o_full, 1)
                        elif kind == "project":
                            u = out_turn[kind, n]
                            pe.wait_ge(tr_read, tr_turn["oT", 2 * n + 1] + 1)
                            pe.wait_ge(o_read, u - 1)
                            for c in range(INNER // P):
                                mm = nc.tensor.matmul(bank[6 + u % 2][:, 0:D], oT[:, c * P:(c + 1) * P], wout[:, c, :],
                                                      start=(c == 0), stop=(c == INNER // P - 1))
                            mm.then_inc(o_full, 1)

                @block.scalar
                def _(act):
                    for d in range(DC):
                        act.wait_ge(xt_full, d + 1)
                        nc.scalar.copy(xnT[:, d, :], bank[d][:]).then_inc(xt_read, 1)
                    act.wait_ge(ct_full, 1)
                    nc.scalar.copy(contextT[:].rearrange("p c m -> p (c m)"), bank[2][:, 0:CC * M]).then_inc(ct_read, 1)
                    act.wait_ge(kv_full, 1)
                    nc.scalar.copy(kT[:, :, 0:M], bank[3][:].rearrange("p (c m) -> p c m", m=M)).then_inc(kv_read, 1)
                    for n in range(2):
                        act.wait_ge(kv_full, n + 2)
                        nc.scalar.copy(v[0:M, 8 * n:8 * n + 8, 0:DH], bank[4 + n][0:M, :].rearrange("p (h d) -> p h d", h=8)).then_inc(kv_read, 1)
                    for c in range(INNER // P):
                        act.wait_ge(q_full, c + 1)
                        nc.scalar.mul(qT[:, c, :], bank[6 + c % 2][:], DH ** -0.5).then_inc(q_read, 1)
                    for kind, n in attention:
                        if kind == "exp":
                            act.wait_ge(s_read, n + 1)
                            nc.scalar.activation(prob[:, n % 4], prob[:, n % 4], ACT.Exp).then_inc(exp_done, 1)
                        elif kind == "probT":
                            u = tr_turn[kind, n]
                            act.wait_ge(tr_full, u + 1)
                            if n >= 2:
                                act.wait_ge(o_full, out_turn["values", n - 2] + 1)
                            nc.scalar.copy(probT[:, n % 2], bank[4 + u % 2][0:MN, :]).then_inc(tr_read, 1)
                        elif kind == "oT":
                            u = tr_turn[kind, n]
                            act.wait_ge(tr_full, u + 1)
                            if n >= 2:
                                act.wait_ge(o_full, out_turn["project", n // 2 - 1] + 1)
                            nc.scalar.copy(oT[:, (n % 2) * S:(n % 2 + 1) * S], bank[4 + u % 2][:]).then_inc(tr_read, 1)

                @block.vector
                def _(dve):
                    links = [0]

                    def link(ins):
                        links[0] += 1
                        ins.then_inc(dve_chain, 1)
                        dve.wait_ge(dve_chain, links[0])

                    for kind, n in attention:
                        if kind == "scores":
                            dve.wait_ge(s_full, n + 1)
                            s3 = bank[n % 4][:, 0:GROUP * MN].rearrange("p (g q) -> p g q", g=GROUP)
                            link(nc.vector.tensor_reduce(smax[:, n % 2], s3, AX, ALU.max))
                            if n >= 4:
                                dve.wait_ge(tr_full, tr_turn["probT", n - 4] + 1)
                            nc.vector.tensor_tensor(prob[:, n % 4], s3, smax[:, n % 2, :, None].to_broadcast([P, GROUP, MN]),
                                                    ALU.subtract).then_inc(s_read, 1)
                        elif kind == "values":
                            t, hg = n // GROUP, n % GROUP
                            u = out_turn[kind, n]
                            dve.wait_ge(o_full, u + 1)
                            if n % GROUP == 0 and t >= 2:
                                dve.wait_ge(tr_full, tr_turn["oT", 2 * (t - 2) + 1] + 1)
                            ob = bank[6 + u % 2][:, 0:GROUP * MN].rearrange("p (g d) -> p g d", g=GROUP)
                            link(nc.vector.reciprocal(rsum[:, n % 2, :, None], ob[:, :, DH:MN]))
                            nc.vector.tensor_tensor(o[:, t % 2].rearrange("p (a g b d) -> p a g b d", a=2, g=GROUP, b=2)[:, hg // 2, :, hg % 2],
                                                    ob[:, :, 0:DH], rsum[:, n % 2, :, None].to_broadcast([P, GROUP, DH]),
                                                    ALU.mult).then_inc(o_read, 1)
                        elif kind == "project":
                            u = out_turn[kind, n]
                            dve.wait_ge(o_full, u + 1)
                            nc.vector.tensor_copy(y[:, n, :], bank[6 + u % 2][:, 0:D]).then_inc(o_read, 1)
                    dve.wait_ge(o_read, len(out_turn))
            clear(nc, sems.all)
            normalise(nc, mem, lambda t: y[:, t], lambda t: y[:, t], 1e-6, True)
            with nc.Block() as block:
                @block.vector
                def _(dve):
                    nc.vector.tensor_tensor(y[:], y[:], ln_scale[:, None, :].to_broadcast([P, T, D]), ALU.mult).then_inc(back, 1)
                    dve.wait_ge(back, 1)
                    nc.vector.tensor_tensor(y[:], y[:], ln_bias[:, None, :].to_broadcast([P, T, D]), ALU.add).then_inc(back, 1)
                    dve.wait_ge(back, 2)
                    nc.vector.tensor_tensor(x_all[:, b], x[:].rearrange("p t d -> p (t d)"), y[:].rearrange("p t d -> p (t d)"), ALU.add).then_inc(back, 1)
                    dve.wait_ge(back, 3)
            clear(nc, sems.all)



HD = D // HEADS
SLOT = 32
HPC = P // SLOT
HC = HEADS // HPC
E, FF = 8, 512


def causal_attention(nc, mem, w):
    with ExitStack() as ctx:
        def sb(name, shape, dt=F32):
            return ctx.enter_context(nc.sbuf_tensor("ca_" + name, shape, dt))

        x_all, ident, ident_bf, bank = mem["x_all"], mem["ident"], mem["ident_bf"], mem["bank"]
        wqkv = sb("wqkv", [P, DC, 3 * D])
        wo = sb("wo", [P, HC, D])
        wr = sb("wr", [P, DC, E])
        g12 = sb("g12", [P, 2 * DC])
        rope = sb("rope", [P, T, 2, HD])
        causal = sb("causal", [P, P])
        causal_bf = sb("causal_bf", [P, P], BF16)
        z = sb("z", [P, T, D])
        zr = sb("zr", [P, T, D])
        zT = sb("zT", [P, DC, S])
        cosd = sb("cosd", [P, 2, 2 * D])
        rot = sb("rot", [P, 2, 2 * D])
        qk = sb("qk", [P, 2, 2 * HEADS, SLOT])
        qT = sb("qT", [P, HC, S])
        kT = sb("kT", [P, HC, S])
        v = sb("v", [P, T, HEADS, SLOT])
        smax = sb("smax", [P, 2 * HPC])
        total = sb("total", [P, 2 * HPC])
        prob = sb("prob", [P, HPC, S])
        probT = sb("probT", [P, 2 * HPC, S])
        oT = sb("oT", [P, 2, HC, P])
        sems = Semaphores(nc, ctx, "ca", "wload setup xin zt_full zt_read qk_full qk_read v_read padded tr_full tr_read s_full "
                          "max_done exp_done normed o_full o_read p_full p_read dve_chain back")
        (wload, setup, xin, zt_full, zt_read, qk_full, qk_read, v_read, padded, tr_full, tr_read, s_full,
         max_done, exp_done, normed, o_full, o_read, p_full, p_read, dve_chain, back) = sems.all
        HS = HD ** -0.5

        with nc.Block() as block:
            @block.sync
            def _(sp):
                sp.dma_start(wqkv[:], w["w_qkv"].rearrange("(c p) n -> p c n", p=P)).then_inc(wload, 16)
                sp.wait_ge(setup, 1)
                for h in range(HPC):
                    sp.dma_start(wo[h * SLOT:h * SLOT + HD], w["w_o"].rearrange("(c h i) n -> h i c n", h=HPC, i=HD)[h]).then_inc(wload, 16)
                sp.dma_start(wr[:], w["w_router"].rearrange("(c p) n -> p c n", p=P)).then_inc(wload, 16)
                sp.dma_start(g12[:], w["g12"]).then_inc(wload, 16)
                sp.dma_start(rope[:], w["rope0"].rearrange("(t p) k d -> p t k d", p=P)).then_inc(wload, 16)
                sp.dma_start(causal[:], w["causal"]).then_inc(wload, 16)
                sp.wait_ge(wload, 16 * (5 + HPC))

            @block.vector
            def _(dve):
                nc.vector.memset(wo[:], 0.0).then_inc(setup, 1)
                nc.vector.memset(v[:], 0.0).then_inc(setup, 1)
                nc.vector.memset(qk[:], 0.0).then_inc(setup, 1)
                dve.wait_ge(wload, 16 * (5 + HPC))
                nc.vector.tensor_copy(causal_bf[:], causal[:]).then_inc(setup, 1)
                dve.wait_ge(setup, 4)
        clear(nc, sems.all)

        pairs = T * HEADS // 2
        attention = []
        for k in range(pairs + 7):
            if k < pairs:
                attention.append(("scores", k))
            if 0 <= k - 1 < pairs:
                attention += [("exp", 2 * (k - 1)), ("exp", 2 * (k - 1) + 1)]
            r = (k - 4) // 2
            if k % 2 == 1 and r >= 0 and r % HC == HC - 1:
                attention.append(("project", r // HC))
            if k % 2 == 0 and 0 <= r < T * HC:
                attention += [("values", r), ("gather", r)]
            if 0 <= k - 2 < pairs:
                attention += [("probT", 2 * (k - 2)), ("probT", 2 * (k - 2) + 1)]
            if 0 <= k - 1 < pairs:
                attention.append(("norm", k - 1))
        tr_turn = {key: n for n, key in enumerate([("qk", n) for n in range(2 * T)] + [a for a in attention if a[0] == "probT"])}

        with nc.Fori(0, B) as b:
            with nc.Block() as block:
                @block.vector
                def _(dve):
                    nc.vector.tensor_copy(z[:].rearrange("p t d -> p (t d)"), x_all[:, b]).then_inc(xin, 1)
                    dve.wait_ge(xin, 1)
            clear(nc, sems.all)
            normalise(nc, mem, lambda t: z[:, t], lambda t: z[:, t], 1e-5, True)
            normalise(nc, mem, lambda t: z[:, t], lambda t: zr[:, t], 1e-6, False)

            with nc.Block() as block:
                @block.tensor
                def _(pe):
                    for d in range(DC):
                        for t in range(T):
                            mm = nc.tensor.transpose(bank[d][:, t * P:(t + 1) * P], zr[:, t, d * P:(d + 1) * P], ident[:])
                        mm.then_inc(zt_full, 1)
                    pe.wait_ge(zt_read, DC)
                    for t in range(T + 1):
                        if t < T:
                            if t >= 2:
                                pe.wait_ge(qk_read, t - 1)
                                pe.wait_ge(v_read, t - 1)
                            for at, n, to in ((0, 2 * D, bank[t % 2]), (2 * D, D, bank[2 + t % 2])):
                                for d in range(DC):
                                    mm = nc.tensor.matmul(to[:, 0:n], zT[:, d, t * P:(t + 1) * P], wqkv[:, d, at:at + n],
                                                          start=(d == 0), stop=(d == DC - 1))
                                mm.then_inc(qk_full, 1)
                        if t >= 1:
                            pe.wait_ge(padded, t)
                            for part in range(2):
                                u = 2 * (t - 1) + part
                                if u >= 2:
                                    pe.wait_ge(tr_read, u - 1)
                                for c in range(HC):
                                    head = part * HEADS + c * HPC
                                    mm = nc.tensor.transpose(bank[4 + u % 2][:, c * P:(c + 1) * P],
                                                             qk[:, (t - 1) % 2, head:head + HPC, :].rearrange("p h d -> p (h d)"), ident[:])
                                mm.then_inc(tr_full, 1)
                    pe.wait_ge(tr_read, 2 * T)
                    pe.wait_ge(v_read, T)
                    for kind, n in attention:
                        if kind == "scores":
                            t, c = n // (HEADS // 2), n // 2 % HC
                            keys = (t + 1) * P
                            if n >= 2:
                                pe.wait_ge(exp_done, 2 * n - 2)
                            for h in range(2):
                                r = SLOT * ((2 * n + h) % HPC)
                                nc.tensor.matmul(bank[(2 * n + h) % 4][:, 0:keys], qT[r:r + SLOT, c, t * P:(t + 1) * P], kT[r:r + SLOT, c, 0:keys],
                                                 start=True, stop=False)
                            for h in range(2):
                                nc.tensor.matmul(bank[(2 * n + h) % 4][:, t * P:keys], ident_bf[:], causal_bf[:], start=False, stop=True).then_inc(s_full, 1)
                        elif kind == "probT":
                            u = tr_turn[kind, n]
                            pe.wait_ge(tr_read, u - 1)
                            pe.wait_ge(normed, n + 1)
                            for k in range(n // HEADS + 1):
                                mm = nc.tensor.transpose(bank[4 + u % 2][:, k * P:(k + 1) * P], prob[:, n % HPC, k * P:(k + 1) * P], ident[:])
                            mm.then_inc(tr_full, 1)
                        elif kind == "values":
                            t, c = n // HC, n % HC
                            pe.wait_ge(tr_read, tr_turn["probT", HPC * n + HPC - 1] + 1)
                            if t >= 1:
                                pe.wait_ge(o_read, n - HC + 1)
                            for k in range(t + 1):
                                for h in range(HPC):
                                    mm = nc.tensor.matmul(bank[6][h * SLOT:(h + 1) * SLOT, c * P:(c + 1) * P], v[:, k, HPC * c + h, :],
                                                          probT[:, (HPC * n + h) % (2 * HPC), k * P:(k + 1) * P],
                                                          start=(k == 0), stop=(k == t), skip_group_check=True)
                            mm.then_inc(o_full, 1)
                        elif kind == "project":
                            pe.wait_ge(o_read, HC * n + HC)
                            if n >= 1:
                                pe.wait_ge(p_read, n)
                            for c in range(HC):
                                mm = nc.tensor.matmul(bank[7][:, 0:D], oT[:, n % 2, c], wo[:, c, :], start=(c == 0), stop=(c == HC - 1))
                            mm.then_inc(p_full, 1)

                @block.scalar
                def _(act):
                    for d in range(DC):
                        act.wait_ge(zt_full, d + 1)
                        nc.scalar.mul(zT[:, d, :], bank[d][:], g12[:, d:d + 1]).then_inc(zt_read, 1)
                    for t in range(T + 1):
                        if t < T:
                            act.wait_ge(qk_full, 2 * t + 2)
                            nc.scalar.copy(v[:, t, :, 0:HD], bank[2 + t % 2][:, 0:D].rearrange("p (h d) -> p h d", h=HEADS)).then_inc(v_read, 1)
                        if t >= 1:
                            for part, dst in ((0, qT), (1, kT)):
                                u = 2 * (t - 1) + part
                                act.wait_ge(tr_full, u + 1)
                                nc.scalar.copy(dst[:, :, (t - 1) * P:t * P], bank[4 + u % 2][:].rearrange("p (c q) -> p c q", c=HC)).then_inc(tr_read, 1)
                    for kind, n in attention:
                        if kind == "exp":
                            keys = (n // HEADS + 1) * P
                            act.wait_ge(max_done, n // 2 + 1)
                            if n >= HPC:
                                act.wait_ge(tr_full, tr_turn["probT", n - HPC] + 1)
                            i = n % (2 * HPC)
                            nc.scalar.activation(prob[:, n % HPC, 0:keys], bank[n % HPC][:, 0:keys], ACT.Exp, bias=smax[:, i:i + 1],
                                                 scale=HS, accum_out=total[:, i:i + 1]).then_inc(exp_done, 1)
                        elif kind == "probT":
                            u, keys = tr_turn[kind, n], (n // HEADS + 1) * P
                            act.wait_ge(tr_full, u + 1)
                            if n >= 2 * HPC:
                                act.wait_ge(o_full, n // HPC - 1)
                            nc.scalar.copy(probT[:, n % (2 * HPC), 0:keys], bank[4 + u % 2][:, 0:keys]).then_inc(tr_read, 1)
                        elif kind == "gather":
                            t, c = n // HC, n % HC
                            act.wait_ge(o_full, n + 1)
                            if t >= 2:
                                act.wait_ge(p_full, t - 1)
                            nc.scalar.copy(oT[:, t % 2, c], bank[6][:, c * P:(c + 1) * P]).then_inc(o_read, 1)

                @block.vector
                def _(dve):
                    links = [0]

                    def link(ins):
                        links[0] += 1
                        ins.then_inc(dve_chain, 1)
                        dve.wait_ge(dve_chain, links[0])

                    for t in range(T):
                        dve.wait_ge(qk_full, 2 * t + 1)
                        src = bank[t % 2][:].rearrange("p (h d) -> p h d", d=HD)
                        pairs = bank[t % 2][:].rearrange("p (h k i) -> p h k i", i=2, k=HD // 2)
                        cd = cosd[:, t % 2].rearrange("p (h d) -> p h d", d=HD)
                        rt = rot[:, t % 2].rearrange("p (h d) -> p h d", d=HD)
                        rp = rot[:, t % 2].rearrange("p (h k i) -> p h k i", i=2, k=HD // 2)
                        sn = rope[:, t, 1].rearrange("p (k i) -> p k i", i=2)
                        shape = [P, 2 * HEADS, HD // 2]
                        nc.vector.tensor_tensor(cd, src, rope[:, t, 0, None, :].to_broadcast([P, 2 * HEADS, HD]), ALU.mult).then_inc(dve_chain, 1)
                        nc.vector.tensor_tensor(rp[:, :, :, 0], pairs[:, :, :, 1], sn[:, None, :, 0].to_broadcast(shape), ALU.mult).then_inc(dve_chain, 1)
                        nc.vector.tensor_tensor(rp[:, :, :, 1], pairs[:, :, :, 0], sn[:, None, :, 1].to_broadcast(shape), ALU.mult).then_inc(qk_read, 1)
                        links[0] += 2
                        dve.wait_ge(dve_chain, links[0])
                        dve.wait_ge(qk_read, t + 1)
                        if t >= 2:
                            dve.wait_ge(tr_full, 2 * (t - 1))
                        nc.vector.tensor_tensor(qk[:, t % 2, :, 0:HD], cd, rt, ALU.add).then_inc(padded, 1)

                    for kind, n in attention:
                        if kind == "scores":
                            keys = (2 * n // HEADS + 1) * P
                            i = 2 * n % (2 * HPC)
                            if n >= HPC:
                                dve.wait_ge(exp_done, 2 * (n - HPC) + 2)
                            for h in range(2):
                                dve.wait_ge(s_full, 2 * n + h + 1)
                                red = nc.vector.tensor_reduce(smax[:, i + h:i + h + 1], bank[(2 * n + h) % 4][:, 0:keys], AX, ALU.max)
                            link(red)
                            nc.vector.tensor_scalar(smax[:, i:i + 2], smax[:, i:i + 2], -HS, None, ALU.mult).then_inc(max_done, 1)
                        elif kind == "norm":
                            keys = (2 * n // HEADS + 1) * P
                            i = 2 * n % (2 * HPC)
                            dve.wait_ge(exp_done, 2 * n + 2)
                            link(nc.vector.reciprocal(total[:, i:i + 2], total[:, i:i + 2]))
                            for h in range(2):
                                p1 = prob[:, (2 * n + h) % HPC, 0:keys]
                                nc.vector.tensor_scalar(p1, p1, total[:, i + h:i + h + 1], None, ALU.mult).then_inc(normed, 1)
                        elif kind == "project":
                            dve.wait_ge(p_full, n + 1)
                            nc.vector.tensor_tensor(z[:, n], z[:, n], bank[7][:, 0:D], ALU.add).then_inc(p_read, 1)
                    dve.wait_ge(p_read, T)
            clear(nc, sems.all)
            normalise(nc, mem, lambda t: z[:, t], lambda t: zr[:, t], 1e-6, False)
            with nc.Block() as block:
                @block.tensor
                def _(pe):
                    for d in range(DC):
                        for t in range(T):
                            mm = nc.tensor.transpose(bank[d][:, t * P:(t + 1) * P], zr[:, t, d * P:(d + 1) * P], ident[:])
                        mm.then_inc(zt_full, 1)
                    pe.wait_ge(zt_read, DC)
                    for t in range(T):
                        for d in range(DC):
                            mm = nc.tensor.matmul(bank[2][:, t * E:(t + 1) * E], zT[:, d, t * P:(t + 1) * P], wr[:, d, :],
                                                  start=(d == 0), stop=(d == DC - 1), skip_group_check=True)
                    mm.then_inc(qk_full, 1)

                @block.scalar
                def _(act):
                    for d in range(DC):
                        act.wait_ge(zt_full, d + 1)
                        nc.scalar.mul(zT[:, d, :], bank[d][:], g12[:, DC + d:DC + d + 1]).then_inc(zt_read, 1)
                    act.wait_ge(zt_read, DC)
                    act.copy(mem["moe_inT"][:, b], zT[:]).then_inc(back, 1)
                    act.wait_ge(back, 1)

                @block.vector
                def _(dve):
                    nc.vector.tensor_tensor(x_all[:, b], x_all[:, b], z[:].rearrange("p t d -> p (t d)"), ALU.add).then_inc(setup, 1)
                    dve.wait_ge(qk_full, 1)
                    nc.vector.tensor_copy(mem["logits"][:, b], bank[2][:, 0:T * E].rearrange("p (t e) -> p t e", e=E)).then_inc(setup, 1)
                    dve.wait_ge(setup, 2)
            clear(nc, sems.all)



NT = B * T
TOP_K = 2
CAP = max(-(-(2 * 512 * TOP_K * 5) // (4 * E)), 1)
BITS = 30


def gating(nc, mem, w):
    with ExitStack() as ctx:
        def sb(name, shape, dt=F32):
            return ctx.enter_context(nc.sbuf_tensor("gt_" + name, shape, dt))

        bank = mem["bank"]
        prob = mem["logits"][:].rearrange("p b t e -> p (b t) e")
        gates = mem["gates"]
        ones = sb("ones", [P, P])
        upper = sb("upper", [P, P])
        col = sb("col", [P, NT])
        rcp = sb("rcp", [P, NT])
        rest = sb("rest", [P, NT, E])
        equal = sb("equal", [P, NT, E])
        seen = sb("seen", [P, NT, E])
        first = sb("first", [P, NT, E])
        chosen = sb("chosen", [P, NT, E])
        hit = sb("hit", [P, NT, E])
        count = sb("count", [P, E])
        least = sb("least", [P, E], I32)
        trial = sb("trial", [P, E], I32)
        bit = sb("bit", [P, E], I32)
        bit_f = sb("bit_f", [P, E])
        taken = sb("taken", [P, E], I32)
        room = sb("room", [P, E])
        rank = sb("rank", [P, NT, E])
        before = sb("before", [P, NT, E])
        sems = Semaphores(nc, ctx, "gt", "loaded dve_chain to_exp exp_done counted totals")
        loaded, dve_chain, to_exp, exp_done, counted, totals = sems.all
        wide = [P, NT, E]

        with nc.Block() as block:
            @block.sync
            def _(sp):
                sp.dma_start(ones[:], w["ones"]).then_inc(loaded, 16)
                sp.dma_start(upper[:], w["upper"]).then_inc(loaded, 16)
                sp.wait_ge(loaded, 32)

            @block.scalar
            def _(act):
                act.wait_ge(to_exp, 1)
                nc.scalar.activation(prob, prob, ACT.Exp).then_inc(exp_done, 1)

            @block.vector
            def _(dve):
                links = [0]

                def link(ins):
                    links[0] += 1
                    ins.then_inc(dve_chain, 1)
                    dve.wait_ge(dve_chain, links[0])

                link(nc.vector.tensor_reduce(col[:], prob, AX, ALU.max))
                nc.vector.tensor_tensor(prob, prob, col[:, :, None].to_broadcast(wide), ALU.subtract).then_inc(to_exp, 1)
                dve.wait_ge(exp_done, 1)
                link(nc.vector.tensor_reduce(col[:], prob, AX, ALU.add))
                link(nc.vector.reciprocal(rcp[:], col[:]))
                link(nc.vector.tensor_tensor(prob, prob, rcp[:, :, None].to_broadcast(wide), ALU.mult))
                link(nc.vector.memset(seen[:], 0.0))
                for k in range(TOP_K):
                    src = prob if k == 0 else rest[:]
                    dst = chosen if k == 0 else first
                    link(nc.vector.tensor_reduce(col[:], src, AX, ALU.max))
                    link(nc.vector.tensor_tensor(equal[:], src, col[:, :, None].to_broadcast(wide), ALU.is_equal))
                    for e in range(1, E):
                        link(nc.vector.tensor_tensor(seen[:, :, e], seen[:, :, e - 1], equal[:, :, e - 1], ALU.add))
                    link(nc.vector.scalar_tensor_tensor(dst[:], seen[:], 0.0, equal[:], ALU.is_equal, ALU.mult))
                    if k == 0:
                        link(nc.vector.scalar_tensor_tensor(rest[:], chosen[:], -4.0, prob, ALU.mult, ALU.add))
                link(nc.vector.tensor_tensor(chosen[:], chosen[:], first[:], ALU.add))
                link(nc.vector.tensor_tensor(gates[:], prob, chosen[:], ALU.mult))
                link(nc.vector.memset(least[:], 0))
                link(nc.vector.memset(bit_f[:], float(2 ** (BITS - 1))))
                link(nc.vector.tensor_copy(bit[:], bit_f[:]))
                link(nc.vector.tensor_copy(trial[:], bit[:]))
        clear(nc, sems.all)

        by_expert = "p n e -> p e n"
        bcast = [P, NT, E]

        with nc.Block() as block:
            @block.tensor
            def _(pe):
                with pe.Fori(0, BITS) as i:
                    pe.wait_ge(counted, i + 1)
                    nc.tensor.matmul(bank[0][:, 0:E], ones[:], count[:], start=True, stop=True).then_inc(totals, 1)

            @block.vector
            def _(dve):
                with dve.Fori(0, BITS) as i:
                    nc.vector.tensor_tensor(hit[:], gates[:], trial[:].bitcast(F32)[:, None, :].to_broadcast(bcast), ALU.is_ge).then_inc(dve_chain, 1)
                    dve.wait_ge(dve_chain, 5 * i + 1)
                    nc.vector.tensor_reduce(count[:], hit[:].rearrange(by_expert), AX, ALU.add).then_inc(counted, 1)
                    dve.wait_ge(totals, i + 1)
                    nc.vector.scalar_tensor_tensor(taken[:], bank[0][:, 0:E], float(CAP), bit_f[:], ALU.is_ge, ALU.mult).then_inc(dve_chain, 1)
                    dve.wait_ge(dve_chain, 5 * i + 2)
                    nc.vector.tensor_tensor(least[:], least[:], taken[:], ALU.bitwise_or)
                    nc.vector.tensor_scalar(bit_f[:], bit_f[:], 0.5, None, ALU.mult).then_inc(dve_chain, 1)
                    dve.wait_ge(dve_chain, 5 * i + 3)
                    nc.vector.tensor_copy(bit[:], bit_f[:]).then_inc(dve_chain, 1)
                    dve.wait_ge(dve_chain, 5 * i + 4)
                    nc.vector.tensor_tensor(trial[:], least[:], bit[:], ALU.bitwise_or).then_inc(dve_chain, 1)
                    dve.wait_ge(dve_chain, 5 * i + 5)
        clear(nc, sems.all)

        with nc.Block() as block:
            @block.tensor
            def _(pe):
                pe.wait_ge(counted, 1)
                nc.tensor.matmul(bank[0][:, 0:E], ones[:], count[:], start=True, stop=True).then_inc(totals, 1)
                pe.wait_ge(counted, 2)
                flat = equal[:].rearrange("p n e -> p (n e)")
                nc.tensor.matmul(bank[1][:, 0:NT * E], upper[:], flat, start=True, stop=True).then_inc(totals, 1)
                nc.tensor.matmul(bank[2][:, 0:NT * E], ones[:], flat, start=True, stop=True).then_inc(totals, 1)

            @block.vector
            def _(dve):
                links = [0]

                def link(ins):
                    links[0] += 1
                    ins.then_inc(dve_chain, 1)
                    dve.wait_ge(dve_chain, links[0])

                edge = least[:].bitcast(F32)[:, None, :].to_broadcast(bcast)
                link(nc.vector.tensor_tensor(hit[:], gates[:], edge, ALU.is_gt))
                nc.vector.tensor_reduce(count[:], hit[:].rearrange(by_expert), AX, ALU.add).then_inc(counted, 1)
                nc.vector.tensor_tensor(equal[:], gates[:], edge, ALU.is_equal).then_inc(counted, 1)
                dve.wait_ge(totals, 1)
                link(nc.vector.tensor_scalar(room[:], bank[0][:, 0:E], -1.0, float(CAP), ALU.mult, ALU.add))
                link(nc.vector.memset(before[:, 0, :], 0.0))
                dve.wait_ge(totals, 3)
                tiles = bank[2][:, 0:NT * E].rearrange("p (n e) -> p n e", e=E)
                for n in range(1, NT):
                    link(nc.vector.tensor_tensor(before[:, n], before[:, n - 1], tiles[:, n - 1], ALU.add))
                link(nc.vector.tensor_tensor(rank[:], before[:], bank[1][:, 0:NT * E].rearrange("p (n e) -> p n e", e=E), ALU.add))
                link(nc.vector.tensor_tensor(rank[:], rank[:], room[:, None, :].to_broadcast(bcast), ALU.is_lt))
                link(nc.vector.tensor_tensor(rank[:], rank[:], equal[:], ALU.mult))
                link(nc.vector.tensor_tensor(hit[:], hit[:], rank[:], ALU.add))
                link(nc.vector.tensor_tensor(gates[:], gates[:], hit[:], ALU.mult))
        clear(nc, sems.all)


def experts(nc, mem, w):
    with ExitStack() as ctx:
        def sb(name, shape, dt=F32):
            return ctx.enter_context(nc.sbuf_tensor("ex_" + name, shape, dt))

        x_all, bank, moe_inT = mem["x_all"], mem["bank"], mem["moe_inT"]
        w1 = sb("w1", [P, 2, DC, FF])
        w2 = sb("w2", [P, 2, FF // P, D])
        gate = sb("gate", [P, 2, NT])
        hT = sb("hT", [P, 2, FF // P, S])
        sems = Semaphores(nc, ctx, "ex", "wload gate_in h_full h_read y_full y_read")
        wload, gate_in, h_full, h_read, y_full, y_read = sems.all
        NF = FF // P
        jobs = [(k, b) for k in range(2) for b in range(B)]

        order = []
        for m in range(len(jobs) + 1):
            if m < len(jobs):
                order += [("relu", NF * m + f) for f in range(1, NF, 2)]
            if m >= 1:
                order += [("add", T * (m - 1) + t) for t in range(T)]
        relu_count = {n: i + 1 for i, (kind, n) in enumerate(order) if kind == "relu"}
        add_count = {n: i + 1 for i, (kind, n) in enumerate(order) if kind == "add"}
        reads_before = {n: (relu_count[n - 4] if n % 2 else (n - 4) // 2 + 1) for n in range(4, NF * len(jobs))}

        with nc.Fori(0, E // 2) as pair:
            with nc.Block() as block:
                @block.sync
                def _(sp):
                    for k in range(2):
                        sp.dma_start(w1[:, k], w["w1"][2 * pair + k].rearrange("(c p) n -> p c n", p=P)).then_inc(wload, 16)
                    sp.wait_ge(wload, 16 * 4)

                @block.scalar
                def _(act):
                    for k in range(2):
                        act.dma_start(w2[:, k], w["w2"][2 * pair + k].rearrange("(c p) n -> p c n", p=P)).then_inc(wload, 16)
                    for m, (k, b) in enumerate(jobs):
                        for f in range(0, NF, 2):
                            n = NF * m + f
                            act.wait_ge(h_full, n + 1)
                            if m >= 2:
                                act.wait_ge(y_full, T * (m - 1))
                            nc.scalar.activation(hT[:, m % 2, f], bank[n % 4][:], ACT.Relu).then_inc(h_read, 1)

                @block.tensor
                def _(pe):
                    def second(m):
                        k, b = jobs[m]
                        pe.wait_ge(h_read, NF // 2 * (m + 1))
                        pe.wait_ge(y_read, relu_count[NF * m + NF - 1])
                        for t in range(T):
                            n = T * m + t
                            if n >= 4:
                                pe.wait_ge(y_read, add_count[n - 4])
                            for f in range(NF):
                                mm = nc.tensor.matmul(bank[4 + n % 4][:, 0:D], hT[:, m % 2, f, t * P:(t + 1) * P], w2[:, k, f, :],
                                                      start=(f == 0), stop=(f == NF - 1))
                            mm.then_inc(y_full, 1)

                    pe.wait_ge(wload, 16 * 4)
                    for m, (k, b) in enumerate(jobs):
                        for f in range(NF):
                            n = NF * m + f
                            if n >= 4:
                                pe.wait_ge(h_read if f % 2 == 0 else y_read, reads_before[n])
                            for d in range(DC):
                                mm = nc.tensor.matmul(bank[n % 4][:], w1[:, k, d, f * P:(f + 1) * P], moe_inT[:, b, d, :],
                                                      start=(d == 0), stop=(d == DC - 1))
                            mm.then_inc(h_full, 1)
                        if m >= 1:
                            second(m - 1)
                    second(len(jobs) - 1)

                @block.vector
                def _(dve):
                    for k in range(2):
                        nc.vector.tensor_copy(gate[:, k, :, None], mem["gates"][:, :, bass.ds(2 * pair + k, 1)]).then_inc(gate_in, 1)
                    dve.wait_ge(gate_in, 2)
                    for kind, n in order:
                        if kind == "relu":
                            m = n // NF
                            dve.wait_ge(h_full, n + 1)
                            if m >= 2:
                                dve.wait_ge(y_full, T * (m - 1))
                            nc.vector.tensor_scalar(hT[:, m % 2, n % NF], bank[n % 4][:], 0.0, None, ALU.max).then_inc(y_read, 1)
                        else:
                            (k, b), t = jobs[n // T], n % T
                            dve.wait_ge(y_full, n + 1)
                            xs = x_all[:, b, t * D:(t + 1) * D]
                            nc.vector.scalar_tensor_tensor(xs, bank[4 + n % 4][:, 0:D], gate[:, k, b * T + t:b * T + t + 1], xs,
                                                           ALU.mult, ALU.add).then_inc(y_read, 1)
                    dve.wait_ge(y_read, len(order))
            clear(nc, sems.all)



MH = 8
MD = D // MH


def memory_attention(nc, mem, w):
    with ExitStack() as ctx:
        def sb(name, shape, dt=F32):
            return ctx.enter_context(nc.sbuf_tensor("ma_" + name, shape, dt))

        x_all, ident, psum, bank = mem["x_all"], mem["ident"], mem["psum"], mem["bank"]
        x = sb("x", [P, T, D])
        xn = sb("xn", [P, T, D])
        qT = sb("qT", [P, DC, S])
        context = sb("context", [P, CTX])
        kT = sb("kT", [P, DC, M])
        bias = sb("bias", [P, 1])
        mask_i = sb("mask_i", [P, M], I32)
        mask = sb("mask", [P, M])
        smax = sb("smax", [P, MH])
        rsum = sb("rsum", [P, MH])
        prob = sb("prob", [P, 2, MH * M])
        probT = sb("probT", [P, 2, MH * M])
        sems = Semaphores(nc, ctx, "ma", "loaded xin xt_full xt_read s_full s_read exp_in exp_done normed tr_full tr_read o_full o_read "
                          "dve_chain masked")
        (loaded, xin, xt_full, xt_read, s_full, s_read, exp_in, exp_done, normed, tr_full, tr_read, o_full, o_read,
         dve_chain, masked) = sems.all
        R = P // MD

        with nc.Fori(0, B) as b:
            with nc.Block() as block:
                @block.sync
                def _(sp):
                    for half in range(2):
                        sp.dma_start(context[half * M:(half + 1) * M, :], w["ctx"][b]).then_inc(loaded, 16)
                    sp.dma_start(mask_i[:], w["mask"][b, None, :].to_broadcast([P, M])).then_inc(loaded, 16)
                    sp.dma_start(bias[:], w["b"][None, :].to_broadcast([P, 1])).then_inc(loaded, 16)
                    sp.wait_ge(loaded, 64)

                @block.vector
                def _(dve):
                    nc.vector.tensor_copy(x[:].rearrange("p t d -> p (t d)"), x_all[:, b]).then_inc(xin, 1)
                    dve.wait_ge(loaded, 64)
                    nc.vector.tensor_copy(mask[:], mask_i[:]).then_inc(masked, 1)
                    dve.wait_ge(masked, 1)
                    nc.vector.tensor_scalar(mask[:], mask[:], -1.0, 1.0, ALU.mult, ALU.add).then_inc(masked, 1)
                    dve.wait_ge(masked, 2)
                    nc.vector.tensor_scalar(mask[:], mask[:], NEG, None, ALU.mult).then_inc(masked, 1)
                    dve.wait_ge(masked, 3)
                    dve.wait_ge(xin, 1)
            clear(nc, sems.all)
            normalise(nc, mem, lambda t: x[:, t], lambda t: xn[:, t], 1e-5, True)
            with nc.Block() as block:
                @block.tensor
                def _(pe):
                    for d in range(DC):
                        for t in range(T):
                            mm = nc.tensor.transpose(bank[d][:, t * P:(t + 1) * P], xn[:, t, d * P:(d + 1) * P], ident[:])
                        mm.then_inc(xt_full, 1)
                    for d in range(DC):
                        mm = nc.tensor.transpose(bank[2][:, d * M:(d + 1) * M], context[0:M, d * P:(d + 1) * P], ident[0:M, 0:M])
                    mm.then_inc(xt_full, 1)
                    pe.wait_ge(xt_read, DC + 1)
                    for t in range(T + 1):
                        if t < T:
                            if t >= 1:
                                pe.wait_ge(s_read, t)
                            for r in range(R):
                                for c in range(DC):
                                    mm = nc.tensor.matmul(bank[r][:, c * M:(c + 1) * M], qT[r * MD:(r + 1) * MD, c, t * P:(t + 1) * P],
                                                          kT[r * MD:(r + 1) * MD, c, :], start=True, stop=True, skip_group_check=True)
                            mm.then_inc(s_full, 1)
                        if t >= 1:
                            u = t - 1
                            pe.wait_ge(normed, u + 1)
                            if u >= 1:
                                pe.wait_ge(tr_read, u)
                            for r in range(R):
                                mm = nc.tensor.transpose(bank[4][:, r * P:(r + 1) * P], prob[:, u % 2, r * P:(r + 1) * P], ident[:])
                            mm.then_inc(tr_full, 1)
                            pe.wait_ge(tr_read, u + 1)
                            if u >= 1:
                                pe.wait_ge(o_read, u)
                            for c in range(DC):
                                for r in range(R):
                                    at = D + (R * c + r) * MD
                                    mm = nc.tensor.matmul(bank[5 + c][:, r * MD:(r + 1) * MD], probT[c * M:(c + 1) * M, u % 2, r * P:(r + 1) * P],
                                                          context[c * M:(c + 1) * M, at:at + MD], start=True, stop=True, skip_group_check=True)
                            mm.then_inc(o_full, 1)

                @block.scalar
                def _(act):
                    for d in range(DC):
                        act.wait_ge(xt_full, d + 1)
                        nc.scalar.mul(qT[:, d, :], bank[d][:], MD ** -0.5).then_inc(xt_read, 1)
                    act.wait_ge(xt_full, DC + 1)
                    nc.scalar.copy(kT[:].rearrange("p c m -> p (c m)"), bank[2][:, 0:DC * M]).then_inc(xt_read, 1)
                    for t in range(T):
                        act.wait_ge(exp_in, t + 1)
                        nc.scalar.activation(prob[:, t % 2], prob[:, t % 2], ACT.Exp).then_inc(exp_done, 1)
                        act.wait_ge(tr_full, t + 1)
                        if t >= 2:
                            act.wait_ge(o_full, t - 1)
                        nc.scalar.copy(probT[:, t % 2], bank[4][:]).then_inc(tr_read, 1)

                @block.vector
                def _(dve):
                    links = [0]

                    def link(ins):
                        links[0] += 1
                        ins.then_inc(dve_chain, 1)
                        dve.wait_ge(dve_chain, links[0])

                    for t in range(T):
                        dve.wait_ge(s_full, t + 1)
                        if t >= 2:
                            dve.wait_ge(tr_full, t - 1)
                        for r in range(R):
                            s3 = bank[r][:, 0:DC * M].rearrange("p (c m) -> p c m", m=M)
                            p3 = prob[:, t % 2, r * P:(r + 1) * P].rearrange("p (c m) -> p c m", m=M)
                            op = nc.vector.scalar_tensor_tensor(p3, s3, bias[:, 0:1], mask[:, None, :].to_broadcast([P, DC, M]), ALU.add, ALU.add)
                        op.then_inc(s_read, 1)
                        dve.wait_ge(s_read, t + 1)
                        p8 = prob[:, t % 2].rearrange("p (h m) -> p h m", m=M)
                        link(nc.vector.tensor_reduce(smax[:], p8, AX, ALU.max))
                        nc.vector.tensor_tensor(p8, p8, smax[:, :, None].to_broadcast([P, MH, M]), ALU.subtract).then_inc(exp_in, 1)
                        dve.wait_ge(exp_done, t + 1)
                        link(nc.vector.tensor_reduce(rsum[:], p8, AX, ALU.add))
                        link(nc.vector.reciprocal(rsum[:], rsum[:]))
                        nc.vector.tensor_tensor(p8, p8, rsum[:, :, None].to_broadcast([P, MH, M]), ALU.mult).then_inc(normed, 1)
                        dve.wait_ge(o_full, t + 1)
                        for c in range(DC):
                            xs = x[:, t, c * P:(c + 1) * P]
                            op = nc.vector.tensor_tensor(xs, xs, bank[5 + c][:, 0:P], ALU.add)
                        op.then_inc(o_read, 1)
                    dve.wait_ge(o_read, T)
                    link(nc.vector.tensor_copy(x_all[:, b], x[:].rearrange("p t d -> p (t d)")))
            clear(nc, sems.all)




NB = 2
NTL = NB * T
PAIR = 2 * P


STEPS = {"X": "xT", "c": "chunk", "n": "norm", "t": "turn", "q": "qk", "s": "scores", "p": "probT", "v": "values", "o": "oT",
         "P": "project", "S": "shift", "N": "xn", "T": "xnT", "g": "ga", "f": "ffn"}
ORDER = """
    XcnctcncntccncqtnqctqtcnncqcqtnsqscttccpnqcpqtvnpnsvqpstvcccvtnqctpnocpcqnovqpvttpcqnnvcsqscXvPtctqpntcoqconqcctpvnncS
    pvNtpcvnqvsPotoScpcTqtnNPqTncgqtnspcvgvtpspqsvcpvSNgogcpovvtpqncnqtggsctvnpqcpvnTtcpqPfosSNtcocvqcnnqPvpstfvptTccvpgnn
    qogovstpcqtSgNcqqggsvppPgTvSvNspfTfpgoovvpgvpgvPogoggPSSNNfTTfggggggff
"""


def layer_order():
    seen, order = dict.fromkeys(STEPS, 0), []
    for letter in "".join(ORDER.split()):
        order.append((STEPS[letter], seen[letter]))
        seen[letter] += 1
    per_tile = {"c": 6, "n": 4, "t": 4, "q": 4, "s": GROUP // 2, "p": GROUP, "v": GROUP, "o": 2, "P": 1, "S": 1, "N": 1, "T": 1, "f": 1}
    assert all(seen[k] == n * NTL for k, n in per_tile.items()) and seen["X"] == NB and seen["g"] == FC * NTL // 2
    return order


def local_layers(nc, mem, w):
    with ExitStack() as ctx:
        def sb(name, shape, dt=F32):
            return ctx.enter_context(nc.sbuf_tensor("l1_" + name, shape, dt))

        x_all, ident, ident_bf, bank = mem["x_all"], mem["ident"], mem["ident_bf"], mem["bank"]
        wqkv = sb("wqkv", [P, DC, 3 * INNER])
        wo = sb("wo", [P, INNER // P, D])
        w1 = sb("w1", [P, DC, 2 * FI])
        w2 = sb("w2", [P, FC, D])
        cols = sb("cols", [P, 2 * FC + 2 * DC])
        b1 = cols[:, 0:2 * FC].rearrange("p (k c) -> p k c", k=2)
        ln_g = cols[:, 2 * FC:2 * FC + DC]
        ln_b = cols[:, 2 * FC + DC:2 * FC + 2 * DC]
        scale_qk = sb("scale_qk", [P, 2, DH])
        rope = sb("rope", [P, 4, T, DH])
        turn = sb("turn", [P, 4, T, DH])
        shift = sb("shift", [P, 2, P])
        mask = sb("mask", [P, 2, P])
        mask_bf = sb("mask_bf", [P, 2, P], BF16)
        x = sb("x", [P, NB * T, D])
        xT = sb("xT", [P, DC, S + 1])
        sq = sb("sq", [P, S])
        norm = sb("norm", [P, 2, 8])
        minus_half = sb("minus_half", [P, 8])
        qn = sb("qn", [P, 2, S])
        rot = sb("rot", [P, 2, S])
        cosd = sb("cosd", [P, 2, S])
        qr = sb("qr", [P, 2, S])
        qT = sb("qT", [P, INNER // P, S])
        kT = sb("kT", [P, INNER // P, S])
        v_odd = sb("v_odd", [P, T, HEADS, DH + 1])
        v_even = sb("v_even", [P, T, HEADS, DH + 1])
        smax = sb("smax", [P, 2, GROUP])
        prob = sb("prob", [P, 4, GROUP * P])
        probT = sb("probT", [P, 2, GROUP * P])
        rsum = sb("rsum", [P, 2, GROUP])
        o = sb("o", [P, INNER])
        oT = sb("oT", [P, INNER])
        stats = sb("stats", [P, 2, 2, 6])
        mv = sb("mv", [P, 2, 2])
        rstd = sb("rstd", [P, 2])
        xn = sb("xn", [P, 2, D])
        xnT = sb("xnT", [P, DC, PAIR])
        gate = sb("gate", [P, 2, PAIR])
        x_kept = sb("x_kept", [P, P])
        h = sb("h", [P, FC, PAIR])

        names = ("table setup back xin xt_full xt_read chunk_full sq_done ss_done norm_done qn_done rot_done qr_done v_read "
                 "tr_full tr_read s_full s_read exp_done o_full o_read sh_full mv_done rstd_done xn_done ga_full gelu_done h_done "
                 "kept dve_chain pow_chain")
        sems = Semaphores(nc, ctx, "l1", names)
        (table, setup, back, xin, xt_full, xt_read, chunk_full, sq_done, ss_done, norm_done, qn_done, rot_done, qr_done,
         v_read, tr_full, tr_read, s_full, s_read, exp_done, o_full, o_read, sh_full, mv_done, rstd_done, xn_done, ga_full,
         gelu_done, h_done, kept, dve_chain, pow_chain) = sems.all

        weight_sems = Semaphores(nc, ctx, "l1w", "q_in k_in v_in rest_in")
        qkv_in, rest_in = weight_sems.all[0:3], weight_sems.all[3]

        with nc.Block() as block:
            @block.sync
            def _(sp):
                sp.dma_start(rope[:], w["rope1"].rearrange("k (t p) d -> p k t d", p=P)).then_inc(table, 16)
                sp.dma_start(shift[:], w["shift"].rearrange("k p q -> p k q")).then_inc(table, 16)
                sp.dma_start(mask[:], w["win_mask"].rearrange("k p q -> p k q")).then_inc(table, 16)

            @block.gpsimd
            def _(pool):
                nc.gpsimd.memset(v_odd[:], 1.0).then_inc(setup, 1)
                nc.gpsimd.memset(v_even[:], 1.0).then_inc(setup, 1)
                nc.gpsimd.memset(xT[:, 1, 0:1], 0.0).then_inc(setup, 1)
                nc.gpsimd.memset(minus_half[:], -0.5).then_inc(setup, 1)

            @block.vector
            def _(dve):
                nc.vector.memset(h[32:64, FC - 1, :], 1.0).then_inc(setup, 1)
                dve.wait_ge(table, 48)
                for k in range(2):
                    nc.vector.tensor_copy(mask_bf[:, k], mask[:, k]).then_inc(setup, 1)
                dve.wait_ge(setup, 7)
        clear(nc, sems.all)

        order = layer_order()
        keeps = [t for t in range(1, NTL, 2) if t % T < T - 1]
        big_turn, released, tr_turn, out_turn = {}, [], {}, {}
        for kind, n in order:
            if kind == "xT":
                for d in range(DC):
                    big_turn["xT", DC * n + d] = len(released)
                    released.append((xt_read, DC * n + d + 1))
            elif kind == "chunk":
                t, c = n // 6, n % 6
                big_turn[kind, n] = len(released)
                released.append((qn_done, 4 * t + c + 1) if c < 4 else (v_read, 2 * t + c - 3))
            elif kind == "scores":
                for g in (2 * n, 2 * n + 1):
                    big_turn[kind, g] = len(released)
                    released.append((s_read, g + 1))
            elif kind in ("shift", "ga"):
                big_turn[kind, n] = len(released)
                released.append((xn_done if kind == "shift" else h_done, n + 1))
            elif kind in ("qk", "probT", "oT", "xnT"):
                tr_turn[kind, n] = len(tr_turn)
            if kind in ("values", "project", "ffn"):
                out_turn[kind, n] = len(out_turn)

        def chunk_at(m):
            return big_turn["chunk", 6 * (m // 4) + m % 4]

        with nc.Fori(0, DEPTH) as layer:
            clear(nc, weight_sems.all)
            with nc.Block() as block:
                @block.sync
                def _(sp):
                    for s in range(2):
                        sp.dma_start(scale_qk[:, s], w["qk_scale"][s][layer, None, :].to_broadcast([P, DH])).then_inc(table, 16)
                    for part, arrived in enumerate(qkv_in):
                        cut = slice(part * INNER, (part + 1) * INNER)
                        sp.dma_start(wqkv[:, :, cut], w["Wqkv"][layer].rearrange("(c p) n -> p c n", p=P)[:, :, cut]).then_inc(arrived, 16)
                    sp.dma_start(wo[:], w["Wo"][layer].rearrange("(c p) n -> p c n", p=P)).then_inc(rest_in, 16)
                    sp.dma_start(cols[:], w["cols"][layer]).then_inc(rest_in, 16)
                    sp.dma_start(w1[:], w["W1"][layer].rearrange("(c p) n -> p c n", p=P)).then_inc(rest_in, 16)
                    sp.dma_start(w2[:, 0:FC - 1], w["W2"][layer][0:(FC - 1) * P].rearrange("(c p) n -> p c n", p=P)).then_inc(rest_in, 16)
                    sp.dma_start(w2[0:FR, FC - 1], w["W2"][layer][(FC - 1) * P:FI]).then_inc(rest_in, 16)
                    sp.dma_start(w2[FR:FR + 1, FC - 1], w["b2"][layer, None, :]).then_inc(rest_in, 16)

                @block.vector
                def _(dve):
                    dve.wait_ge(table, 32)
                    for s in range(2):
                        sc = scale_qk[:, s]
                        nc.vector.tensor_tensor(turn[:, 2 * s], rope[:, 2 * s], sc[:, None, :].to_broadcast([P, T, DH]), ALU.mult).then_inc(back, 1)
                        nc.vector.tensor_tensor(turn[:, 2 * s + 1, :, 0:HALF], rope[:, 2 * s + 1, :, 0:HALF],
                                                sc[:, None, HALF:DH].to_broadcast([P, T, HALF]), ALU.mult).then_inc(back, 1)
                        nc.vector.tensor_tensor(turn[:, 2 * s + 1, :, HALF:DH], rope[:, 2 * s + 1, :, HALF:DH],
                                                sc[:, None, 0:HALF].to_broadcast([P, T, HALF]), ALU.mult).then_inc(back, 1)
                    dve.wait_ge(back, 6)
            clear(nc, sems.all)

            with nc.Fori(0, B // NB) as part:
                with nc.Block() as block:
                    @block.tensor
                    def _(pe):
                        def shared_bank(turn):
                            if turn >= 4:
                                pe.wait_ge(*released[turn - 4])
                            return bank[turn % 4]

                        def transposed_bank(turn):
                            if turn >= 2:
                                pe.wait_ge(tr_read, turn - 1)
                            return bank[4 + turn % 2]

                        def output_bank(turn):
                            if turn >= 2:
                                pe.wait_ge(o_read, turn - 1)
                            return bank[6 + turn % 2]

                        pe.wait_ge(xin, 1)
                        for kind, n in order:
                            if kind == "xT":
                                for d in range(DC):
                                    dst = shared_bank(big_turn[kind, DC * n + d])
                                    for t in range(T):
                                        mm = nc.tensor.transpose(dst[:, t * P:(t + 1) * P], x[:, T * n + t, d * P:(d + 1) * P], ident[:])
                                    mm.then_inc(xt_full, 1)
                            elif kind == "chunk":
                                t, c = n // 6, n % 6
                                if n % (6 * T) == 0:
                                    pe.wait_ge(xt_read, DC * (t // T + 1))
                                if t == 0 and c % 2 == 0:
                                    pe.wait_ge(qkv_in[c // 2], 16)
                                dst = shared_bank(big_turn[kind, n])
                                for d in range(DC):
                                    mm = nc.tensor.matmul(dst, xT[:, d, (t % T) * P:(t % T + 1) * P], wqkv[:, d, c * S:(c + 1) * S],
                                                          start=(d == 0), stop=(d == DC - 1))
                                mm.then_inc(chunk_full, 1)
                            elif kind == "qk":
                                pe.wait_ge(qr_done, n + 1)
                                dst = transposed_bank(tr_turn[kind, n])
                                for j in range(4):
                                    mm = nc.tensor.transpose(dst[:, j * P:(j + 1) * P], qr[:, n % 2, j * P:(j + 1) * P], ident[:])
                                mm.then_inc(tr_full, 1)
                            elif kind == "scores":
                                t, hg = 2 * n // GROUP, 2 * n % GROUP
                                pe.wait_ge(tr_read, tr_turn["qk", 4 * t + 3] + 1)
                                both = [shared_bank(big_turn[kind, 2 * n + k]) for k in range(2)]
                                for s in both:
                                    nc.tensor.matmul(s.rearrange("p (g q) -> p g q", g=GROUP), ident_bf[:],
                                                     mask_bf[:, 0 if t % T == 0 else 1, None, :].to_broadcast([P, GROUP, P]),
                                                     start=True, stop=False, skip_group_check=True)
                                for j in range(GROUP):
                                    c = GROUP * (hg // 2) + j
                                    for odd in range(2):
                                        for k in range(2):
                                            half = odd ^ k
                                            r, q0 = DH * k, (t % T) * P + half * WIN
                                            before = WIN if q0 > 0 else 0
                                            mm = nc.tensor.matmul(both[k][half * WIN:(half + 1) * WIN, j * P + WIN - before:(j + 1) * P],
                                                                  qT[r:r + DH, c, q0:q0 + WIN], kT[r:r + DH, c, q0 - before:q0 + WIN],
                                                                  start=False, stop=(j == GROUP - 1 and odd == 1), skip_group_check=True)
                                            if j == GROUP - 1 and odd == 1:
                                                mm.then_inc(s_full, 1)
                            elif kind in ("probT", "oT"):
                                if kind == "probT":
                                    pe.wait_ge(exp_done, n + 1)
                                    src = prob[:, n % 4]
                                else:
                                    pe.wait_ge(o_read, out_turn["values", GROUP * (n // 2) + GROUP - 1] + 1)
                                    src = o[:, (n % 2) * S:(n % 2 + 1) * S]
                                dst = transposed_bank(tr_turn[kind, n])
                                for j in range(4):
                                    mm = nc.tensor.transpose(dst[:, j * P:(j + 1) * P], src[:, j * P:(j + 1) * P], ident[:])
                                mm.then_inc(tr_full, 1)
                            elif kind == "values":
                                t, hg = n // GROUP, n % GROUP
                                pe.wait_ge(tr_read, tr_turn["probT", n] + 1)
                                pe.wait_ge(v_read, 2 * t + 2)
                                dst = output_bank(out_turn[kind, n])
                                for j in range(GROUP):
                                    for half, v in ((0, v_even), (1, v_odd)):
                                        mm = nc.tensor.matmul(dst[half * WIN:(half + 1) * WIN, j * (DH + 1):(j + 1) * (DH + 1)],
                                                              probT[:, n % 2, j * P + half * WIN:j * P + (half + 1) * WIN],
                                                              v[:, t % T, 2 * (GROUP * (hg // 2) + j) + hg % 2, :], start=True, stop=True, skip_group_check=True)
                                mm.then_inc(o_full, 1)
                            elif kind == "project":
                                if n == 0:
                                    pe.wait_ge(rest_in, 16 * 6)
                                pe.wait_ge(tr_read, tr_turn["oT", 2 * n + 1] + 1)
                                dst = output_bank(out_turn[kind, n])
                                for c in range(INNER // P):
                                    mm = nc.tensor.matmul(dst[:, 0:D], oT[:, c * P:(c + 1) * P], wo[:, c, :], start=(c == 0), stop=(c == INNER // P - 1))
                                mm.then_inc(o_full, 1)
                            elif kind == "shift":
                                pe.wait_ge(o_read, out_turn["project", n] + 1)
                                dst = shared_bank(big_turn[kind, n])
                                mm = nc.tensor.matmul(dst[:, 0:P], shift[:, 0], x[:, n, P:D], start=True, stop=(n % T == 0))
                                if n % T > 0:
                                    before = x[:, n - 1, P:D] if n % 2 else x_kept[:]
                                    if n % 2 == 0:
                                        pe.wait_ge(kept, keeps.index(n - 1) + 1)
                                    mm = nc.tensor.matmul(dst[:, 0:P], shift[:, 1], before, start=False, stop=True)
                                mm.then_inc(sh_full, 1)
                            elif kind == "xnT":
                                pe.wait_ge(xn_done, n + 1)
                                dst = transposed_bank(tr_turn[kind, n])
                                for d in range(DC):
                                    mm = nc.tensor.transpose(dst[:, d * P:(d + 1) * P], xn[:, n % 2, d * P:(d + 1) * P], ident[:])
                                mm.then_inc(tr_full, 1)
                            elif kind == "ga":
                                p, i = n // FC, n % FC
                                rows_out = P if i < FC - 1 else FR
                                if i == 0:
                                    pe.wait_ge(tr_read, tr_turn["xnT", 2 * p + 1] + 1)
                                dst = shared_bank(big_turn[kind, n])
                                for k, at in ((1, FI), (0, 0)):
                                    for d in range(DC):
                                        mm = nc.tensor.matmul(dst[0:rows_out, k * PAIR:(k + 1) * PAIR], w1[:, d, at + i * P:at + i * P + rows_out],
                                                              xnT[:, d, :], start=(d == 0), stop=(d == DC - 1), skip_group_check=True)
                                mm.then_inc(ga_full, 1)
                            elif kind == "ffn":
                                pe.wait_ge(h_done, FC * (n // 2 + 1))
                                dst = output_bank(out_turn[kind, n])
                                for i in range(FC):
                                    rows_in = P if i < FC - 1 else FR + 1
                                    mm = nc.tensor.matmul(dst[:, 0:D], h[0:rows_in, i, (n % 2) * P:(n % 2 + 1) * P], w2[0:rows_in, i, :],
                                                          start=(i == 0), stop=(i == FC - 1))
                                mm.then_inc(o_full, 1)

                    @block.scalar
                    def _(act):
                        for kind, n in order:
                            if kind == "xT":
                                if n > 0:
                                    act.wait_ge(chunk_full, 6 * T * n)
                                for d in range(DC):
                                    act.wait_ge(xt_full, DC * n + d + 1)
                                    nc.scalar.copy(xT[:, d, d:d + S], bank[big_turn[kind, DC * n + d] % 4]).then_inc(xt_read, 1)
                            elif kind == "chunk":
                                t, c = n // 6, n % 6
                                act.wait_ge(chunk_full, n + 1)
                                src = bank[big_turn[kind, n] % 4]
                                if c < 4:
                                    m = 4 * t + c
                                    if m >= 1:
                                        act.wait_ge(ss_done, m)
                                    nc.scalar.activation(sq[:], src, ACT.Square).then_inc(sq_done, 1)
                                else:
                                    s3 = src.rearrange("p (h d) -> p h d", h=8)
                                    hs = slice(8 * (c - 4), 8 * (c - 3))
                                    if t >= T:
                                        act.wait_ge(o_full, out_turn["values", GROUP * (t - T) + GROUP - 1] + 1)
                                        if t % T < T - 1:
                                            act.wait_ge(o_full, out_turn["values", GROUP * (t - T + 1) + GROUP - 1] + 1)
                                    nc.scalar.copy(v_even[WIN:P, t % T, hs, 0:DH], s3[0:WIN])
                                    if t % T < T - 1:
                                        nc.scalar.copy(v_even[0:WIN, t % T + 1, hs, 0:DH], s3[WIN:P])
                                    nc.scalar.copy(v_odd[:, t % T, hs, 0:DH], s3).then_inc(v_read, 1)
                            elif kind == "qk":
                                t, c = n // 4, n % 4
                                u = tr_turn[kind, n]
                                act.wait_ge(tr_full, u + 1)
                                if t >= T:
                                    last = GROUP * (t - T + (2 if t % T < T - 1 else 1))
                                    act.wait_ge(s_full, last)
                                dst = qT if c < 2 else kT
                                nc.scalar.copy(dst[:, 4 * (c % 2):4 * (c % 2) + 4, (t % T) * P:(t % T + 1) * P],
                                               bank[4 + u % 2].rearrange("p (c q) -> p c q", c=4)).then_inc(tr_read, 1)
                            elif kind == "scores":
                                for g in (2 * n, 2 * n + 1):
                                    act.wait_ge(s_read, g + 1)
                                    nc.scalar.activation(prob[:, g % 4], prob[:, g % 4], ACT.Exp, scale=QK_SCALE).then_inc(exp_done, 1)
                            elif kind == "probT":
                                u = tr_turn[kind, n]
                                act.wait_ge(tr_full, u + 1)
                                if n >= 2:
                                    act.wait_ge(o_full, out_turn["values", n - 2] + 1)
                                nc.scalar.copy(probT[:, n % 2], bank[4 + u % 2]).then_inc(tr_read, 1)
                            elif kind == "oT":
                                u = tr_turn[kind, n]
                                act.wait_ge(tr_full, u + 1)
                                if n >= 2:
                                    act.wait_ge(o_full, out_turn["project", n // 2 - 1] + 1)
                                nc.scalar.copy(oT[:, (n % 2) * S:(n % 2 + 1) * S], bank[4 + u % 2]).then_inc(tr_read, 1)
                            elif kind == "shift" and n in keeps:
                                act.wait_ge(o_read, out_turn["project", n] + 1)
                                if n > keeps[0]:
                                    act.wait_ge(sh_full, keeps[keeps.index(n) - 1] + 2)
                                nc.scalar.copy(x_kept[:], x[:, n, P:D]).then_inc(kept, 1)
                            elif kind == "xnT":
                                u = tr_turn[kind, n]
                                act.wait_ge(tr_full, u + 1)
                                if n == 0:
                                    act.wait_ge(rest_in, 16 * 6)
                                if n >= 2:
                                    act.wait_ge(ga_full, FC * (n // 2))
                                for d in range(DC):
                                    cp = nc.scalar.activation(xnT[:, d, (n % 2) * P:(n % 2 + 1) * P], bank[4 + u % 2][:, d * P:(d + 1) * P],
                                                              ACT.Identity, bias=ln_b[:, d:d + 1], scale=ln_g[:, d:d + 1])
                                cp.then_inc(tr_read, 1)
                            elif kind == "ga":
                                i = n % FC
                                rows_out = P if i < FC - 1 else FR
                                act.wait_ge(ga_full, n + 1)
                                if n >= 2:
                                    act.wait_ge(h_done, n - 1)
                                nc.scalar.activation(gate[0:rows_out, n % 2], bank[big_turn[kind, n] % 4][0:rows_out, PAIR:2 * PAIR], ACT.Gelu,
                                                     bias=b1[0:rows_out, 1, i:i + 1]).then_inc(gelu_done, 1)

                    @block.gpsimd
                    def _(pool):
                        powers = 0
                        for kind, n in order:
                            if kind == "chunk" and n % 6 < 4:
                                m = 4 * (n // 6) + n % 6
                                pool.wait_ge(ss_done, m + 1)
                                nc.gpsimd.tensor_scalar(norm[:, m % 2], norm[:, m % 2], 1e-24, None, ALU.max).then_inc(pow_chain, 1)
                                powers += 1
                                pool.wait_ge(pow_chain, powers)
                                nc.gpsimd.tensor_tensor(norm[:, m % 2], norm[:, m % 2], minus_half[:], ALU.pow).then_inc(norm_done, 1)
                            elif kind == "norm":
                                t, c = (n // 4) % T, n % 4
                                pool.wait_ge(qn_done, n + 1)
                                if n >= 2:
                                    pool.wait_ge(qr_done, n - 1)
                                q3 = qn[:, n % 2].rearrange("p (h d) -> p h d", h=8)
                                r3 = rot[:, n % 2].rearrange("p (h d) -> p h d", h=8)
                                sn = turn[:, 2 * (c // 2) + 1, t, None, :]
                                nc.gpsimd.tensor_tensor(r3[:, :, 0:HALF], q3[:, :, HALF:DH],
                                                        sn[:, :, 0:HALF].to_broadcast([P, 8, HALF]), ALU.mult)
                                nc.gpsimd.tensor_tensor(r3[:, :, HALF:DH], q3[:, :, 0:HALF],
                                                        sn[:, :, HALF:DH].to_broadcast([P, 8, HALF]), ALU.mult).then_inc(rot_done, 1)
                            elif kind == "shift":
                                col = rstd[:, n % 2:n % 2 + 1]
                                pool.wait_ge(mv_done, n + 1)
                                if n >= 2:
                                    pool.wait_ge(xn_done, n - 1)
                                nc.gpsimd.tensor_scalar(col, mv[:, n % 2, 1:2], 1e-5, None, ALU.add).then_inc(pow_chain, 1)
                                powers += 1
                                pool.wait_ge(pow_chain, powers)
                                nc.gpsimd.tensor_tensor(col, col, minus_half[:, 0:1], ALU.pow).then_inc(rstd_done, 1)

                    @block.vector
                    def _(dve):
                        links = [0]

                        def link(ins):
                            links[0] += 1
                            ins.then_inc(dve_chain, 1)
                            dve.wait_ge(dve_chain, links[0])

                        nc.vector.tensor_copy(x[:].rearrange("p (b t) d -> p b (t d)", b=NB), x_all[:, bass.ds(part * NB, NB)]).then_inc(xin, 1)
                        for kind, n in order:
                            if kind == "chunk" and n % 6 < 4:
                                m = 4 * (n // 6) + n % 6
                                dve.wait_ge(sq_done, m + 1)
                                if m >= 2:
                                    dve.wait_ge(qn_done, m - 1)
                                nc.vector.tensor_reduce(norm[:, m % 2], sq[:].rearrange("p (h d) -> p h d", h=8), AX, ALU.add).then_inc(ss_done, 1)
                            elif kind == "norm":
                                t, c = (n // 4) % T, n % 4
                                src = bank[chunk_at(n) % 4].rearrange("p (h d) -> p h d", h=8)
                                q3 = qn[:, n % 2].rearrange("p (h d) -> p h d", h=8)
                                dve.wait_ge(norm_done, n + 1)
                                if n >= 2:
                                    dve.wait_ge(rot_done, n - 1)
                                nc.vector.tensor_tensor(q3, src, norm[:, n % 2, :, None].to_broadcast([P, 8, DH]), ALU.mult).then_inc(qn_done, 1)
                                dve.wait_ge(qn_done, n + 1)
                                link(nc.vector.tensor_tensor(cosd[:, n % 2].rearrange("p (h d) -> p h d", h=8), q3,
                                                             turn[:, 2 * (c // 2), t, None, :].to_broadcast([P, 8, DH]), ALU.mult))
                            elif kind == "turn":
                                dve.wait_ge(rot_done, n + 1)
                                if n >= 2:
                                    dve.wait_ge(tr_full, tr_turn["qk", n - 2] + 1)
                                nc.vector.tensor_tensor(qr[:, n % 2], cosd[:, n % 2], rot[:, n % 2], ALU.add).then_inc(qr_done, 1)
                            elif kind == "scores":
                                for g in (2 * n, 2 * n + 1):
                                    dve.wait_ge(s_full, g + 1)
                                    s3 = bank[big_turn[kind, g] % 4].rearrange("p (g q) -> p g q", g=GROUP)
                                    link(nc.vector.tensor_reduce(smax[:, g % 2], s3, AX, ALU.max))
                                    if g >= 4:
                                        dve.wait_ge(tr_full, tr_turn["probT", g - 4] + 1)
                                    nc.vector.tensor_tensor(prob[:, g % 4].rearrange("p (g q) -> p g q", g=GROUP), s3,
                                                            smax[:, g % 2, :, None].to_broadcast([P, GROUP, P]), ALU.subtract).then_inc(s_read, 1)
                            elif kind == "values":
                                t, hg = n // GROUP, n % GROUP
                                u = out_turn[kind, n]
                                dve.wait_ge(o_full, u + 1)
                                if hg == 0 and t >= 1:
                                    dve.wait_ge(tr_full, tr_turn["oT", 2 * t - 1] + 1)
                                ob = bank[6 + u % 2][:, 0:GROUP * (DH + 1)].rearrange("p (g d) -> p g d", g=GROUP)
                                link(nc.vector.reciprocal(rsum[:, n % 2, :, None], ob[:, :, DH:DH + 1]))
                                nc.vector.tensor_tensor(o[:].rearrange("p (a g b d) -> p a g b d", a=2, g=GROUP, b=2)[:, hg // 2, :, hg % 2],
                                                        ob[:, :, 0:DH], rsum[:, n % 2, :, None].to_broadcast([P, GROUP, DH]),
                                                        ALU.mult).then_inc(o_read, 1)
                            elif kind in ("project", "ffn"):
                                u = out_turn[kind, n]
                                dve.wait_ge(o_full, u + 1)
                                if kind == "ffn" and n in keeps:
                                    dve.wait_ge(kept, keeps.index(n) + 1)
                                nc.vector.tensor_tensor(x[:, n, :], x[:, n, :], bank[6 + u % 2][:, 0:D], ALU.add).then_inc(o_read, 1)
                            elif kind == "shift":
                                dve.wait_ge(o_read, out_turn["project", n] + 1)
                                nc.vector.bn_stats(stats[:, n % 2, 0, :], x[:, n, 0:P])
                                dve.wait_ge(sh_full, n + 1)
                                link(nc.vector.bn_stats(stats[:, n % 2, 1, :], bank[big_turn[kind, n] % 4][:, 0:P]))
                                if n >= 2:
                                    dve.wait_ge(rstd_done, n - 1)
                                nc.vector.bn_aggr(mv[:, n % 2], stats[:, n % 2].rearrange("p a b -> p (a b)")).then_inc(mv_done, 1)
                            elif kind == "xn":
                                dve.wait_ge(rstd_done, n + 1)
                                if n >= 2:
                                    dve.wait_ge(tr_full, tr_turn["xnT", n - 2] + 1)
                                mean, scale = mv[:, n % 2, 0:1], rstd[:, n % 2:n % 2 + 1]
                                dve.wait_ge(mv_done, n + 1)
                                nc.vector.tensor_scalar(xn[:, n % 2, 0:P], x[:, n, 0:P], mean, scale, ALU.subtract, ALU.mult)
                                nc.vector.tensor_scalar(xn[:, n % 2, P:D], bank[big_turn["shift", n] % 4][:, 0:P], mean, scale,
                                                        ALU.subtract, ALU.mult).then_inc(xn_done, 1)
                            elif kind == "ga":
                                i = n % FC
                                rows_out = P if i < FC - 1 else FR
                                dve.wait_ge(gelu_done, n + 1)
                                if n == 0:
                                    dve.wait_ge(rest_in, 16 * 6)
                                if i == 0 and n > 0:
                                    dve.wait_ge(o_full, out_turn["ffn", 2 * (n // FC) - 1] + 1)
                                nc.vector.scalar_tensor_tensor(h[0:rows_out, i, :], bank[big_turn[kind, n] % 4][0:rows_out, 0:PAIR], b1[0:rows_out, 0, i:i + 1],
                                                               gate[0:rows_out, n % 2], ALU.add, ALU.mult).then_inc(h_done, 1)
                        dve.wait_ge(o_read, len(out_turn))
                        nc.vector.tensor_copy(x_all[:, bass.ds(part * NB, NB)], x[:].rearrange("p (b t) d -> p b (t d)", b=NB)).then_inc(back, 1)
                        dve.wait_ge(back, 1)
                clear(nc, sems.all)




def constants(nc, mem, w):
    with ExitStack() as ctx:
        sems = Semaphores(nc, ctx, "init", "loaded done")
        loaded, done = sems.all
        with nc.Block() as block:
            @block.sync
            def _(sp):
                sp.dma_start(mem["ident"][:], w["ident"]).then_inc(loaded, 16)
                sp.dma_start(mem["x_all"][:].rearrange("p b (t d) -> p b t d", t=T),
                             w["x"].rearrange("b (t p) d -> p b t d", p=P)).then_inc(loaded, 16)
                sp.wait_ge(loaded, 32)

            @block.vector
            def _(dve):
                dve.wait_ge(loaded, 32)
                nc.vector.tensor_copy(mem["ident_bf"][:], mem["ident"][:]).then_inc(done, 1)
                dve.wait_ge(done, 1)
        clear(nc, sems.all)


def setup_exponent(nc, mem):
    sems = mem["norm_sems"]
    with nc.Block() as block:
        @block.vector
        def _(dve):
            nc.vector.memset(mem["exponent"][:], -0.5).then_inc(sems["chain"], 1)
            dve.wait_ge(sems["chain"], 1)
    clear(nc, sems.all)


def layer_norm(nc, mem, w):
    x_all = mem["x_all"]
    with ExitStack() as ctx:
        stats = ctx.enter_context(nc.sbuf_tensor("ln_stats", [P, B * T, 6], F32))
        mv = ctx.enter_context(nc.sbuf_tensor("ln_mv", [P, B * T, 2], F32))
        rstd = ctx.enter_context(nc.sbuf_tensor("ln_rstd", [P, B * T, 1], F32))
        exponent = ctx.enter_context(nc.sbuf_tensor("ln_exponent", [P, B * T, 1], F32))
        sems = Semaphores(nc, ctx, "ln", "kept chain pow_chain")
        kept, chain, pow_chain = sems.all
        x3 = x_all[:].rearrange("p b (t d) -> p (b t) d", t=T)
        with nc.Block() as block:
            @block.sync
            def _(sp):
                sp.dma_start(w["x_kept"], x_all[:].rearrange("p b n -> p (b n)")).then_inc(kept, 16)
                sp.wait_ge(kept, 16)

            @block.gpsimd
            def _(pool):
                nc.gpsimd.memset(exponent[:], -0.5).then_inc(pow_chain, 1)
                pool.wait_ge(pow_chain, 1)
                pool.wait_ge(chain, 2 * B * T + 1)
                nc.gpsimd.tensor_tensor(rstd[:], rstd[:], exponent[:], ALU.pow).then_inc(pow_chain, 1)

            @block.vector
            def _(dve):
                for k in range(B * T):
                    nc.vector.bn_stats(stats[:, k], x3[:, k]).then_inc(chain, 1)
                    dve.wait_ge(chain, 2 * k + 1)
                    nc.vector.bn_aggr(mv[:, k], stats[:, k]).then_inc(chain, 1)
                dve.wait_ge(chain, 2 * B * T)
                nc.vector.tensor_scalar(rstd[:], mv[:, :, 1:2], 1e-5, None, ALU.add).then_inc(chain, 1)
                dve.wait_ge(pow_chain, 2)
                dve.wait_ge(kept, 16)
                for k in range(B * T):
                    nc.vector.tensor_scalar(x3[:, k], x3[:, k], mv[:, k, 0:1], rstd[:, k], ALU.subtract, ALU.mult).then_inc(chain, 1)
                dve.wait_ge(chain, 3 * B * T + 1)
        clear(nc, sems.all)


def finish(nc, mem, w, out):
    x_all = mem["x_all"]
    with ExitStack() as ctx:
        kept = ctx.enter_context(nc.sbuf_tensor("kept_x", [P, B, T * D], F32))
        sems = Semaphores(nc, ctx, "fin", "loaded added stored")
        loaded, added, stored = sems.all
        with nc.Block() as block:
            @block.sync
            def _(sp):
                for b in range(B):
                    sp.dma_start(kept[:, b], w["x_kept"][:, b * T * D:(b + 1) * T * D]).then_inc(loaded, 16)
                    sp.wait_ge(loaded, 16 * (b + 1))
                for b in range(B):
                    sp.wait_ge(added, b + 1)
                    sp.dma_start(out[b].rearrange("(t p) d -> p t d", p=P), x_all[:, b].rearrange("p (t d) -> p t d", t=T)).then_inc(stored, 16)
                sp.wait_ge(stored, 16 * B)

            @block.vector
            def _(dve):
                for b in range(B):
                    dve.wait_ge(loaded, 16 * (b + 1))
                    nc.vector.tensor_tensor(x_all[:, b], x_all[:, b], kept[:, b], ALU.add).then_inc(added, 1)
        clear(nc, sems.all)


def program(nc, a, out):
    w = {"x": a["x"], "ident": a["c_ident"], "shift": a["c_shift"], "win_mask": a["c_win_mask"], "rope1": a["c_rope1"],
         "rope0": a["c_rope0"], "causal": a["c_causal"], "ones": a["c_ones"], "upper": a["c_upper"],
         "ctx": a["ctx_2048"], "mask": a["mask_BxS2_ik0"],
         "Wq": a["L0_xattn_Wq"], "Wkv": a["L0_xattn_Wkv"], "null_kv": a["L0_xattn_null_kv"], "Wout": a["L0_xattn_Wout"],
         "ln_scale": a["L0_xattn_ln_scale"], "ln_bias": a["L0_xattn_ln_bias"],
         "w_qkv": a["L0_ffn_w_qkv"], "w_o": a["L0_ffn_w_o"], "w_router": a["L0_ffn_w_router"], "g12": a["c_l0_g12"],
         "w1": a["L0_ffn_w1"], "w2": a["L0_ffn_w2"], "b": a["L1_xattn_b"],
         "Wqkv": a["L1_ffn_Wqkv"], "qk_scale": (a["L1_ffn_q_scale"], a["L1_ffn_k_scale"]), "Wo": a["L1_ffn_Wo"],
         "W1": a["L1_ffn_W1"], "cols": a["c_l1_cols"], "W2": a["L1_ffn_W2"], "b2": a["L1_ffn_b2"]}
    w["x_kept"] = nc.dram_tensor("x_kept", (P, B * T * D), F32, kind="Internal").ap()
    with ExitStack() as ctx:
        psum = ctx.enter_context(nc.psum_tensor("psum", [P, 8, 512], F32))
        mem = {"x_all": ctx.enter_context(nc.sbuf_tensor("x_all", [P, B, T * D], F32)),
               "ident": ctx.enter_context(nc.sbuf_tensor("ident", [P, P], F32)),
               "ident_bf": ctx.enter_context(nc.sbuf_tensor("ident_bf", [P, P], BF16)),
               "psum": psum, "bank": [psum[:, i] for i in range(8)]}
        constants(nc, mem, w)
        with ExitStack() as l0:
            for name, shape in (("stats", [P, T, 6]), ("mv", [P, T, 2]), ("rstd", [P, T]), ("exponent", [P, T])):
                mem[name] = l0.enter_context(nc.sbuf_tensor(name, shape, F32))
            mem["norm_sems"] = Semaphores(nc, l0, "nm", "mv_done chain pow_done scaled")
            setup_exponent(nc, mem)
            null_attention(nc, mem, w)
            with ExitStack() as moe:
                mem["moe_inT"] = moe.enter_context(nc.sbuf_tensor("moe_inT", [P, B, DC, S], F32))
                mem["logits"] = moe.enter_context(nc.sbuf_tensor("logits", [P, B, T, E], F32))
                mem["gates"] = moe.enter_context(nc.sbuf_tensor("gates", [P, NT, E], F32))
                causal_attention(nc, mem, w)
                gating(nc, mem, w)
                experts(nc, mem, w)
            memory_attention(nc, mem, w)
        layer_norm(nc, mem, w)
        local_layers(nc, mem, w)
        finish(nc, mem, w, out)


def shape_constants():
    f = np.float32
    out = {"c_ident": np.eye(P, dtype=f)}
    shift = np.zeros((2, P, P), f)
    shift[0, np.arange(P - 1), np.arange(1, P)] = 1.0
    shift[1, P - 1, 0] = 1.0
    out["c_shift"] = shift
    i = np.arange(WIN)[:, None]
    k = np.arange(WIN)[None, :]
    own, before = np.where(k <= i, 0, NEG), np.where(k >= i, 0, NEG)
    both = np.concatenate([before, own], 1)
    first = np.concatenate([np.full_like(before, NEG), own], 1)
    out["c_win_mask"] = np.stack([np.concatenate([first, both], 0), np.concatenate([both, both], 0)]).astype(f)
    half = np.arange(0, DH, 2, dtype=f)
    inv = (f(1.0) / f(10000.0) ** (half / f(DH))).astype(f)
    t = np.arange(S, dtype=f)
    fr = t[:, None] * inv[None, :]
    fr = np.concatenate([fr, fr], -1)
    base = (half + f(0.4 * DH)) / f(1.4 * DH)
    power = (t - S // 2) / f(WIN // 2)
    sc = base[None, :] ** power[:, None]
    sc = np.concatenate([sc, sc], -1).astype(f)
    sign = np.where(np.arange(DH) < HALF, -1.0, 1.0).astype(f)
    cos, sin = np.cos(fr), np.sin(fr) * sign
    out["c_rope1"] = np.stack([cos * sc, sin * sc, cos * (f(1.0) / sc), sin * (f(1.0) / sc)]).astype(f)
    theta = f(10000.0) ** (f(-2.0) * (np.arange(HD // 2, dtype=f) / f(HD)))
    fr0 = (t[:, None] * theta[None, :].astype(f)).astype(f)
    cos0 = np.repeat(np.cos(fr0), 2, axis=1)
    sin0 = np.repeat(np.sin(fr0), 2, axis=1) * np.where(np.arange(HD) % 2 == 0, -1.0, 1.0)
    out["c_rope0"] = np.stack([cos0, sin0], 1).astype(f)
    q = np.arange(P)
    out["c_causal"] = np.where(q[None, :] <= q[:, None], 0, NEG).astype(f)
    out["c_ones"] = np.ones((P, P), f)
    out["c_upper"] = (q[:, None] < q[None, :]).astype(f)
    return out


_INS = ['x', 'ctx_2048', 'mask_BxS2_ik0', 'L0_xattn_Wq', 'L0_xattn_Wkv', 'L0_xattn_null_kv', 'L0_xattn_Wout', 'L0_xattn_ln_scale', 'L0_xattn_ln_bias', 'L0_ffn_w_qkv', 'L0_ffn_w_o', 'L0_ffn_w_router', 'L0_ffn_w1', 'L0_ffn_w2', 'L1_xattn_b', 'L1_ffn_Wqkv', 'L1_ffn_q_scale', 'L1_ffn_k_scale', 'L1_ffn_Wo', 'L1_ffn_W1', 'L1_ffn_W2', 'L1_ffn_b2']
_OUT = (B, S, D)


def l1_columns(b1, ln_g, ln_b):
    halves = b1.reshape(DEPTH, 2, FI)
    padded = np.zeros((DEPTH, 2, FC * P), b1.dtype)
    padded[:, :, 0:FI] = halves
    columns = [padded.reshape(DEPTH, 2 * FC, P), ln_g.reshape(DEPTH, DC, P), ln_b.reshape(DEPTH, DC, P)]
    return np.ascontiguousarray(np.concatenate(columns, 1).transpose(0, 2, 1))


def kernel(**inputs):
    import concourse.bacc as bacc
    from concourse.bass_utils import run_bass_kernel_spmd

    nc = bacc.Bacc("TRN2", target_bir_lowering=False, num_devices=1)
    arrays = {name: np.ascontiguousarray(inputs[name]) for name in _INS}
    arrays.update(shape_constants())
    arrays["c_l1_cols"] = l1_columns(*(np.asarray(inputs[n]) for n in ("L1_ffn_b1", "L1_ffn_ln_g", "L1_ffn_ln_b")))
    arrays["c_l0_g12"] = np.ascontiguousarray(np.concatenate([np.asarray(inputs[n]).reshape(DC, P) for n in ("L0_ffn_g1", "L0_ffn_g2")]).T)
    aps = {name: nc.dram_tensor(name, a.shape, mybir.dt.from_np(a.dtype), kind="ExternalInput").ap() for name, a in arrays.items()}
    out = nc.dram_tensor("out", _OUT, F32, kind="ExternalOutput").ap()
    program(nc, aps, out)
    return run_bass_kernel_spmd(nc, [arrays], core_ids=[0]).results[0]["out"]
```

```python
from contextlib import ExitStack

import numpy as np
import concourse.bass as bass
from concourse import mybir

F32 = mybir.dt.float32
BF16 = mybir.dt.bfloat16
F32R = mybir.dt.float32r
I32 = mybir.dt.int32
ALU = mybir.AluOpType
ACT = mybir.ActivationFunctionType
AX = mybir.AxisListType.X

P = 128
B, S, D = 4, 512, 256
T = S // P
DC = D // P
NT = B * T
NEG = -1e30

DEPTH, HEADS, DH, WIN = 6, 16, 64, 64
INNER = HEADS * DH
FI = int(D * 4 * 2 / 3)
FC = -(-FI // P)
FR = FI - (FC - 1) * P
HALF = DH // 2
GROUP = 4
NG = T * HEADS // GROUP
QK_SCALE = 8.0


def clear(nc, sems):
    nums = [s.num for s in sems]
    assert nums == list(range(nums[0], nums[0] + len(nums)))
    nc.gpsimd.sem_clear(range(nums[0], nums[0] + len(nums)))
    nc.all_engine_barrier()


class Semaphores:

    def __init__(self, nc, ctx, stage, names):
        self.all = [ctx.enter_context(nc.semaphore(f"s_{stage}_{n}")) for n in names.split()]
        self.by_name = dict(zip(names.split(), self.all))

    def __getitem__(self, name):
        return self.by_name[name]




def normalise(nc, mem, src, dst, eps, centred):
    stats, mv, rstd, exponent = mem["stats"], mem["mv"], mem["rstd"], mem["exponent"]
    sems = mem["norm_sems"]
    mv_done, chain, pow_done, scaled = sems.all

    def tile(y, n):
        return y[:, n // T, n % T * D:(n % T + 1) * D]

    with nc.Block() as block:
        @block.vector
        def _(dve):
            for n in range(NT):
                nc.vector.bn_stats(stats[:, n], tile(src, n)).then_inc(chain, 1)
            for n in range(NT):
                dve.wait_ge(chain, n + 1)
                nc.vector.bn_aggr(mv[:, n], stats[:, n]).then_inc(mv_done, 1)
            dve.wait_ge(mv_done, NT)
            if centred:
                nc.vector.tensor_scalar(rstd[:], mv[:, :, 1], eps, None, ALU.add).then_inc(chain, 1)
            else:
                nc.vector.tensor_tensor(rstd[:], mv[:, :, 0], mv[:, :, 0], ALU.mult).then_inc(mv_done, 1)
                dve.wait_ge(mv_done, NT + 1)
                nc.vector.scalar_tensor_tensor(rstd[:], mv[:, :, 1], eps, rstd[:], ALU.add, ALU.add).then_inc(chain, 1)
            dve.wait_ge(pow_done, 1)
            for n in range(NT):
                if centred:
                    nc.vector.tensor_scalar(tile(dst, n), tile(src, n), mv[:, n, 0:1], rstd[:, n:n + 1], ALU.subtract, ALU.mult).then_inc(scaled, 1)
                else:
                    nc.vector.tensor_scalar(tile(dst, n), tile(src, n), rstd[:, n:n + 1], None, ALU.mult).then_inc(scaled, 1)
            dve.wait_ge(scaled, NT)

        @block.gpsimd
        def _(pool):
            pool.wait_ge(chain, NT + 1)
            nc.gpsimd.tensor_tensor(rstd[:], rstd[:], exponent[:], ALU.pow).then_inc(pow_done, 1)
            pool.wait_ge(pow_done, 1)
    clear(nc, sems.all)



CTX, M = 512, 64
CC = CTX // P
MN = M + 1


def null_attention(nc, mem, w):
    with ExitStack() as ctx:
        def sb(name, shape, dt=F32):
            return ctx.enter_context(nc.sbuf_tensor("xa_" + name, shape, dt))

        x_all, ident, bank = mem["x_all"], mem["ident"], mem["bank"]
        wq = sb("wq", [P, DC, INNER])
        wkv = sb("wkv", [P, CC, 2 * INNER])
        wout = sb("wout", [P, INNER // P, D])
        ln_scale = sb("ln_scale", [P, D])
        ln_bias = sb("ln_bias", [P, D])
        null_k = sb("null_k", [P, 1])
        null_v = sb("null_v", [MN, DH])
        xn = sb("xn", [P, B, T * D])
        xn_b = sb("xn_b", [P, T * D])
        xnT = sb("xnT", [P, DC, S])
        contexts = sb("contexts", [M, B, CTX])
        contextT = sb("contextT", [P, CC, B, M])
        kTs = sb("kTs", [P, INNER // P, B, MN])
        vs = sb("vs", [MN, B, HEADS, DH])
        qT = sb("qT", [P, INNER // P, S])
        kT = sb("kT", [P, INNER // P, MN])
        v = sb("v", [MN, HEADS, DH])
        smax = sb("smax", [P, 2, GROUP])
        prob = sb("prob", [P, 6, GROUP, MN])
        probT = sb("probT", [MN, 4, GROUP * P])
        rsum = sb("rsum", [P, 2, GROUP])
        oT = sb("oT", [P, 2, INNER // P, P])
        y = sb("y", [P, B, T * D])

        sems = Semaphores(nc, ctx, "xa", "wload setup xin kv_in xt_full xt_read ct_full ct_read kv_full kv_read v_full v_read q_full q_read "
                          "s_full s_read exp_done normed tr_full tr_read o_full o_read p_full p_read dve_chain back")
        (wload, setup, xin, kv_in, xt_full, xt_read, ct_full, ct_read, kv_full, kv_read, v_full, v_read, q_full, q_read,
         s_full, s_read, exp_done, normed, tr_full, tr_read, o_full, o_read, p_full, p_read, dve_chain, back) = sems.all

        with nc.Block() as block:
            @block.sync
            def _(sp):
                sp.dma_start(wq[:], w["Wq"].rearrange("(c p) n -> p c n", p=P)).then_inc(wload, 16)
                sp.dma_start(wout[:], w["Wout"].rearrange("(c p) n -> p c n", p=P)).then_inc(wload, 16)
                sp.dma_start(ln_scale[:], w["ln_scale"][None, :].to_broadcast([P, D])).then_inc(wload, 16)
                sp.dma_start(ln_bias[:], w["ln_bias"][None, :].to_broadcast([P, D])).then_inc(wload, 16)
                for r in range(2):
                    sp.dma_start(null_k[r * DH:(r + 1) * DH, :], w["null_kv"][0, :, None]).then_inc(wload, 16)
                sp.dma_start(contexts[:], w["ctx"].rearrange("b m d -> m b d")).then_inc(wload, 16)
                sp.dma_start(null_v[M:MN, :], w["null_kv"][1, None, :]).then_inc(wload, 16)

            @block.scalar
            def _(act):
                act.dma_start(wkv[:], w["Wkv"].rearrange("(c p) n -> p c n", p=P)).then_inc(wload, 16)
        normalise(nc, mem, x_all, xn, 1e-5, True)

        with nc.Block() as block:
            @block.tensor
            def _(pe):
                pe.wait_ge(wload, 16 * 9)
                for b in range(B):
                    for c in range(CC):
                        mm = nc.tensor.transpose(bank[b][:, c * M:(c + 1) * M], contexts[:, b, c * P:(c + 1) * P], ident[0:M, 0:M])
                    mm.then_inc(ct_full, 1)
                pe.wait_ge(ct_read, B)
                for c in range(INNER // P):
                    if c >= 2:
                        pe.wait_ge(kv_read, c - 1)
                    for k in range(CC):
                        mm = nc.tensor.matmul(bank[4 + c % 2][:, 0:B * M], wkv[:, k, c * P:(c + 1) * P], contextT[:, k].rearrange("p b m -> p (b m)"),
                                              start=(k == 0), stop=(k == CC - 1))
                    mm.then_inc(kv_full, 1)
                for n in range(2 * B):
                    if n >= 2:
                        pe.wait_ge(v_read, n - 1)
                    for k in range(CC):
                        mm = nc.tensor.matmul(bank[6 + n % 2][0:M, :], contextT[:, k, n // 2, :], wkv[:, k, INNER + n % 2 * S:INNER + (n % 2 + 1) * S],
                                              start=(k == 0), stop=(k == CC - 1))
                    mm.then_inc(v_full, 1)

            @block.scalar
            def _(act):
                for b in range(B):
                    act.wait_ge(ct_full, b + 1)
                    nc.scalar.copy(contextT[:, :, b, :], bank[b][:, 0:CC * M].rearrange("p (c m) -> p c m", c=CC)).then_inc(ct_read, 1)
                for c in range(INNER // P):
                    act.wait_ge(kv_full, c + 1)
                    nc.scalar.copy(kTs[:, c, :, 0:M], bank[4 + c % 2][:, 0:B * M].rearrange("p (b m) -> p b m", b=B)).then_inc(kv_read, 1)
                act.wait_ge(kv_read, INNER // P)

            @block.vector
            def _(dve):
                dve.wait_ge(wload, 16 * 9)
                for b in range(B):
                    nc.vector.tensor_copy(vs[M:MN, b], null_v[M:MN, None, :].to_broadcast([1, HEADS, DH])).then_inc(setup, 1)
                    nc.vector.tensor_copy(kTs[:, :, b, M:MN], null_k[:, None, :].to_broadcast([P, INNER // P, 1])).then_inc(setup, 1)
                for n in range(2 * B):
                    dve.wait_ge(v_full, n + 1)
                    nc.vector.tensor_copy(vs[0:M, n // 2, 8 * (n % 2):8 * (n % 2) + 8, :],
                                          bank[6 + n % 2][0:M, :].rearrange("p (h d) -> p h d", h=8)).then_inc(v_read, 1)
                dve.wait_ge(v_read, 2 * B)
                dve.wait_ge(setup, 2 * B)
        clear(nc, sems.all)

        pairs = NG // 2
        attention = []
        for k in range(pairs + 4):
            if k < pairs:
                attention.append(("scores", k))
            if 0 <= k - 1 < pairs:
                attention += [("exp", 2 * k - 2), ("exp", 2 * k - 1)]
            if k % 2 == 1 and 0 <= (k - 5) // 2 < T:
                attention.append(("project", (k - 5) // 2))
            if 0 <= k - 3 < pairs:
                attention += [("values", k - 3), ("gather", k - 3)]
            if 0 <= k - 2 < pairs:
                attention += [("probT", 2 * k - 4), ("probT", 2 * k - 3)]
            if 0 <= k - 1 < pairs:
                attention += [("norm", 2 * k - 2), ("norm", 2 * k - 1)]
        out_turn, out_read = {}, []
        for kind, n in attention:
            if kind in ("values", "project"):
                out_turn[kind, n] = len(out_read)
                out_read.append((o_read if kind == "values" else p_read, n + 1))

        with nc.Fori(0, B) as b:
            with nc.Block() as block:
                @block.tensor
                def _(pe):
                    pe.wait_ge(xin, 1)
                    for d in range(DC):
                        for t in range(T):
                            mm = nc.tensor.transpose(bank[d][:, t * P:(t + 1) * P], xn_b[:, t * D + d * P:t * D + (d + 1) * P], ident[:])
                        mm.then_inc(xt_full, 1)
                    pe.wait_ge(xt_read, DC)
                    for c in range(INNER // P):
                        if c >= 2:
                            pe.wait_ge(q_read, c - 1)
                        for d in range(DC):
                            mm = nc.tensor.matmul(bank[6 + c % 2][:], wq[:, d, c * P:(c + 1) * P], xnT[:, d, :], start=(d == 0), stop=(d == DC - 1))
                        mm.then_inc(q_full, 1)

                    pe.wait_ge(kv_in, 2)
                    pe.wait_ge(q_read, INNER // P)
                    def output_bank(turn):
                        if turn >= 2:
                            pe.wait_ge(*out_read[turn - 2])
                        return bank[6 + turn % 2]

                    for kind, n in attention:
                        if kind == "scores":
                            t, c0 = n // 2, GROUP * (n % 2)
                            if n >= 2:
                                pe.wait_ge(s_read, 2 * n - 2)
                            for j in range(GROUP):
                                for odd in range(2):
                                    for k in range(2):
                                        r, q0 = DH * k, DH * (odd ^ k)
                                        mm = nc.tensor.matmul(bank[(2 * n + k) % 4][q0:q0 + DH, j * MN:(j + 1) * MN],
                                                              qT[r:r + DH, c0 + j, t * P + q0:t * P + q0 + DH], kT[r:r + DH, c0 + j, :],
                                                              start=True, stop=True, skip_group_check=True)
                                        if j == GROUP - 1 and odd == 1:
                                            mm.then_inc(s_full, 1)
                        elif kind == "probT":
                            if n >= 2:
                                pe.wait_ge(tr_read, n - 1)
                            pe.wait_ge(normed, n + 1)
                            for j in range(GROUP):
                                mm = nc.tensor.transpose(bank[4 + n % 2][0:MN, j * P:(j + 1) * P], prob[:, n % 6, j, :], ident[:])
                            mm.then_inc(tr_full, 1)
                        elif kind == "values":
                            pe.wait_ge(tr_read, 2 * n + 2)
                            dst = output_bank(out_turn[kind, n])
                            for j in range(GROUP):
                                for k in range(2):
                                    mm = nc.tensor.matmul(dst[k * DH:(k + 1) * DH, j * P:(j + 1) * P], v[:, 2 * (GROUP * (n % 2) + j) + k, :],
                                                          probT[:, (2 * n + k) % 4, j * P:(j + 1) * P], start=True, stop=True, skip_group_check=True)
                            mm.then_inc(o_full, 1)
                        elif kind == "project":
                            pe.wait_ge(o_read, 2 * n + 2)
                            dst = output_bank(out_turn[kind, n])
                            for c in range(INNER // P):
                                mm = nc.tensor.matmul(dst[:, 0:D], oT[:, n % 2, c], wout[:, c, :], start=(c == 0), stop=(c == INNER // P - 1))
                            mm.then_inc(p_full, 1)

                @block.scalar
                def _(act):
                    for d in range(DC):
                        act.wait_ge(xt_full, d + 1)
                        nc.scalar.copy(xnT[:, d, :], bank[d][:]).then_inc(xt_read, 1)
                    for c in range(INNER // P):
                        act.wait_ge(q_full, c + 1)
                        nc.scalar.mul(qT[:, c, :], bank[6 + c % 2][:], DH ** -0.5).then_inc(q_read, 1)
                    for kind, n in attention:
                        if kind == "exp":
                            act.wait_ge(s_read, n + 1)
                            nc.scalar.activation(prob[:, n % 6], prob[:, n % 6], ACT.Exp).then_inc(exp_done, 1)
                        elif kind == "probT":
                            act.wait_ge(tr_full, n + 1)
                            if n >= 4:
                                act.wait_ge(o_full, n // 2 - 1)
                            nc.scalar.copy(probT[:, n % 4], bank[4 + n % 2][0:MN, :]).then_inc(tr_read, 1)
                        elif kind == "gather":
                            t = n // 2
                            act.wait_ge(o_full, n + 1)
                            if t >= 2:
                                act.wait_ge(p_full, t - 1)
                            nc.scalar.copy(oT[:, t % 2, GROUP * (n % 2):GROUP * (n % 2) + GROUP],
                                           bank[6 + out_turn["values", n] % 2].rearrange("p (c q) -> p c q", c=GROUP)).then_inc(o_read, 1)

                @block.vector
                def _(dve):
                    links = [0]

                    def link(ins):
                        links[0] += 1
                        ins.then_inc(dve_chain, 1)
                        dve.wait_ge(dve_chain, links[0])

                    nc.vector.tensor_copy(xn_b[:], xn[:, b]).then_inc(xin, 1)
                    nc.vector.tensor_copy(kT[:], kTs[:, :, b]).then_inc(kv_in, 1)
                    nc.vector.tensor_copy(v[:], vs[:, b]).then_inc(kv_in, 1)
                    for kind, n in attention:
                        if kind == "scores":
                            for g in (2 * n, 2 * n + 1):
                                dve.wait_ge(s_full, g + 1)
                                s3 = bank[g % 4][:, 0:GROUP * MN].rearrange("p (g q) -> p g q", g=GROUP)
                                link(nc.vector.tensor_reduce(smax[:, g % 2], s3, AX, ALU.max))
                                if g >= 6:
                                    dve.wait_ge(tr_full, g - 5)
                                nc.vector.tensor_tensor(prob[:, g % 6], s3, smax[:, g % 2, :, None].to_broadcast([P, GROUP, MN]),
                                                        ALU.subtract).then_inc(s_read, 1)
                        elif kind == "norm":
                            dve.wait_ge(exp_done, n + 1)
                            link(nc.vector.tensor_reduce(rsum[:, n % 2], prob[:, n % 6], AX, ALU.add))
                            link(nc.vector.reciprocal(rsum[:, n % 2], rsum[:, n % 2]))
                            nc.vector.tensor_tensor(prob[:, n % 6], prob[:, n % 6], rsum[:, n % 2, :, None].to_broadcast([P, GROUP, MN]),
                                                    ALU.mult).then_inc(normed, 1)
                        elif kind == "project":
                            dve.wait_ge(p_full, n + 1)
                            nc.vector.tensor_copy(y[:, b, n * D:(n + 1) * D], bank[6 + out_turn[kind, n] % 2][:, 0:D]).then_inc(p_read, 1)
                    dve.wait_ge(p_read, T)
            clear(nc, sems.all)
        normalise(nc, mem, y, y, 1e-6, True)
        with nc.Block() as block:
            @block.vector
            def _(dve):
                for b in range(B):
                    yb, whole = y[:, b].rearrange("p (t d) -> p t d", t=T), [P, T, D]
                    nc.vector.tensor_tensor(yb, yb, ln_scale[:, None, :].to_broadcast(whole), ALU.mult).then_inc(back, 1)
                for b in range(B):
                    yb, whole = y[:, b].rearrange("p (t d) -> p t d", t=T), [P, T, D]
                    dve.wait_ge(back, b + 1)
                    nc.vector.tensor_tensor(yb, yb, ln_bias[:, None, :].to_broadcast(whole), ALU.add).then_inc(back, 1)
                for b in range(B):
                    dve.wait_ge(back, B + b + 1)
                    nc.vector.tensor_tensor(x_all[:, b], x_all[:, b], y[:, b], ALU.add).then_inc(back, 1)
                dve.wait_ge(back, 3 * B)
        clear(nc, sems.all)



HD = D // HEADS
SLOT = 32
HPC = P // SLOT
HC = HEADS // HPC
E, FF = 8, 512


def causal_attention(nc, mem, w):
    with ExitStack() as ctx:
        def sb(name, shape, dt=F32):
            return ctx.enter_context(nc.sbuf_tensor("ca_" + name, shape, dt))

        x_all, ident, ident_bf, bank = mem["x_all"], mem["ident"], mem["ident_bf"], mem["bank"]
        wqkv = sb("wqkv", [P, DC, 3 * D])
        wo = sb("wo", [P, HC, D])
        wr = sb("wr", [P, DC, E])
        g12 = sb("g12", [P, 2 * DC])
        rope = sb("rope", [P, T, 2, HD])
        causal = sb("causal", [P, P])
        causal_bf = sb("causal_bf", [P, P], BF16)
        z = sb("z", [P, B, T * D])
        zr = sb("zr", [P, B, T * D])
        zr_b = sb("zr_b", [P, T * D])
        zT = sb("zT", [P, DC, S])
        cosd = sb("cosd", [P, 2, 2 * D])
        rot = sb("rot", [P, 2, 2 * D])
        qk = sb("qk", [P, 2, 2 * HEADS, SLOT])
        qT = sb("qT", [P, HC, S])
        kT = sb("kT", [P, HC, S])
        v = sb("v", [P, T, HEADS, SLOT])
        smax = sb("smax", [P, 2 * HPC])
        total = sb("total", [P, 2 * HPC])
        prob = sb("prob", [P, HPC, S])
        probT = sb("probT", [P, 2 * HPC, S])
        oT = sb("oT", [P, 2, HC, P])
        sems = Semaphores(nc, ctx, "ca", "wload setup xin zt_full zt_read qk_full qk_read v_read padded tr_full tr_read s_full "
                          "max_done exp_done normed o_full o_read p_full p_read dve_chain")
        (wload, setup, xin, zt_full, zt_read, qk_full, qk_read, v_read, padded, tr_full, tr_read, s_full,
         max_done, exp_done, normed, o_full, o_read, p_full, p_read, dve_chain) = sems.all
        HS = HD ** -0.5

        with nc.Block() as block:
            @block.sync
            def _(sp):
                sp.dma_start(wqkv[:], w["w_qkv"].rearrange("(c p) n -> p c n", p=P)).then_inc(wload, 16)
                sp.wait_ge(setup, 1)
                for h in range(HPC):
                    sp.dma_start(wo[h * SLOT:h * SLOT + HD], w["w_o"].rearrange("(c h i) n -> h i c n", h=HPC, i=HD)[h]).then_inc(wload, 16)
                sp.dma_start(wr[:], w["w_router"].rearrange("(c p) n -> p c n", p=P)).then_inc(wload, 16)
                sp.dma_start(g12[:], w["g12"]).then_inc(wload, 16)
                sp.dma_start(rope[:], w["rope0"].rearrange("(t p) k d -> p t k d", p=P)).then_inc(wload, 16)
                sp.dma_start(causal[:], w["causal"]).then_inc(wload, 16)
                sp.wait_ge(wload, 16 * (5 + HPC))

            @block.vector
            def _(dve):
                nc.vector.memset(wo[:], 0.0).then_inc(setup, 1)
                nc.vector.memset(v[:], 0.0).then_inc(setup, 1)
                nc.vector.memset(qk[:], 0.0).then_inc(setup, 1)
                dve.wait_ge(wload, 16 * (5 + HPC))
                nc.vector.tensor_copy(causal_bf[:], causal[:]).then_inc(setup, 1)
                dve.wait_ge(setup, 4)
        clear(nc, sems.all)

        pairs = T * HEADS // 2
        attention = []
        for k in range(pairs + 7):
            if k < pairs:
                attention.append(("scores", k))
            if 0 <= k - 1 < pairs:
                attention += [("exp", 2 * (k - 1)), ("exp", 2 * (k - 1) + 1)]
            r = (k - 4) // 2
            if k % 2 == 1 and r >= 0 and r % HC == HC - 1:
                attention.append(("project", r // HC))
            if k % 2 == 0 and 0 <= r < T * HC:
                attention += [("values", r), ("gather", r)]
            if 0 <= k - 2 < pairs:
                attention += [("probT", 2 * (k - 2)), ("probT", 2 * (k - 2) + 1)]
            if 0 <= k - 1 < pairs:
                attention.append(("norm", k - 1))
        tr_turn = {key: n for n, key in enumerate([("qk", n) for n in range(2 * T)] + [a for a in attention if a[0] == "probT"])}

        normalise(nc, mem, x_all, z, 1e-5, True)
        normalise(nc, mem, z, zr, 1e-6, False)
        with nc.Fori(0, B) as b:
            with nc.Block() as block:
                @block.tensor
                def _(pe):
                    pe.wait_ge(xin, 1)
                    for d in range(DC):
                        for t in range(T):
                            mm = nc.tensor.transpose(bank[d][:, t * P:(t + 1) * P], zr_b[:, t * D + d * P:t * D + (d + 1) * P], ident[:])
                        mm.then_inc(zt_full, 1)
                    pe.wait_ge(zt_read, DC)
                    for t in range(T + 1):
                        if t < T:
                            if t >= 2:
                                pe.wait_ge(qk_read, t - 1)
                                pe.wait_ge(v_read, t - 1)
                            for at, n, to in ((0, 2 * D, bank[t % 2]), (2 * D, D, bank[2 + t % 2])):
                                for d in range(DC):
                                    mm = nc.tensor.matmul(to[:, 0:n], zT[:, d, t * P:(t + 1) * P], wqkv[:, d, at:at + n],
                                                          start=(d == 0), stop=(d == DC - 1))
                                mm.then_inc(qk_full, 1)
                        if t >= 1:
                            pe.wait_ge(padded, t)
                            for part in range(2):
                                u = 2 * (t - 1) + part
                                if u >= 2:
                                    pe.wait_ge(tr_read, u - 1)
                                for c in range(HC):
                                    head = part * HEADS + c * HPC
                                    mm = nc.tensor.transpose(bank[4 + u % 2][:, c * P:(c + 1) * P],
                                                             qk[:, (t - 1) % 2, head:head + HPC, :].rearrange("p h d -> p (h d)"), ident[:])
                                mm.then_inc(tr_full, 1)
                    pe.wait_ge(tr_read, 2 * T)
                    pe.wait_ge(v_read, T)
                    for kind, n in attention:
                        if kind == "scores":
                            t, c = n // (HEADS // 2), n // 2 % HC
                            keys = (t + 1) * P
                            if n >= 2:
                                pe.wait_ge(exp_done, 2 * n - 2)
                            for h in range(2):
                                r = SLOT * ((2 * n + h) % HPC)
                                nc.tensor.matmul(bank[(2 * n + h) % 4][:, 0:keys], qT[r:r + SLOT, c, t * P:(t + 1) * P], kT[r:r + SLOT, c, 0:keys],
                                                 start=True, stop=False)
                            for h in range(2):
                                nc.tensor.matmul(bank[(2 * n + h) % 4][:, t * P:keys], ident_bf[:], causal_bf[:], start=False, stop=True).then_inc(s_full, 1)
                        elif kind == "probT":
                            u = tr_turn[kind, n]
                            pe.wait_ge(tr_read, u - 1)
                            pe.wait_ge(normed, n + 1)
                            for k in range(n // HEADS + 1):
                                mm = nc.tensor.transpose(bank[4 + u % 2][:, k * P:(k + 1) * P], prob[:, n % HPC, k * P:(k + 1) * P], ident[:])
                            mm.then_inc(tr_full, 1)
                        elif kind == "values":
                            t, c = n // HC, n % HC
                            pe.wait_ge(tr_read, tr_turn["probT", HPC * n + HPC - 1] + 1)
                            if t >= 1:
                                pe.wait_ge(o_read, n - HC + 1)
                            for k in range(t + 1):
                                for h in range(HPC):
                                    mm = nc.tensor.matmul(bank[6][h * SLOT:(h + 1) * SLOT, c * P:(c + 1) * P], v[:, k, HPC * c + h, :],
                                                          probT[:, (HPC * n + h) % (2 * HPC), k * P:(k + 1) * P],
                                                          start=(k == 0), stop=(k == t), skip_group_check=True)
                            mm.then_inc(o_full, 1)
                        elif kind == "project":
                            pe.wait_ge(o_read, HC * n + HC)
                            if n >= 1:
                                pe.wait_ge(p_read, n)
                            for c in range(HC):
                                mm = nc.tensor.matmul(bank[7][:, 0:D], oT[:, n % 2, c], wo[:, c, :], start=(c == 0), stop=(c == HC - 1))
                            mm.then_inc(p_full, 1)

                @block.scalar
                def _(act):
                    for d in range(DC):
                        act.wait_ge(zt_full, d + 1)
                        nc.scalar.mul(zT[:, d, :], bank[d][:], g12[:, d:d + 1]).then_inc(zt_read, 1)
                    for t in range(T + 1):
                        if t < T:
                            act.wait_ge(qk_full, 2 * t + 2)
                            nc.scalar.copy(v[:, t, :, 0:HD], bank[2 + t % 2][:, 0:D].rearrange("p (h d) -> p h d", h=HEADS)).then_inc(v_read, 1)
                        if t >= 1:
                            for part, dst in ((0, qT), (1, kT)):
                                u = 2 * (t - 1) + part
                                act.wait_ge(tr_full, u + 1)
                                nc.scalar.copy(dst[:, :, (t - 1) * P:t * P], bank[4 + u % 2][:].rearrange("p (c q) -> p c q", c=HC)).then_inc(tr_read, 1)
                    for kind, n in attention:
                        if kind == "exp":
                            keys = (n // HEADS + 1) * P
                            act.wait_ge(max_done, n // 2 + 1)
                            if n >= HPC:
                                act.wait_ge(tr_full, tr_turn["probT", n - HPC] + 1)
                            i = n % (2 * HPC)
                            nc.scalar.activation(prob[:, n % HPC, 0:keys], bank[n % HPC][:, 0:keys], ACT.Exp, bias=smax[:, i:i + 1],
                                                 scale=HS, accum_out=total[:, i:i + 1]).then_inc(exp_done, 1)
                        elif kind == "probT":
                            u, keys = tr_turn[kind, n], (n // HEADS + 1) * P
                            act.wait_ge(tr_full, u + 1)
                            if n >= 2 * HPC:
                                act.wait_ge(o_full, n // HPC - 1)
                            nc.scalar.copy(probT[:, n % (2 * HPC), 0:keys], bank[4 + u % 2][:, 0:keys]).then_inc(tr_read, 1)
                        elif kind == "gather":
                            t, c = n // HC, n % HC
                            act.wait_ge(o_full, n + 1)
                            if t >= 2:
                                act.wait_ge(p_full, t - 1)
                            nc.scalar.copy(oT[:, t % 2, c], bank[6][:, c * P:(c + 1) * P]).then_inc(o_read, 1)

                @block.vector
                def _(dve):
                    links = [0]

                    def link(ins):
                        links[0] += 1
                        ins.then_inc(dve_chain, 1)
                        dve.wait_ge(dve_chain, links[0])

                    nc.vector.tensor_copy(zr_b[:], zr[:, b]).then_inc(xin, 1)
                    for t in range(T):
                        dve.wait_ge(qk_full, 2 * t + 1)
                        src = bank[t % 2][:].rearrange("p (h d) -> p h d", d=HD)
                        pairs = bank[t % 2][:].rearrange("p (h k i) -> p h k i", i=2, k=HD // 2)
                        cd = cosd[:, t % 2].rearrange("p (h d) -> p h d", d=HD)
                        rt = rot[:, t % 2].rearrange("p (h d) -> p h d", d=HD)
                        rp = rot[:, t % 2].rearrange("p (h k i) -> p h k i", i=2, k=HD // 2)
                        sn = rope[:, t, 1].rearrange("p (k i) -> p k i", i=2)
                        shape = [P, 2 * HEADS, HD // 2]
                        nc.vector.tensor_tensor(cd, src, rope[:, t, 0, None, :].to_broadcast([P, 2 * HEADS, HD]), ALU.mult).then_inc(dve_chain, 1)
                        nc.vector.tensor_tensor(rp[:, :, :, 0], pairs[:, :, :, 1], sn[:, None, :, 0].to_broadcast(shape), ALU.mult).then_inc(dve_chain, 1)
                        nc.vector.tensor_tensor(rp[:, :, :, 1], pairs[:, :, :, 0], sn[:, None, :, 1].to_broadcast(shape), ALU.mult).then_inc(qk_read, 1)
                        links[0] += 2
                        dve.wait_ge(dve_chain, links[0])
                        dve.wait_ge(qk_read, t + 1)
                        if t >= 2:
                            dve.wait_ge(tr_full, 2 * (t - 1))
                        nc.vector.tensor_tensor(qk[:, t % 2, :, 0:HD], cd, rt, ALU.add).then_inc(padded, 1)

                    for kind, n in attention:
                        if kind == "scores":
                            keys = (2 * n // HEADS + 1) * P
                            i = 2 * n % (2 * HPC)
                            if n >= HPC:
                                dve.wait_ge(exp_done, 2 * (n - HPC) + 2)
                            for h in range(2):
                                dve.wait_ge(s_full, 2 * n + h + 1)
                                red = nc.vector.tensor_reduce(smax[:, i + h:i + h + 1], bank[(2 * n + h) % 4][:, 0:keys], AX, ALU.max)
                            link(red)
                            nc.vector.tensor_scalar(smax[:, i:i + 2], smax[:, i:i + 2], -HS, None, ALU.mult).then_inc(max_done, 1)
                        elif kind == "norm":
                            keys = (2 * n // HEADS + 1) * P
                            i = 2 * n % (2 * HPC)
                            dve.wait_ge(exp_done, 2 * n + 2)
                            link(nc.vector.reciprocal(total[:, i:i + 2], total[:, i:i + 2]))
                            for h in range(2):
                                p1 = prob[:, (2 * n + h) % HPC, 0:keys]
                                nc.vector.tensor_scalar(p1, p1, total[:, i + h:i + h + 1], None, ALU.mult).then_inc(normed, 1)
                        elif kind == "project":
                            dve.wait_ge(p_full, n + 1)
                            zs = z[:, b, n * D:(n + 1) * D]
                            nc.vector.tensor_tensor(zs, zs, bank[7][:, 0:D], ALU.add).then_inc(p_read, 1)
                    dve.wait_ge(p_read, T)
            clear(nc, sems.all)
        normalise(nc, mem, z, zr, 1e-6, False)
        moe_inT = mem["moe_inT"]
        with nc.Block() as block:
            @block.tensor
            def _(pe):
                for b in range(B + 1):
                    if b < B:
                        for d in range(DC):
                            if b >= 2:
                                pe.wait_ge(zt_read, DC * (b - 2) + d + 1)
                            for t in range(T):
                                mm = nc.tensor.transpose(bank[DC * (b % 2) + d][:, t * P:(t + 1) * P], zr[:, b, t * D + d * P:t * D + (d + 1) * P], ident[:])
                            mm.then_inc(zt_full, 1)
                    if b >= 1:
                        pe.wait_ge(zt_read, DC * b)
                        for t in range(T):
                            for d in range(DC):
                                mm = nc.tensor.matmul(bank[3 + b][:, t * E:(t + 1) * E], moe_inT[:, b - 1, d, t * P:(t + 1) * P], wr[:, d, :],
                                                      start=(d == 0), stop=(d == DC - 1), skip_group_check=True)
                        mm.then_inc(qk_full, 1)

            @block.scalar
            def _(act):
                for n in range(B * DC):
                    b, d = n // DC, n % DC
                    act.wait_ge(zt_full, n + 1)
                    nc.scalar.mul(moe_inT[:, b, d, :], bank[DC * (b % 2) + d][:], g12[:, DC + d:DC + d + 1]).then_inc(zt_read, 1)
                act.wait_ge(zt_read, B * DC)

            @block.vector
            def _(dve):
                for b in range(B):
                    nc.vector.tensor_tensor(x_all[:, b], x_all[:, b], z[:, b], ALU.add).then_inc(setup, 1)
                for b in range(B):
                    dve.wait_ge(qk_full, b + 1)
                    nc.vector.tensor_copy(mem["logits"][:, b], bank[4 + b][:, 0:T * E].rearrange("p (t e) -> p t e", e=E)).then_inc(setup, 1)
                dve.wait_ge(setup, 2 * B)
        clear(nc, sems.all)



TOP_K = 2
CAP = max(-(-(2 * 512 * TOP_K * 5) // (4 * E)), 1)
BITS = 30


def gating(nc, mem, w):
    with ExitStack() as ctx:
        def sb(name, shape, dt=F32):
            return ctx.enter_context(nc.sbuf_tensor("gt_" + name, shape, dt))

        bank = mem["bank"]
        prob = mem["logits"][:].rearrange("p b t e -> p (b t) e")
        gates = mem["gates"]
        ones = sb("ones", [P, P])
        upper = sb("upper", [P, P])
        col = sb("col", [P, NT])
        rcp = sb("rcp", [P, NT])
        rest = sb("rest", [P, NT, E])
        equal = sb("equal", [P, NT, E])
        seen = sb("seen", [P, NT, E])
        first = sb("first", [P, NT, E])
        chosen = sb("chosen", [P, NT, E])
        hit = sb("hit", [P, NT, E])
        count = sb("count", [P, E])
        least = sb("least", [P, E], I32)
        trial = sb("trial", [P, 3, E], I32)
        digit = sb("digit", [P, 3, E])
        digit_i = sb("digit_i", [P, 3, E], I32)
        digit_next = sb("digit_next", [P, 3, E])
        reached = sb("reached", [P, 3, E])
        taken = sb("taken", [P, E], I32)
        hits = sb("hits", [P, 3, NT, E])
        counts = sb("counts", [P, 3, E])
        room = sb("room", [P, E])
        rank = sb("rank", [P, NT, E])
        before = sb("before", [P, NT, E])
        sems = Semaphores(nc, ctx, "gt", "loaded dve_chain to_exp exp_done counted totals")
        loaded, dve_chain, to_exp, exp_done, counted, totals = sems.all
        wide = [P, NT, E]

        with nc.Block() as block:
            @block.sync
            def _(sp):
                sp.dma_start(ones[:], w["ones"]).then_inc(loaded, 16)
                sp.dma_start(upper[:], w["upper"]).then_inc(loaded, 16)
                sp.wait_ge(loaded, 32)

            @block.scalar
            def _(act):
                act.wait_ge(to_exp, 1)
                nc.scalar.activation(prob, prob, ACT.Exp).then_inc(exp_done, 1)

            @block.vector
            def _(dve):
                links = [0]

                def link(ins):
                    links[0] += 1
                    ins.then_inc(dve_chain, 1)
                    dve.wait_ge(dve_chain, links[0])

                link(nc.vector.tensor_reduce(col[:], prob, AX, ALU.max))
                nc.vector.tensor_tensor(prob, prob, col[:, :, None].to_broadcast(wide), ALU.subtract).then_inc(to_exp, 1)
                dve.wait_ge(exp_done, 1)
                link(nc.vector.tensor_reduce(col[:], prob, AX, ALU.add))
                link(nc.vector.reciprocal(rcp[:], col[:]))
                link(nc.vector.tensor_tensor(prob, prob, rcp[:, :, None].to_broadcast(wide), ALU.mult))
                link(nc.vector.memset(seen[:], 0.0))
                for k in range(TOP_K):
                    src = prob if k == 0 else rest[:]
                    dst = chosen if k == 0 else first
                    link(nc.vector.tensor_reduce(col[:], src, AX, ALU.max))
                    link(nc.vector.tensor_tensor(equal[:], src, col[:, :, None].to_broadcast(wide), ALU.is_equal))
                    for e in range(1, E):
                        link(nc.vector.tensor_tensor(seen[:, :, e], seen[:, :, e - 1], equal[:, :, e - 1], ALU.add))
                    link(nc.vector.scalar_tensor_tensor(dst[:], seen[:], 0.0, equal[:], ALU.is_equal, ALU.mult))
                    if k == 0:
                        link(nc.vector.scalar_tensor_tensor(rest[:], chosen[:], -4.0, prob, ALU.mult, ALU.add))
                link(nc.vector.tensor_tensor(chosen[:], chosen[:], first[:], ALU.add))
                link(nc.vector.tensor_tensor(gates[:], prob, chosen[:], ALU.mult))
                link(nc.vector.memset(least[:], 0))
                for k in range(3):
                    link(nc.vector.memset(digit[:, k], float((k + 1) * 2 ** (BITS - 2))))
                link(nc.vector.tensor_copy(trial[:], digit[:]))
        clear(nc, sems.all)

        by_expert = "p n e -> p e n"
        bcast = [P, NT, E]

        with nc.Block() as block:
            @block.tensor
            def _(pe):
                with pe.Fori(0, BITS // 2) as i:
                    pe.wait_ge(counted, i + 1)
                    nc.tensor.matmul(bank[0][:, 0:3 * E], ones[:], counts[:].rearrange("p k e -> p (k e)"), start=True, stop=True).then_inc(totals, 1)

            @block.vector
            def _(dve):
                LINKS = 7
                with dve.Fori(0, BITS // 2) as i:
                    nc.vector.tensor_tensor(hits[:], gates[:, None].to_broadcast([P, 3, NT, E]),
                                            trial[:].bitcast(F32)[:, :, None, :].to_broadcast([P, 3, NT, E]), ALU.is_ge).then_inc(dve_chain, 1)
                    dve.wait_ge(dve_chain, LINKS * i + 1)
                    nc.vector.tensor_reduce(counts[:], hits[:].rearrange("p k n e -> p k e n"), AX, ALU.add).then_inc(counted, 1)
                    nc.vector.tensor_scalar(digit_next[:], digit[:], 0.25, None, ALU.mult).then_inc(dve_chain, 1)
                    dve.wait_ge(dve_chain, LINKS * i + 2)
                    nc.vector.tensor_copy(digit_i[:], digit_next[:]).then_inc(dve_chain, 1)
                    dve.wait_ge(totals, i + 1)
                    nc.vector.scalar_tensor_tensor(reached[:], bank[0][:, 0:3 * E].rearrange("p (k e) -> p k e", e=E), float(CAP), digit[:],
                                                   ALU.is_ge, ALU.mult).then_inc(dve_chain, 1)
                    dve.wait_ge(dve_chain, LINKS * i + 4)
                    nc.vector.tensor_reduce(taken[:], reached[:].rearrange("p k e -> p e k"), AX, ALU.max).then_inc(dve_chain, 1)
                    nc.vector.tensor_copy(digit[:], digit_next[:])
                    dve.wait_ge(dve_chain, LINKS * i + 5)
                    nc.vector.tensor_tensor(least[:], least[:], taken[:], ALU.bitwise_or).then_inc(dve_chain, 1)
                    dve.wait_ge(dve_chain, LINKS * i + 6)
                    nc.vector.tensor_tensor(trial[:], least[:, None].to_broadcast([P, 3, E]), digit_i[:], ALU.bitwise_or).then_inc(dve_chain, 1)
                    dve.wait_ge(dve_chain, LINKS * i + 7)
        clear(nc, sems.all)

        with nc.Block() as block:
            @block.tensor
            def _(pe):
                pe.wait_ge(counted, 1)
                nc.tensor.matmul(bank[0][:, 0:E], ones[:], count[:], start=True, stop=True).then_inc(totals, 1)
                pe.wait_ge(counted, 2)
                flat = equal[:].rearrange("p n e -> p (n e)")
                nc.tensor.matmul(bank[1][:, 0:NT * E], upper[:], flat, start=True, stop=True).then_inc(totals, 1)
                nc.tensor.matmul(bank[2][:, 0:NT * E], ones[:], flat, start=True, stop=True).then_inc(totals, 1)

            @block.vector
            def _(dve):
                links = [0]

                def link(ins):
                    links[0] += 1
                    ins.then_inc(dve_chain, 1)
                    dve.wait_ge(dve_chain, links[0])

                edge = least[:].bitcast(F32)[:, None, :].to_broadcast(bcast)
                link(nc.vector.tensor_tensor(hit[:], gates[:], edge, ALU.is_gt))
                nc.vector.tensor_reduce(count[:], hit[:].rearrange(by_expert), AX, ALU.add).then_inc(counted, 1)
                nc.vector.tensor_tensor(equal[:], gates[:], edge, ALU.is_equal).then_inc(counted, 1)
                dve.wait_ge(totals, 1)
                link(nc.vector.tensor_scalar(room[:], bank[0][:, 0:E], -1.0, float(CAP), ALU.mult, ALU.add))
                link(nc.vector.memset(before[:, 0, :], 0.0))
                dve.wait_ge(totals, 3)
                tiles = bank[2][:, 0:NT * E].rearrange("p (n e) -> p n e", e=E)
                for n in range(1, NT):
                    link(nc.vector.tensor_tensor(before[:, n], before[:, n - 1], tiles[:, n - 1], ALU.add))
                link(nc.vector.tensor_tensor(rank[:], before[:], bank[1][:, 0:NT * E].rearrange("p (n e) -> p n e", e=E), ALU.add))
                link(nc.vector.tensor_tensor(rank[:], rank[:], room[:, None, :].to_broadcast(bcast), ALU.is_lt))
                link(nc.vector.tensor_tensor(rank[:], rank[:], equal[:], ALU.mult))
                link(nc.vector.tensor_tensor(hit[:], hit[:], rank[:], ALU.add))
                link(nc.vector.tensor_tensor(gates[:], gates[:], hit[:], ALU.mult))
        clear(nc, sems.all)


def experts(nc, mem, w):
    with ExitStack() as ctx:
        def sb(name, shape, dt=F32):
            return ctx.enter_context(nc.sbuf_tensor("ex_" + name, shape, dt))

        x_all, bank, moe_inT = mem["x_all"], mem["bank"], mem["moe_inT"]
        NF = FF // P
        w1 = sb("w1", [P, 2, DC, FF])
        w2 = sb("w2", [P, 2, NF, D])
        w1_parts = sb("w1_parts", [P, 2, 2, DC, FF], F32R)
        w2_parts = sb("w2_parts", [P, 2, 2, NF, D], F32R)
        in_parts = sb("in_parts", [P, 2, B, DC, S], F32R)
        h_parts = sb("h_parts", [P, 2, 2, NF, S], F32R)
        gate = sb("gate", [P, 2, NT])
        sems = Semaphores(nc, ctx, "ex", "wload gate_in split_high split_low h_full high_done y_full y_read")
        wload, gate_in, split_high, split_low, h_full, high_done, y_full, y_read = sems.all
        products = ((0, 0), (0, 1), (1, 0))
        jobs = [(k, b) for k in range(2) for b in range(B)]

        def load(sp, pair):
            for k in range(2):
                sp.dma_start(w1[:, k], w["w1"][2 * pair + k].rearrange("(c p) n -> p c n", p=P)).then_inc(wload, 16)
                sp.dma_start(w2[:, k], w["w2"][2 * pair + k].rearrange("(c p) n -> p c n", p=P)).then_inc(wload, 16)

        with nc.Block() as block:
            @block.sync
            def _(sp):
                load(sp, 0)

            @block.scalar
            def _(act):
                for b in range(B):
                    nc.scalar.copy(in_parts[:, 0, b], moe_inT[:, b]).then_inc(split_high, 1)

            @block.vector
            def _(dve):
                for b in range(B):
                    dve.wait_ge(split_high, b + 1)
                    nc.vector.tensor_tensor(in_parts[:, 1, b], moe_inT[:, b], in_parts[:, 0, b], ALU.subtract).then_inc(split_low, 1)
                dve.wait_ge(split_low, B)
        gating(nc, mem, w)
        with nc.Block() as block:
            @block.sync
            def _(sp):
                sp.wait_ge(wload, 16 * 4)
        clear(nc, sems.all)

        order = [("split", 0), ("split", 1)]
        for m in range(len(jobs) + 1):
            if m < len(jobs):
                order += [("part", NF * m + f) for f in range(NF)]
            if m == 0:
                order += [("split", 2), ("split", 3)]
            if m >= 1:
                order += [("add", T * (m - 1) + t) for t in range(T)]
        reads = {step: i + 1 for i, step in enumerate([step for step in order if step[0] != "split"])}

        def body(pair, last):
            with nc.Block() as block:
                @block.sync
                def _(sp):
                    if not last:
                        sp.wait_ge(split_low, 4)
                        load(sp, pair + 1)
                        sp.wait_ge(wload, 16 * 4)

                @block.tensor
                def _(pe):
                    def second(m):
                        k, b = jobs[m]
                        pe.wait_ge(split_low, 2 * k + 2)
                        pe.wait_ge(y_read, reads["part", NF * m + NF - 1])
                        for t in range(T):
                            n = T * m + t
                            if n >= 4:
                                pe.wait_ge(y_read, reads["add", n - 4])
                            for f in range(NF):
                                for i, j in products:
                                    mm = nc.tensor.matmul(bank[4 + n % 4][:, 0:D], h_parts[:, m % 2, i, f, t * P:(t + 1) * P], w2_parts[:, k, j, f, :],
                                                          start=(f == 0 and i + j == 0), stop=(f == NF - 1 and i == 1))
                            mm.then_inc(y_full, 1)

                    for m, (k, b) in enumerate(jobs):
                        pe.wait_ge(split_low, 2 * k + 1)
                        for f in range(NF):
                            n = NF * m + f
                            if n >= 4:
                                pe.wait_ge(y_read, reads["part", n - 4])
                            for d in range(DC):
                                for i, j in products:
                                    mm = nc.tensor.matmul(bank[n % 4][:], w1_parts[:, k, i, d, f * P:(f + 1) * P], in_parts[:, j, b, d, :],
                                                          start=(d == 0 and i + j == 0), stop=(d == DC - 1 and i == 1))
                            mm.then_inc(h_full, 1)
                        if m >= 1:
                            second(m - 1)
                    second(len(jobs) - 1)

                @block.scalar
                def _(act):
                    for kind, n in order:
                        if kind == "split":
                            src, dst = ((w1, w1_parts), (w2, w2_parts))[n % 2]
                            nc.scalar.copy(dst[:, n // 2, 0], src[:, n // 2]).then_inc(split_high, 1)
                        elif kind == "part":
                            m = n // NF
                            act.wait_ge(h_full, n + 1)
                            if m >= 2:
                                act.wait_ge(y_full, T * (m - 1))
                            nc.scalar.activation(h_parts[:, m % 2, 0, n % NF], bank[n % 4][:], ACT.Relu).then_inc(high_done, 1)

                @block.vector
                def _(dve):
                    for k in range(2):
                        nc.vector.tensor_copy(gate[:, k, :, None], mem["gates"][:, :, bass.ds(2 * pair + k, 1)]).then_inc(gate_in, 1)
                    dve.wait_ge(gate_in, 2)
                    for kind, n in order:
                        if kind == "split":
                            src, dst = ((w1, w1_parts), (w2, w2_parts))[n % 2]
                            dve.wait_ge(split_high, n + 1)
                            nc.vector.tensor_tensor(dst[:, n // 2, 1], src[:, n // 2], dst[:, n // 2, 0], ALU.subtract).then_inc(split_low, 1)
                        elif kind == "part":
                            m = n // NF
                            dve.wait_ge(high_done, n + 1)
                            nc.vector.scalar_tensor_tensor(h_parts[:, m % 2, 1, n % NF], bank[n % 4][:], 0.0, h_parts[:, m % 2, 0, n % NF],
                                                           ALU.max, ALU.subtract).then_inc(y_read, 1)
                        else:
                            (k, b), t = jobs[n // T], n % T
                            dve.wait_ge(y_full, n + 1)
                            xs = x_all[:, b, t * D:(t + 1) * D]
                            nc.vector.scalar_tensor_tensor(xs, bank[4 + n % 4][:, 0:D], gate[:, k, b * T + t:b * T + t + 1], xs,
                                                           ALU.mult, ALU.add).then_inc(y_read, 1)
                    dve.wait_ge(y_read, len(reads))
            clear(nc, sems.all)

        with nc.Fori(0, E // 2 - 1) as pair:
            body(pair, False)
        body(E // 2 - 1, True)



MH = 8
MD = D // MH


def memory_attention(nc, mem, w):
    with ExitStack() as ctx:
        def sb(name, shape, dt=F32):
            return ctx.enter_context(nc.sbuf_tensor("ma_" + name, shape, dt))

        x_all, ident, bank = mem["x_all"], mem["ident"], mem["bank"]
        stats = sb("stats", [P, NT, 6])
        mv = sb("mv", [P, NT, 2])
        rstd = sb("rstd", [P, NT])
        minus_half = sb("minus_half", [P, NT])
        xn = sb("xn", [P, B, T * D])
        context = sb("context", [P, B, CTX])
        mask_i = sb("mask_i", [P, B, M], I32)
        mask = sb("mask", [P, B, M])
        bias = sb("bias", [P, 1])
        xn_b = sb("xn_b", [P, T * D])
        context_b = sb("context_b", [P, CTX])
        qT = sb("qT", [P, DC, S])
        kT = sb("kT", [P, DC, M])
        smax = sb("smax", [P, MH])
        rsum = sb("rsum", [P, 2, MH])
        prob = sb("prob", [P, 3, MH * M])
        probT = sb("probT", [P, 2, MH * M])
        sems = Semaphores(nc, ctx, "ma", "loaded masked chain pow_chain scaled staged xt_full xt_read s_full s_read exp_in exp_done summed normed "
                          "tr_full tr_read o_full o_read dve_chain")
        (loaded, masked, chain, pow_chain, scaled, staged, xt_full, xt_read, s_full, s_read, exp_in, exp_done, summed, normed,
         tr_full, tr_read, o_full, o_read, dve_chain) = sems.all
        R = P // MD

        with nc.Block() as block:
            @block.sync
            def _(sp):
                for half in range(2):
                    sp.dma_start(context[half * M:(half + 1) * M], w["ctx"].rearrange("b m d -> m b d")).then_inc(loaded, 16)
                for b in range(B):
                    sp.dma_start(mask_i[:, b], w["mask"][b, None, :].to_broadcast([P, M])).then_inc(loaded, 16)
                sp.dma_start(bias[:], w["b"][None, :].to_broadcast([P, 1])).then_inc(loaded, 16)
                sp.wait_ge(loaded, 16 * (B + 3))

            @block.gpsimd
            def _(pool):
                nc.gpsimd.memset(minus_half[:], -0.5).then_inc(pow_chain, 1)
                pool.wait_ge(pow_chain, 1)
                pool.wait_ge(chain, 2 * NT + 1)
                nc.gpsimd.tensor_tensor(rstd[:], rstd[:], minus_half[:], ALU.pow).then_inc(pow_chain, 1)
                pool.wait_ge(pow_chain, 2)

            @block.vector
            def _(dve):
                def tile(y, n):
                    return y[:, n // T, n % T * D:(n % T + 1) * D]

                for n in range(NT):
                    nc.vector.bn_stats(stats[:, n], tile(x_all, n)).then_inc(chain, 1)
                for n in range(NT):
                    dve.wait_ge(chain, n + 1)
                    nc.vector.bn_aggr(mv[:, n], stats[:, n]).then_inc(chain, 1)
                dve.wait_ge(chain, 2 * NT)
                nc.vector.tensor_scalar(rstd[:], mv[:, :, 1], 1e-5, None, ALU.add).then_inc(chain, 1)
                dve.wait_ge(loaded, 16 * (B + 3))
                nc.vector.tensor_copy(mask[:], mask_i[:]).then_inc(masked, 1)
                dve.wait_ge(masked, 1)
                nc.vector.tensor_scalar(mask[:], mask[:], -1.0, 1.0, ALU.mult, ALU.add).then_inc(masked, 1)
                dve.wait_ge(masked, 2)
                nc.vector.tensor_scalar(mask[:], mask[:], NEG, None, ALU.mult).then_inc(masked, 1)
                dve.wait_ge(masked, 3)
                dve.wait_ge(pow_chain, 2)
                for n in range(NT):
                    nc.vector.tensor_scalar(tile(xn, n), tile(x_all, n), mv[:, n, 0:1], rstd[:, n:n + 1], ALU.subtract, ALU.mult).then_inc(scaled, 1)
                dve.wait_ge(scaled, NT)
        clear(nc, sems.all)

        order = []
        for k in range(T + 2):
            for kind, t in (("norm", k - 1), ("scores", k), ("exp", k), ("values", k - 2), ("probT", k - 1)):
                if 0 <= t < T:
                    order.append((kind, t))

        with nc.Fori(0, B) as b:
            with nc.Block() as block:
                @block.tensor
                def _(pe):
                    pe.wait_ge(staged, 2)
                    for d in range(DC):
                        for t in range(T):
                            mm = nc.tensor.transpose(bank[d][:, t * P:(t + 1) * P], xn_b[:, t * D + d * P:t * D + (d + 1) * P], ident[:])
                        mm.then_inc(xt_full, 1)
                    for d in range(DC):
                        mm = nc.tensor.transpose(bank[2][:, d * M:(d + 1) * M], context_b[0:M, d * P:(d + 1) * P], ident[0:M, 0:M])
                    mm.then_inc(xt_full, 1)
                    pe.wait_ge(xt_read, DC + 1)
                    for kind, t in order:
                        if kind == "scores":
                            if t >= 1:
                                pe.wait_ge(s_read, t)
                            for c in range(DC):
                                for odd in range(2):
                                    for r in range(R):
                                        q0 = DH * ((r + odd) % 2)
                                        mm = nc.tensor.matmul(bank[r][q0:q0 + DH, c * M:(c + 1) * M], qT[r * MD:(r + 1) * MD, c, t * P + q0:t * P + q0 + DH],
                                                              kT[r * MD:(r + 1) * MD, c, :], start=True, stop=True, skip_group_check=True)
                            mm.then_inc(s_full, 1)
                        elif kind == "probT":
                            pe.wait_ge(normed, t + 1)
                            if t >= 1:
                                pe.wait_ge(tr_read, t)
                            for r in range(R):
                                mm = nc.tensor.transpose(bank[4][:, r * P:(r + 1) * P], prob[:, t % 3, r * P:(r + 1) * P], ident[:])
                            mm.then_inc(tr_full, 1)
                        elif kind == "values":
                            pe.wait_ge(tr_read, t + 1)
                            if t >= 1:
                                pe.wait_ge(o_read, t)
                            for r in range(R):
                                for odd in range(2):
                                    for c in range(DC):
                                        at, q0 = D + (R * c + r) * MD, DH * (odd ^ c)
                                        mm = nc.tensor.matmul(bank[5 + c][q0:q0 + DH, r * MD:(r + 1) * MD],
                                                              probT[c * M:(c + 1) * M, t % 2, r * P + q0:r * P + q0 + DH],
                                                              context_b[c * M:(c + 1) * M, at:at + MD], start=True, stop=True, skip_group_check=True)
                            mm.then_inc(o_full, 1)

                @block.scalar
                def _(act):
                    nc.scalar.copy(context_b[:], context[:, b]).then_inc(staged, 1)
                    for d in range(DC):
                        act.wait_ge(xt_full, d + 1)
                        nc.scalar.mul(qT[:, d, :], bank[d][:], MD ** -0.5).then_inc(xt_read, 1)
                    act.wait_ge(xt_full, DC + 1)
                    nc.scalar.copy(kT[:].rearrange("p c m -> p (c m)"), bank[2][:, 0:DC * M]).then_inc(xt_read, 1)
                    for kind, t in order:
                        if kind == "exp":
                            act.wait_ge(exp_in, t + 1)
                            nc.scalar.activation(prob[:, t % 3], prob[:, t % 3], ACT.Exp).then_inc(exp_done, 1)
                        elif kind == "probT":
                            act.wait_ge(tr_full, t + 1)
                            if t >= 2:
                                act.wait_ge(o_full, t - 1)
                            nc.scalar.copy(probT[:, t % 2], bank[4][:]).then_inc(tr_read, 1)

                @block.gpsimd
                def _(pool):
                    for t in range(T):
                        pool.wait_ge(summed, t + 1)
                        p8 = prob[:, t % 3].rearrange("p (h m) -> p h m", m=M)
                        nc.gpsimd.tensor_tensor(p8, p8, rsum[:, t % 2, :, None].to_broadcast([P, MH, M]), ALU.mult).then_inc(normed, 1)

                @block.vector
                def _(dve):
                    links = [0]

                    def link(ins):
                        links[0] += 1
                        ins.then_inc(dve_chain, 1)
                        dve.wait_ge(dve_chain, links[0])

                    nc.vector.tensor_copy(xn_b[:], xn[:, b]).then_inc(staged, 1)
                    for kind, t in order:
                        p8 = prob[:, t % 3].rearrange("p (h m) -> p h m", m=M)
                        if kind == "scores":
                            dve.wait_ge(s_full, t + 1)
                            if t >= 3:
                                dve.wait_ge(tr_full, t - 2)
                            for r in range(R):
                                s3 = bank[r][:, 0:DC * M].rearrange("p (c m) -> p c m", m=M)
                                p3 = prob[:, t % 3, r * P:(r + 1) * P].rearrange("p (c m) -> p c m", m=M)
                                op = nc.vector.scalar_tensor_tensor(p3, s3, bias[:, 0:1], mask[:, b, None, :].to_broadcast([P, DC, M]), ALU.add, ALU.add)
                            op.then_inc(s_read, 1)
                            dve.wait_ge(s_read, t + 1)
                            link(nc.vector.tensor_reduce(smax[:], p8, AX, ALU.max))
                            nc.vector.tensor_tensor(p8, p8, smax[:, :, None].to_broadcast([P, MH, M]), ALU.subtract).then_inc(exp_in, 1)
                        elif kind == "norm":
                            dve.wait_ge(exp_done, t + 1)
                            if t >= 2:
                                dve.wait_ge(normed, t - 1)
                            link(nc.vector.tensor_reduce(rsum[:, t % 2], p8, AX, ALU.add))
                            nc.vector.reciprocal(rsum[:, t % 2], rsum[:, t % 2]).then_inc(summed, 1)
                        elif kind == "values":
                            dve.wait_ge(o_full, t + 1)
                            for c in range(DC):
                                xs = x_all[:, b, t * D + c * P:t * D + (c + 1) * P]
                                op = nc.vector.tensor_tensor(xs, xs, bank[5 + c][:, 0:P], ALU.add)
                            op.then_inc(o_read, 1)
                    dve.wait_ge(o_read, T)
            clear(nc, sems.all)




NB = 2
NTL = NB * T
PAIR = 2 * P


STEPS = {"X": "xT", "c": "chunk", "n": "norm", "t": "turn", "q": "qk", "s": "scores", "d": "divide", "p": "probT", "v": "values",
         "P": "project", "S": "shift", "N": "xn", "T": "xnT", "g": "ga", "f": "ffn"}
ORDER = """
    XccnnccccttnnqcqttcnqnqssttcdccqqncpdncdpctnvtcnqtcndqtcncqpcptqtnsvqqsdcdcncPcptntnpcqqddXsSdpctpvNtcpdvqnsnpTPtcdqSc
    ncptNvcqnTtsqdqddgcgtgnpcvqptcnsqpdndgPgtsSdqNcpncpccvtctgTqncptqnvdtnfspqdsdcPtpdncpsqSdctNvcnqpcvtcqdpfTdnPnsdpgvpsp
    tdSdcvNccnPqqgptgqdggptgSqNTvpsvdfsdPpTdfpgpdggSNvpggvgPTSNfTfggggggff
"""


def layer_order():
    seen, order = dict.fromkeys(STEPS, 0), []
    for letter in "".join(ORDER.split()):
        order.append((STEPS[letter], seen[letter]))
        seen[letter] += 1
    per_tile = {"c": 6, "n": 4, "t": 4, "q": 4, "s": GROUP // 2, "d": GROUP, "p": GROUP, "v": GROUP // 2, "P": 1, "S": 1, "N": 1, "T": 1, "f": 1}
    assert all(seen[k] == n * NTL for k, n in per_tile.items()) and seen["X"] == NB and seen["g"] == FC * NTL // 2
    return order


def local_layers(nc, mem, w):
    with ExitStack() as ctx:
        def sb(name, shape, dt=F32):
            return ctx.enter_context(nc.sbuf_tensor("l1_" + name, shape, dt))

        x_all, ident, ident_bf, bank = mem["x_all"], mem["ident"], mem["ident_bf"], mem["bank"]
        wqkv = sb("wqkv", [P, DC, 3 * INNER])
        wo = sb("wo", [P, INNER // P, D])
        w1 = sb("w1", [P, DC, 2 * FI])
        w2 = sb("w2", [P, FC, D])
        cols = sb("cols", [P, 2 * FC + 2 * DC])
        b1 = cols[:, 0:2 * FC].rearrange("p (k c) -> p k c", k=2)
        ln_g = cols[:, 2 * FC:2 * FC + DC]
        ln_b = cols[:, 2 * FC + DC:2 * FC + 2 * DC]
        scale_qk = sb("scale_qk", [P, 2, DH])
        rope = sb("rope", [P, 4, T, DH])
        turn = sb("turn", [P, 4, T, DH])
        shift = sb("shift", [P, 2, P])
        mask = sb("mask", [P, 2, P])
        mask_bf = sb("mask_bf", [P, 2, P], BF16)
        x = sb("x", [P, NB * T, D])
        xT = sb("xT", [P, DC, S + 1])
        sq = sb("sq", [P, S])
        norm = sb("norm", [P, 2, 8])
        minus_half = sb("minus_half", [P, 8])
        qn = sb("qn", [P, 2, S])
        rot = sb("rot", [P, 2, S])
        cosd = sb("cosd", [P, 2, S])
        qr = sb("qr", [P, 2, S])
        qT = sb("qT", [P, INNER // P, S])
        kT = sb("kT", [P, INNER // P, S])
        v_odd = sb("v_odd", [P, T, HEADS, DH])
        v_even = sb("v_even", [P, T, HEADS, DH])
        smax = sb("smax", [P, 2, GROUP])
        prob = sb("prob", [P, 4, GROUP * P])
        probT = sb("probT", [P, 4, GROUP * P])
        rsum = sb("rsum", [P, 2, GROUP])
        oT = sb("oT", [P, 2, INNER])
        stats = sb("stats", [P, 2, 2, 6])
        mv = sb("mv", [P, 2, 2])
        rstd = sb("rstd", [P, 2])
        xn = sb("xn", [P, 2, D])
        xnT = sb("xnT", [P, DC, PAIR])
        gate = sb("gate", [P, 2, PAIR])
        x_kept = sb("x_kept", [P, P])
        h = sb("h", [P, FC, PAIR])

        names = ("table setup back xin xt_full xt_read chunk_full sq_done ss_done norm_done qn_done rot_done qr_done v_read "
                 "tr_full tr_read s_full s_read exp_done div_done o_full o_read x_done sh_full mv_done rstd_done xn_done ga_full gelu_done h_done "
                 "kept dve_chain pow_chain")
        sems = Semaphores(nc, ctx, "l1", names)
        (table, setup, back, xin, xt_full, xt_read, chunk_full, sq_done, ss_done, norm_done, qn_done, rot_done, qr_done,
         v_read, tr_full, tr_read, s_full, s_read, exp_done, div_done, o_full, o_read, x_done, sh_full, mv_done, rstd_done, xn_done, ga_full,
         gelu_done, h_done, kept, dve_chain, pow_chain) = sems.all

        weight_sems = Semaphores(nc, ctx, "l1w", "q_in k_in v_in rest_in")
        qkv_in, rest_in = weight_sems.all[0:3], weight_sems.all[3]

        with nc.Block() as block:
            @block.sync
            def _(sp):
                sp.dma_start(rope[:], w["rope1"].rearrange("k (t p) d -> p k t d", p=P)).then_inc(table, 16)
                sp.dma_start(shift[:], w["shift"].rearrange("k p q -> p k q")).then_inc(table, 16)
                sp.dma_start(mask[:], w["win_mask"].rearrange("k p q -> p k q")).then_inc(table, 16)

            @block.gpsimd
            def _(pool):
                nc.gpsimd.memset(v_odd[:], 0.0).then_inc(setup, 1)
                nc.gpsimd.memset(v_even[:], 0.0).then_inc(setup, 1)
                nc.gpsimd.memset(xT[:, 1, 0:1], 0.0).then_inc(setup, 1)
                nc.gpsimd.memset(minus_half[:], -0.5).then_inc(setup, 1)

            @block.vector
            def _(dve):
                nc.vector.memset(h[32:64, FC - 1, :], 1.0).then_inc(setup, 1)
                dve.wait_ge(table, 48)
                for k in range(2):
                    nc.vector.tensor_copy(mask_bf[:, k], mask[:, k]).then_inc(setup, 1)
                dve.wait_ge(setup, 7)
        clear(nc, sems.all)

        order = layer_order()
        keeps = [t for t in range(1, NTL, 2) if t % T < T - 1]
        big_turn, released, tr_turn, out_turn, out_read, x_turn = {}, [], {}, {}, [], {}
        for kind, n in order:
            if kind == "xT":
                for d in range(DC):
                    big_turn["xT", DC * n + d] = len(released)
                    released.append((xt_read, DC * n + d + 1))
            elif kind == "chunk":
                t, c = n // 6, n % 6
                big_turn[kind, n] = len(released)
                released.append((qn_done, 4 * t + c + 1) if c < 4 else (v_read, 2 * t + c - 3))
            elif kind == "scores":
                for g in (2 * n, 2 * n + 1):
                    big_turn[kind, g] = len(released)
                    released.append((s_read, g + 1))
            elif kind in ("shift", "ga"):
                big_turn[kind, n] = len(released)
                released.append((xn_done if kind == "shift" else h_done, n + 1))
            elif kind in ("qk", "probT", "xnT"):
                tr_turn[kind, n] = len(tr_turn)
            if kind in ("values", "project", "ffn"):
                out_turn[kind, n] = len(out_turn)
                if kind == "values":
                    out_read.append((o_read, n + 1))
                else:
                    x_turn[kind, n] = len(x_turn)
                    out_read.append((x_done, len(x_turn)))

        def chunk_at(m):
            return big_turn["chunk", 6 * (m // 4) + m % 4]

        with nc.Fori(0, DEPTH) as layer:
            clear(nc, weight_sems.all)
            with nc.Block() as block:
                @block.sync
                def _(sp):
                    for s in range(2):
                        sp.dma_start(scale_qk[:, s], w["qk_scale"][s][layer, None, :].to_broadcast([P, DH])).then_inc(table, 16)
                    for part, arrived in enumerate(qkv_in):
                        cut = slice(part * INNER, (part + 1) * INNER)
                        sp.dma_start(wqkv[:, :, cut], w["Wqkv"][layer].rearrange("(c p) n -> p c n", p=P)[:, :, cut]).then_inc(arrived, 16)
                    sp.dma_start(wo[:], w["Wo"][layer].rearrange("(c p) n -> p c n", p=P)).then_inc(rest_in, 16)
                    sp.dma_start(cols[:], w["cols"][layer]).then_inc(rest_in, 16)
                    sp.dma_start(w1[:], w["W1"][layer].rearrange("(c p) n -> p c n", p=P)).then_inc(rest_in, 16)
                    sp.dma_start(w2[:, 0:FC - 1], w["W2"][layer][0:(FC - 1) * P].rearrange("(c p) n -> p c n", p=P)).then_inc(rest_in, 16)
                    sp.dma_start(w2[0:FR, FC - 1], w["W2"][layer][(FC - 1) * P:FI]).then_inc(rest_in, 16)
                    sp.dma_start(w2[FR:FR + 1, FC - 1], w["b2"][layer, None, :]).then_inc(rest_in, 16)

                @block.vector
                def _(dve):
                    dve.wait_ge(table, 32)
                    for s in range(2):
                        sc = scale_qk[:, s]
                        nc.vector.tensor_tensor(turn[:, 2 * s], rope[:, 2 * s], sc[:, None, :].to_broadcast([P, T, DH]), ALU.mult).then_inc(back, 1)
                        nc.vector.tensor_tensor(turn[:, 2 * s + 1, :, 0:HALF], rope[:, 2 * s + 1, :, 0:HALF],
                                                sc[:, None, HALF:DH].to_broadcast([P, T, HALF]), ALU.mult).then_inc(back, 1)
                        nc.vector.tensor_tensor(turn[:, 2 * s + 1, :, HALF:DH], rope[:, 2 * s + 1, :, HALF:DH],
                                                sc[:, None, 0:HALF].to_broadcast([P, T, HALF]), ALU.mult).then_inc(back, 1)
                    dve.wait_ge(back, 6)
            clear(nc, sems.all)

            with nc.Fori(0, B // NB) as part:
                with nc.Block() as block:
                    @block.tensor
                    def _(pe):
                        def shared_bank(turn):
                            if turn >= 4:
                                pe.wait_ge(*released[turn - 4])
                            return bank[turn % 4]

                        def transposed_bank(turn):
                            if turn >= 2:
                                pe.wait_ge(tr_read, turn - 1)
                            return bank[4 + turn % 2]

                        def output_bank(turn):
                            if turn >= 2:
                                pe.wait_ge(*out_read[turn - 2])
                            return bank[6 + turn % 2]

                        pe.wait_ge(xin, 1)
                        for kind, n in order:
                            if kind == "xT":
                                for d in range(DC):
                                    dst = shared_bank(big_turn[kind, DC * n + d])
                                    for t in range(T):
                                        mm = nc.tensor.transpose(dst[:, t * P:(t + 1) * P], x[:, T * n + t, d * P:(d + 1) * P], ident[:])
                                    mm.then_inc(xt_full, 1)
                            elif kind == "chunk":
                                t, c = n // 6, n % 6
                                if n % (6 * T) == 0:
                                    pe.wait_ge(xt_read, DC * (t // T + 1))
                                if t == 0 and c % 2 == 0:
                                    pe.wait_ge(qkv_in[c // 2], 16)
                                dst = shared_bank(big_turn[kind, n])
                                for d in range(DC):
                                    mm = nc.tensor.matmul(dst, xT[:, d, (t % T) * P:(t % T + 1) * P], wqkv[:, d, c * S:(c + 1) * S],
                                                          start=(d == 0), stop=(d == DC - 1))
                                mm.then_inc(chunk_full, 1)
                            elif kind == "qk":
                                pe.wait_ge(qr_done, n + 1)
                                dst = transposed_bank(tr_turn[kind, n])
                                for j in range(4):
                                    mm = nc.tensor.transpose(dst[:, j * P:(j + 1) * P], qr[:, n % 2, j * P:(j + 1) * P], ident[:])
                                mm.then_inc(tr_full, 1)
                            elif kind == "scores":
                                t, hg = 2 * n // GROUP, 2 * n % GROUP
                                pe.wait_ge(tr_read, tr_turn["qk", 4 * t + 3] + 1)
                                both = [shared_bank(big_turn[kind, 2 * n + k]) for k in range(2)]
                                for s in both:
                                    nc.tensor.matmul(s.rearrange("p (g q) -> p g q", g=GROUP), ident_bf[:],
                                                     mask_bf[:, 0 if t % T == 0 else 1, None, :].to_broadcast([P, GROUP, P]),
                                                     start=True, stop=False, skip_group_check=True)
                                for j in range(GROUP):
                                    c = GROUP * (hg // 2) + j
                                    for odd in range(2):
                                        for k in range(2):
                                            half = odd ^ k
                                            r, q0 = DH * k, (t % T) * P + half * WIN
                                            before = WIN if q0 > 0 else 0
                                            mm = nc.tensor.matmul(both[k][half * WIN:(half + 1) * WIN, j * P + WIN - before:(j + 1) * P],
                                                                  qT[r:r + DH, c, q0:q0 + WIN], kT[r:r + DH, c, q0 - before:q0 + WIN],
                                                                  start=False, stop=(j == GROUP - 1 and odd == 1), skip_group_check=True)
                                            if j == GROUP - 1 and odd == 1:
                                                mm.then_inc(s_full, 1)
                            elif kind == "probT":
                                pe.wait_ge(div_done, n + 1)
                                dst = transposed_bank(tr_turn[kind, n])
                                for j in range(4):
                                    mm = nc.tensor.transpose(dst[:, j * P:(j + 1) * P], prob[:, n % 4, j * P:(j + 1) * P], ident[:])
                                mm.then_inc(tr_full, 1)
                            elif kind == "values":
                                t, c0 = n // 2, GROUP * (n % 2)
                                pe.wait_ge(tr_read, tr_turn["probT", 2 * n + 1] + 1)
                                pe.wait_ge(v_read, 2 * t + 2)
                                dst = output_bank(out_turn[kind, n])
                                for j in range(GROUP):
                                    for half, v in ((0, v_even), (1, v_odd)):
                                        for k in range(2):
                                            q0 = j * P + half * WIN
                                            mm = nc.tensor.matmul(dst[k * DH:(k + 1) * DH, q0:q0 + WIN], v[:, t % T, 2 * (c0 + j) + k, :],
                                                                  probT[:, (2 * n + k) % 4, q0:q0 + WIN], start=True, stop=True, skip_group_check=True)
                                mm.then_inc(o_full, 1)
                            elif kind == "project":
                                if n == 0:
                                    pe.wait_ge(rest_in, 16 * 6)
                                pe.wait_ge(o_read, 2 * n + 2)
                                dst = output_bank(out_turn[kind, n])
                                for c in range(INNER // P):
                                    mm = nc.tensor.matmul(dst[:, 0:D], oT[:, n % 2, c * P:(c + 1) * P], wo[:, c, :], start=(c == 0), stop=(c == INNER // P - 1))
                                mm.then_inc(o_full, 1)
                            elif kind == "shift":
                                pe.wait_ge(x_done, x_turn["project", n] + 1)
                                dst = shared_bank(big_turn[kind, n])
                                mm = nc.tensor.matmul(dst[:, 0:P], shift[:, 0], x[:, n, P:D], start=True, stop=(n % T == 0))
                                if n % T > 0:
                                    before = x[:, n - 1, P:D] if n % 2 else x_kept[:]
                                    if n % 2 == 0:
                                        pe.wait_ge(kept, keeps.index(n - 1) + 1)
                                    mm = nc.tensor.matmul(dst[:, 0:P], shift[:, 1], before, start=False, stop=True)
                                mm.then_inc(sh_full, 1)
                            elif kind == "xnT":
                                pe.wait_ge(xn_done, n + 1)
                                dst = transposed_bank(tr_turn[kind, n])
                                for d in range(DC):
                                    mm = nc.tensor.transpose(dst[:, d * P:(d + 1) * P], xn[:, n % 2, d * P:(d + 1) * P], ident[:])
                                mm.then_inc(tr_full, 1)
                            elif kind == "ga":
                                p, i = n // FC, n % FC
                                rows_out = P if i < FC - 1 else FR
                                if i == 0:
                                    pe.wait_ge(tr_read, tr_turn["xnT", 2 * p + 1] + 1)
                                dst = shared_bank(big_turn[kind, n])
                                for k, at in ((1, FI), (0, 0)):
                                    for d in range(DC):
                                        mm = nc.tensor.matmul(dst[0:rows_out, k * PAIR:(k + 1) * PAIR], w1[:, d, at + i * P:at + i * P + rows_out],
                                                              xnT[:, d, :], start=(d == 0), stop=(d == DC - 1), skip_group_check=True)
                                mm.then_inc(ga_full, 1)
                            elif kind == "ffn":
                                pe.wait_ge(h_done, FC * (n // 2 + 1))
                                dst = output_bank(out_turn[kind, n])
                                for i in range(FC):
                                    rows_in = P if i < FC - 1 else FR + 1
                                    mm = nc.tensor.matmul(dst[:, 0:D], h[0:rows_in, i, (n % 2) * P:(n % 2 + 1) * P], w2[0:rows_in, i, :],
                                                          start=(i == 0), stop=(i == FC - 1))
                                mm.then_inc(o_full, 1)

                    @block.scalar
                    def _(act):
                        for kind, n in order:
                            if kind == "xT":
                                if n > 0:
                                    act.wait_ge(chunk_full, 6 * T * n)
                                for d in range(DC):
                                    act.wait_ge(xt_full, DC * n + d + 1)
                                    nc.scalar.copy(xT[:, d, d:d + S], bank[big_turn[kind, DC * n + d] % 4]).then_inc(xt_read, 1)
                            elif kind == "chunk":
                                t, c = n // 6, n % 6
                                act.wait_ge(chunk_full, n + 1)
                                src = bank[big_turn[kind, n] % 4]
                                if c < 4:
                                    m = 4 * t + c
                                    if m >= 1:
                                        act.wait_ge(ss_done, m)
                                    nc.scalar.activation(sq[:], src, ACT.Square).then_inc(sq_done, 1)
                                else:
                                    s3 = src.rearrange("p (h d) -> p h d", h=8)
                                    hs = slice(8 * (c - 4), 8 * (c - 3))
                                    if t >= T:
                                        act.wait_ge(o_full, out_turn["values", 2 * (t - T) + 1] + 1)
                                        if t % T < T - 1:
                                            act.wait_ge(o_full, out_turn["values", 2 * (t - T + 1) + 1] + 1)
                                    nc.scalar.copy(v_even[WIN:P, t % T, hs, 0:DH], s3[0:WIN])
                                    if t % T < T - 1:
                                        nc.scalar.copy(v_even[0:WIN, t % T + 1, hs, 0:DH], s3[WIN:P])
                                    nc.scalar.copy(v_odd[:, t % T, hs, 0:DH], s3).then_inc(v_read, 1)
                            elif kind == "qk":
                                t, c = n // 4, n % 4
                                u = tr_turn[kind, n]
                                act.wait_ge(tr_full, u + 1)
                                if t >= T:
                                    last = GROUP * (t - T + (2 if t % T < T - 1 else 1))
                                    act.wait_ge(s_full, last)
                                dst = qT if c < 2 else kT
                                nc.scalar.copy(dst[:, 4 * (c % 2):4 * (c % 2) + 4, (t % T) * P:(t % T + 1) * P],
                                               bank[4 + u % 2].rearrange("p (c q) -> p c q", c=4)).then_inc(tr_read, 1)
                            elif kind == "scores":
                                for g in (2 * n, 2 * n + 1):
                                    act.wait_ge(s_read, g + 1)
                                    nc.scalar.activation(prob[:, g % 4], prob[:, g % 4], ACT.Exp, scale=QK_SCALE).then_inc(exp_done, 1)
                            elif kind == "probT":
                                u = tr_turn[kind, n]
                                act.wait_ge(tr_full, u + 1)
                                if n >= 4:
                                    act.wait_ge(o_full, out_turn["values", n // 2 - 2] + 1)
                                nc.scalar.copy(probT[:, n % 4], bank[4 + u % 2]).then_inc(tr_read, 1)
                            elif kind == "values":
                                u = out_turn[kind, n]
                                act.wait_ge(o_full, u + 1)
                                if n >= 4:
                                    act.wait_ge(o_full, out_turn["project", n // 2 - 2] + 1)
                                nc.scalar.copy(oT[:, n // 2 % 2, (n % 2) * S:(n % 2 + 1) * S], bank[6 + u % 2]).then_inc(o_read, 1)
                            elif kind == "shift" and n in keeps:
                                act.wait_ge(x_done, x_turn["project", n] + 1)
                                if n > keeps[0]:
                                    act.wait_ge(sh_full, keeps[keeps.index(n) - 1] + 2)
                                nc.scalar.copy(x_kept[:], x[:, n, P:D]).then_inc(kept, 1)
                            elif kind == "xnT":
                                u = tr_turn[kind, n]
                                act.wait_ge(tr_full, u + 1)
                                if n == 0:
                                    act.wait_ge(rest_in, 16 * 6)
                                if n >= 2:
                                    act.wait_ge(ga_full, FC * (n // 2))
                                for d in range(DC):
                                    cp = nc.scalar.activation(xnT[:, d, (n % 2) * P:(n % 2 + 1) * P], bank[4 + u % 2][:, d * P:(d + 1) * P],
                                                              ACT.Identity, bias=ln_b[:, d:d + 1], scale=ln_g[:, d:d + 1])
                                cp.then_inc(tr_read, 1)
                            elif kind == "ga":
                                i = n % FC
                                rows_out = P if i < FC - 1 else FR
                                act.wait_ge(ga_full, n + 1)
                                if n >= 2:
                                    act.wait_ge(h_done, n - 1)
                                nc.scalar.activation(gate[0:rows_out, n % 2], bank[big_turn[kind, n] % 4][0:rows_out, PAIR:2 * PAIR], ACT.Gelu,
                                                     bias=b1[0:rows_out, 1, i:i + 1]).then_inc(gelu_done, 1)

                    @block.gpsimd
                    def _(pool):
                        powers = 0
                        for kind, n in order:
                            if kind == "chunk" and n % 6 < 4:
                                m = 4 * (n // 6) + n % 6
                                pool.wait_ge(ss_done, m + 1)
                                nc.gpsimd.tensor_scalar(norm[:, m % 2], norm[:, m % 2], 1e-24, None, ALU.max).then_inc(pow_chain, 1)
                                powers += 1
                                pool.wait_ge(pow_chain, powers)
                                nc.gpsimd.tensor_tensor(norm[:, m % 2], norm[:, m % 2], minus_half[:], ALU.pow).then_inc(norm_done, 1)
                            elif kind == "norm":
                                t, c = (n // 4) % T, n % 4
                                pool.wait_ge(qn_done, n + 1)
                                if n >= 2:
                                    pool.wait_ge(qr_done, n - 1)
                                q3 = qn[:, n % 2].rearrange("p (h d) -> p h d", h=8)
                                r3 = rot[:, n % 2].rearrange("p (h d) -> p h d", h=8)
                                sn = turn[:, 2 * (c // 2) + 1, t, None, :]
                                nc.gpsimd.tensor_tensor(r3[:, :, 0:HALF], q3[:, :, HALF:DH],
                                                        sn[:, :, 0:HALF].to_broadcast([P, 8, HALF]), ALU.mult)
                                nc.gpsimd.tensor_tensor(r3[:, :, HALF:DH], q3[:, :, 0:HALF],
                                                        sn[:, :, HALF:DH].to_broadcast([P, 8, HALF]), ALU.mult).then_inc(rot_done, 1)
                            elif kind == "shift":
                                col = rstd[:, n % 2:n % 2 + 1]
                                pool.wait_ge(mv_done, n + 1)
                                if n >= 2:
                                    pool.wait_ge(xn_done, n - 1)
                                nc.gpsimd.tensor_scalar(col, mv[:, n % 2, 1:2], 1e-5, None, ALU.add).then_inc(pow_chain, 1)
                                powers += 1
                                pool.wait_ge(pow_chain, powers)
                                nc.gpsimd.tensor_tensor(col, col, minus_half[:, 0:1], ALU.pow).then_inc(rstd_done, 1)

                    @block.vector
                    def _(dve):
                        links = [0]

                        def link(ins):
                            links[0] += 1
                            ins.then_inc(dve_chain, 1)
                            dve.wait_ge(dve_chain, links[0])

                        nc.vector.tensor_copy(x[:].rearrange("p (b t) d -> p b (t d)", b=NB), x_all[:, bass.ds(part * NB, NB)]).then_inc(xin, 1)
                        for kind, n in order:
                            if kind == "chunk" and n % 6 < 4:
                                m = 4 * (n // 6) + n % 6
                                dve.wait_ge(sq_done, m + 1)
                                if m >= 2:
                                    dve.wait_ge(qn_done, m - 1)
                                nc.vector.tensor_reduce(norm[:, m % 2], sq[:].rearrange("p (h d) -> p h d", h=8), AX, ALU.add).then_inc(ss_done, 1)
                            elif kind == "norm":
                                t, c = (n // 4) % T, n % 4
                                src = bank[chunk_at(n) % 4].rearrange("p (h d) -> p h d", h=8)
                                q3 = qn[:, n % 2].rearrange("p (h d) -> p h d", h=8)
                                dve.wait_ge(norm_done, n + 1)
                                if n >= 2:
                                    dve.wait_ge(rot_done, n - 1)
                                nc.vector.tensor_tensor(q3, src, norm[:, n % 2, :, None].to_broadcast([P, 8, DH]), ALU.mult).then_inc(qn_done, 1)
                                dve.wait_ge(qn_done, n + 1)
                                link(nc.vector.tensor_tensor(cosd[:, n % 2].rearrange("p (h d) -> p h d", h=8), q3,
                                                             turn[:, 2 * (c // 2), t, None, :].to_broadcast([P, 8, DH]), ALU.mult))
                            elif kind == "turn":
                                dve.wait_ge(rot_done, n + 1)
                                if n >= 2:
                                    dve.wait_ge(tr_full, tr_turn["qk", n - 2] + 1)
                                nc.vector.tensor_tensor(qr[:, n % 2], cosd[:, n % 2], rot[:, n % 2], ALU.add).then_inc(qr_done, 1)
                            elif kind == "scores":
                                for g in (2 * n, 2 * n + 1):
                                    dve.wait_ge(s_full, g + 1)
                                    s3 = bank[big_turn[kind, g] % 4].rearrange("p (g q) -> p g q", g=GROUP)
                                    link(nc.vector.tensor_reduce(smax[:, g % 2], s3, AX, ALU.max))
                                    if g >= 4:
                                        dve.wait_ge(tr_full, tr_turn["probT", g - 4] + 1)
                                    nc.vector.tensor_tensor(prob[:, g % 4].rearrange("p (g q) -> p g q", g=GROUP), s3,
                                                            smax[:, g % 2, :, None].to_broadcast([P, GROUP, P]), ALU.subtract).then_inc(s_read, 1)
                            elif kind == "divide":
                                p3 = prob[:, n % 4].rearrange("p (g q) -> p g q", g=GROUP)
                                dve.wait_ge(exp_done, n + 1)
                                link(nc.vector.tensor_reduce(rsum[:, n % 2], p3, AX, ALU.add))
                                link(nc.vector.reciprocal(rsum[:, n % 2], rsum[:, n % 2]))
                                nc.vector.tensor_tensor(p3, p3, rsum[:, n % 2, :, None].to_broadcast([P, GROUP, P]), ALU.mult).then_inc(div_done, 1)
                            elif kind in ("project", "ffn"):
                                u = out_turn[kind, n]
                                dve.wait_ge(o_full, u + 1)
                                if kind == "ffn" and n in keeps:
                                    dve.wait_ge(kept, keeps.index(n) + 1)
                                nc.vector.tensor_tensor(x[:, n, :], x[:, n, :], bank[6 + u % 2][:, 0:D], ALU.add).then_inc(x_done, 1)
                            elif kind == "shift":
                                dve.wait_ge(x_done, x_turn["project", n] + 1)
                                nc.vector.bn_stats(stats[:, n % 2, 0, :], x[:, n, 0:P])
                                dve.wait_ge(sh_full, n + 1)
                                link(nc.vector.bn_stats(stats[:, n % 2, 1, :], bank[big_turn[kind, n] % 4][:, 0:P]))
                                if n >= 2:
                                    dve.wait_ge(rstd_done, n - 1)
                                nc.vector.bn_aggr(mv[:, n % 2], stats[:, n % 2].rearrange("p a b -> p (a b)")).then_inc(mv_done, 1)
                            elif kind == "xn":
                                dve.wait_ge(rstd_done, n + 1)
                                if n >= 2:
                                    dve.wait_ge(tr_full, tr_turn["xnT", n - 2] + 1)
                                mean, scale = mv[:, n % 2, 0:1], rstd[:, n % 2:n % 2 + 1]
                                dve.wait_ge(mv_done, n + 1)
                                nc.vector.tensor_scalar(xn[:, n % 2, 0:P], x[:, n, 0:P], mean, scale, ALU.subtract, ALU.mult)
                                nc.vector.tensor_scalar(xn[:, n % 2, P:D], bank[big_turn["shift", n] % 4][:, 0:P], mean, scale,
                                                        ALU.subtract, ALU.mult).then_inc(xn_done, 1)
                            elif kind == "ga":
                                i = n % FC
                                rows_out = P if i < FC - 1 else FR
                                dve.wait_ge(gelu_done, n + 1)
                                if n == 0:
                                    dve.wait_ge(rest_in, 16 * 6)
                                if i == 0 and n > 0:
                                    dve.wait_ge(o_full, out_turn["ffn", 2 * (n // FC) - 1] + 1)
                                nc.vector.scalar_tensor_tensor(h[0:rows_out, i, :], bank[big_turn[kind, n] % 4][0:rows_out, 0:PAIR], b1[0:rows_out, 0, i:i + 1],
                                                               gate[0:rows_out, n % 2], ALU.add, ALU.mult).then_inc(h_done, 1)
                        dve.wait_ge(x_done, len(x_turn))
                        nc.vector.tensor_copy(x_all[:, bass.ds(part * NB, NB)], x[:].rearrange("p (b t) d -> p b (t d)", b=NB)).then_inc(back, 1)
                        dve.wait_ge(back, 1)
                clear(nc, sems.all)




def constants(nc, mem, w):
    with ExitStack() as ctx:
        sems = Semaphores(nc, ctx, "init", "loaded done")
        loaded, done = sems.all
        with nc.Block() as block:
            @block.sync
            def _(sp):
                sp.dma_start(mem["ident"][:], w["ident"]).then_inc(loaded, 16)
                sp.dma_start(mem["x_all"][:].rearrange("p b (t d) -> p b t d", t=T),
                             w["x"].rearrange("b (t p) d -> p b t d", p=P)).then_inc(loaded, 16)
                sp.wait_ge(loaded, 32)

            @block.vector
            def _(dve):
                dve.wait_ge(loaded, 32)
                nc.vector.tensor_copy(mem["ident_bf"][:], mem["ident"][:]).then_inc(done, 1)
                dve.wait_ge(done, 1)
        clear(nc, sems.all)


def setup_exponent(nc, mem):
    sems = mem["norm_sems"]
    with nc.Block() as block:
        @block.vector
        def _(dve):
            nc.vector.memset(mem["exponent"][:], -0.5).then_inc(sems["chain"], 1)
            dve.wait_ge(sems["chain"], 1)
    clear(nc, sems.all)


def layer_norm(nc, mem, w):
    x_all = mem["x_all"]
    with ExitStack() as ctx:
        stats = ctx.enter_context(nc.sbuf_tensor("ln_stats", [P, B * T, 6], F32))
        mv = ctx.enter_context(nc.sbuf_tensor("ln_mv", [P, B * T, 2], F32))
        rstd = ctx.enter_context(nc.sbuf_tensor("ln_rstd", [P, B * T, 1], F32))
        exponent = ctx.enter_context(nc.sbuf_tensor("ln_exponent", [P, B * T, 1], F32))
        sems = Semaphores(nc, ctx, "ln", "kept chain pow_chain")
        kept, chain, pow_chain = sems.all
        x3 = x_all[:].rearrange("p b (t d) -> p (b t) d", t=T)
        with nc.Block() as block:
            @block.sync
            def _(sp):
                sp.dma_start(w["x_kept"], x_all[:].rearrange("p b n -> p (b n)")).then_inc(kept, 16)
                sp.wait_ge(kept, 16)

            @block.gpsimd
            def _(pool):
                nc.gpsimd.memset(exponent[:], -0.5).then_inc(pow_chain, 1)
                pool.wait_ge(pow_chain, 1)
                pool.wait_ge(chain, 2 * B * T + 1)
                nc.gpsimd.tensor_tensor(rstd[:], rstd[:], exponent[:], ALU.pow).then_inc(pow_chain, 1)

            @block.vector
            def _(dve):
                for k in range(B * T):
                    nc.vector.bn_stats(stats[:, k], x3[:, k]).then_inc(chain, 1)
                    dve.wait_ge(chain, 2 * k + 1)
                    nc.vector.bn_aggr(mv[:, k], stats[:, k]).then_inc(chain, 1)
                dve.wait_ge(chain, 2 * B * T)
                nc.vector.tensor_scalar(rstd[:], mv[:, :, 1:2], 1e-5, None, ALU.add).then_inc(chain, 1)
                dve.wait_ge(pow_chain, 2)
                dve.wait_ge(kept, 16)
                for k in range(B * T):
                    nc.vector.tensor_scalar(x3[:, k], x3[:, k], mv[:, k, 0:1], rstd[:, k], ALU.subtract, ALU.mult).then_inc(chain, 1)
                dve.wait_ge(chain, 3 * B * T + 1)
        clear(nc, sems.all)


def finish(nc, mem, w, out):
    x_all = mem["x_all"]
    with ExitStack() as ctx:
        kept = ctx.enter_context(nc.sbuf_tensor("kept_x", [P, B, T * D], F32))
        sems = Semaphores(nc, ctx, "fin", "loaded added stored")
        loaded, added, stored = sems.all
        with nc.Block() as block:
            @block.sync
            def _(sp):
                for b in range(B):
                    sp.dma_start(kept[:, b], w["x_kept"][:, b * T * D:(b + 1) * T * D]).then_inc(loaded, 16)
                    sp.wait_ge(loaded, 16 * (b + 1))
                for b in range(B):
                    sp.wait_ge(added, b + 1)
                    sp.dma_start(out[b].rearrange("(t p) d -> p t d", p=P), x_all[:, b].rearrange("p (t d) -> p t d", t=T)).then_inc(stored, 16)
                sp.wait_ge(stored, 16 * B)

            @block.vector
            def _(dve):
                for b in range(B):
                    dve.wait_ge(loaded, 16 * (b + 1))
                    nc.vector.tensor_tensor(x_all[:, b], x_all[:, b], kept[:, b], ALU.add).then_inc(added, 1)
        clear(nc, sems.all)


def program(nc, a, out):
    w = {"x": a["x"], "ident": a["c_ident"], "shift": a["c_shift"], "win_mask": a["c_win_mask"], "rope1": a["c_rope1"],
         "rope0": a["c_rope0"], "causal": a["c_causal"], "ones": a["c_ones"], "upper": a["c_upper"],
         "ctx": a["ctx_2048"], "mask": a["mask_BxS2_ik0"],
         "Wq": a["L0_xattn_Wq"], "Wkv": a["L0_xattn_Wkv"], "null_kv": a["L0_xattn_null_kv"], "Wout": a["L0_xattn_Wout"],
         "ln_scale": a["L0_xattn_ln_scale"], "ln_bias": a["L0_xattn_ln_bias"],
         "w_qkv": a["L0_ffn_w_qkv"], "w_o": a["L0_ffn_w_o"], "w_router": a["L0_ffn_w_router"], "g12": a["c_l0_g12"],
         "w1": a["L0_ffn_w1"], "w2": a["L0_ffn_w2"], "b": a["L1_xattn_b"],
         "Wqkv": a["L1_ffn_Wqkv"], "qk_scale": (a["L1_ffn_q_scale"], a["L1_ffn_k_scale"]), "Wo": a["L1_ffn_Wo"],
         "W1": a["L1_ffn_W1"], "cols": a["c_l1_cols"], "W2": a["L1_ffn_W2"], "b2": a["L1_ffn_b2"]}
    w["x_kept"] = nc.dram_tensor("x_kept", (P, B * T * D), F32, kind="Internal").ap()
    with ExitStack() as ctx:
        psum = ctx.enter_context(nc.psum_tensor("psum", [P, 8, 512], F32))
        mem = {"x_all": ctx.enter_context(nc.sbuf_tensor("x_all", [P, B, T * D], F32)),
               "ident": ctx.enter_context(nc.sbuf_tensor("ident", [P, P], F32)),
               "ident_bf": ctx.enter_context(nc.sbuf_tensor("ident_bf", [P, P], BF16)),
               "bank": [psum[:, i] for i in range(8)]}
        constants(nc, mem, w)
        with ExitStack() as l0:
            for name, shape in (("stats", [P, NT, 6]), ("mv", [P, NT, 2]), ("rstd", [P, NT]), ("exponent", [P, NT])):
                mem[name] = l0.enter_context(nc.sbuf_tensor(name, shape, F32))
            mem["norm_sems"] = Semaphores(nc, l0, "nm", "mv_done chain pow_done scaled")
            setup_exponent(nc, mem)
            null_attention(nc, mem, w)
            with ExitStack() as moe:
                mem["moe_inT"] = moe.enter_context(nc.sbuf_tensor("moe_inT", [P, B, DC, S], F32))
                mem["logits"] = moe.enter_context(nc.sbuf_tensor("logits", [P, B, T, E], F32))
                mem["gates"] = moe.enter_context(nc.sbuf_tensor("gates", [P, NT, E], F32))
                causal_attention(nc, mem, w)
                experts(nc, mem, w)
            memory_attention(nc, mem, w)
        layer_norm(nc, mem, w)
        local_layers(nc, mem, w)
        finish(nc, mem, w, out)


def shape_constants():
    f = np.float32
    out = {"c_ident": np.eye(P, dtype=f)}
    shift = np.zeros((2, P, P), f)
    shift[0, np.arange(P - 1), np.arange(1, P)] = 1.0
    shift[1, P - 1, 0] = 1.0
    out["c_shift"] = shift
    i = np.arange(WIN)[:, None]
    k = np.arange(WIN)[None, :]
    own, before = np.where(k <= i, 0, NEG), np.where(k >= i, 0, NEG)
    both = np.concatenate([before, own], 1)
    first = np.concatenate([np.full_like(before, NEG), own], 1)
    out["c_win_mask"] = np.stack([np.concatenate([first, both], 0), np.concatenate([both, both], 0)]).astype(f)
    half = np.arange(0, DH, 2, dtype=f)
    inv = (f(1.0) / f(10000.0) ** (half / f(DH))).astype(f)
    t = np.arange(S, dtype=f)
    fr = t[:, None] * inv[None, :]
    fr = np.concatenate([fr, fr], -1)
    base = (half + f(0.4 * DH)) / f(1.4 * DH)
    power = (t - S // 2) / f(WIN // 2)
    sc = base[None, :] ** power[:, None]
    sc = np.concatenate([sc, sc], -1).astype(f)
    sign = np.where(np.arange(DH) < HALF, -1.0, 1.0).astype(f)
    cos, sin = np.cos(fr), np.sin(fr) * sign
    out["c_rope1"] = np.stack([cos * sc, sin * sc, cos * (f(1.0) / sc), sin * (f(1.0) / sc)]).astype(f)
    theta = f(10000.0) ** (f(-2.0) * (np.arange(HD // 2, dtype=f) / f(HD)))
    fr0 = (t[:, None] * theta[None, :].astype(f)).astype(f)
    cos0 = np.repeat(np.cos(fr0), 2, axis=1)
    sin0 = np.repeat(np.sin(fr0), 2, axis=1) * np.where(np.arange(HD) % 2 == 0, -1.0, 1.0)
    out["c_rope0"] = np.stack([cos0, sin0], 1).astype(f)
    q = np.arange(P)
    out["c_causal"] = np.where(q[None, :] <= q[:, None], 0, NEG).astype(f)
    out["c_ones"] = np.ones((P, P), f)
    out["c_upper"] = (q[:, None] < q[None, :]).astype(f)
    return out


_INS = [
    "x", "ctx_2048", "mask_BxS2_ik0", "L0_xattn_Wq", "L0_xattn_Wkv", "L0_xattn_null_kv", "L0_xattn_Wout",
    "L0_xattn_ln_scale", "L0_xattn_ln_bias", "L0_ffn_w_qkv", "L0_ffn_w_o", "L0_ffn_w_router", "L0_ffn_w1",
    "L0_ffn_w2", "L1_xattn_b", "L1_ffn_Wqkv", "L1_ffn_q_scale", "L1_ffn_k_scale", "L1_ffn_Wo", "L1_ffn_W1",
    "L1_ffn_W2", "L1_ffn_b2",
]
_OUT = (B, S, D)


def l1_columns(b1, ln_g, ln_b):
    halves = b1.reshape(DEPTH, 2, FI)
    padded = np.zeros((DEPTH, 2, FC * P), b1.dtype)
    padded[:, :, 0:FI] = halves
    columns = [padded.reshape(DEPTH, 2 * FC, P), ln_g.reshape(DEPTH, DC, P), ln_b.reshape(DEPTH, DC, P)]
    return np.ascontiguousarray(np.concatenate(columns, 1).transpose(0, 2, 1))


def kernel(**inputs):
    import concourse.bacc as bacc
    from concourse.bass_utils import run_bass_kernel_spmd

    nc = bacc.Bacc("TRN2", target_bir_lowering=False, num_devices=1)
    arrays = {name: np.ascontiguousarray(inputs[name]) for name in _INS}
    arrays.update(shape_constants())
    arrays["c_l1_cols"] = l1_columns(*(np.asarray(inputs[n]) for n in ("L1_ffn_b1", "L1_ffn_ln_g", "L1_ffn_ln_b")))
    arrays["c_l0_g12"] = np.ascontiguousarray(np.concatenate([np.asarray(inputs[n]).reshape(DC, P) for n in ("L0_ffn_g1", "L0_ffn_g2")]).T)
    aps = {name: nc.dram_tensor(name, a.shape, mybir.dt.from_np(a.dtype), kind="ExternalInput").ap() for name, a in arrays.items()}
    out = nc.dram_tensor("out", _OUT, F32, kind="ExternalOutput").ap()
    program(nc, aps, out)
    return run_bass_kernel_spmd(nc, [arrays], core_ids=[0]).results[0]["out"]
```
